# Optimizing a Trainium2 kernel written in Bass

```python
import numpy as np
import jax
import jax.numpy as jnp

def _softmax(x, axis=-1):
    return jax.nn.softmax(x, axis=axis)

def _gelu(x):
    return jax.nn.gelu(x, approximate=True)

def _silu(x):
    return jax.nn.silu(x)

def _sigmoid(x):
    return jax.nn.sigmoid(x)

def _layernorm(x, axis=-1, eps=1e-05):
    m = jnp.mean(x, axis=axis, keepdims=True)
    v = jnp.var(x, axis=axis, keepdims=True)
    return (x - m) / jnp.sqrt(v + eps)

def _scatter_add(tgt, idx, src, axis=0):
    return tgt.at[idx].add(src)

def _segment_sum(src, seg, n):
    return jax.ops.segment_sum(src, seg, n)
kernel_name = 'mk_xattn_seq_d4_seqx_r4_ed7310'

def setup_inputs(seed: int=0):
    np.random.seed(seed)
    _w = jnp.asarray

    def _rec_inputs():
        import jax
        import jax.numpy as jnp
        _rk = jax.random.key(seed)
        x = -0.0002928 + 1 * jax.random.normal(jax.random.fold_in(_rk, 1), (8, 256, 512), jnp.float32)
        _lenS = 256 - jax.random.randint(jax.random.fold_in(_rk, 7), (8,), 0, max(1, 256 // 4) + 1, jnp.int32)
        _lenS2 = 256 - jax.random.randint(jax.random.fold_in(_rk, 8), (8,), 0, max(1, 256 // 4) + 1, jnp.int32)
        _ctx_2048P = jax.random.normal(jax.random.fold_in(_rk, 12), (8, 16, 512), jnp.float32)
        _ctx_2048c = jax.random.dirichlet(jax.random.fold_in(_rk, 512), 0.3 * jnp.ones((16,), jnp.float32), (8, 256))
        _ctx_2048t = jnp.einsum('bsk,bkd->bsd', _ctx_2048c, _ctx_2048P)
        _ctx_2048t = _ctx_2048t * jax.lax.rsqrt(jnp.mean(jnp.square(_ctx_2048t)) + 1e-12) * 0.953939
        ctx_2048 = -1.39393e-06 + 0.999914 * (_ctx_2048t + 0.3 * jax.random.normal(jax.random.fold_in(_rk, 612), (8, 256, 512), jnp.float32))
        _validS = jnp.arange(256)[None, :] < _lenS[:, None]
        _validS2 = jnp.arange(256)[None, :] < _lenS2[:, None]
        _causal = jnp.tril(jnp.ones((256, 256), dtype=bool))
        mask_Bx1x2048_bf1 = jnp.ones((8, 1, 512), dtype=bool)
        return (x, ctx_2048, mask_Bx1x2048_bf1)
    x, ctx_2048, mask_Bx1x2048_bf1 = _rec_inputs()

    def _L0_xattn_setup():
        import jax, jax.numpy as jnp
        import numpy as np
        import math
        N_HEADS = 16
        EPS = 1e-05

        def _masked_instance_norm(x, mask):
            m = mask.astype(x.dtype)
            x = x * m
            n_valid = jnp.sum(m, axis=-1, keepdims=True)
            mean = jnp.sum(x, axis=-1, keepdims=True) / n_valid
            var = jnp.sum(x * x, axis=-1, keepdims=True) / n_valid - mean * mean
            x = (x - mean) / jnp.sqrt(jax.nn.relu(var) + EPS)
            return x * m
        key = jax.random.key(seed)
        ks = jax.random.split(key, 8)
        bs, c, t1, t2 = (2, 256, 512, 512)
        s = 1.0 / math.sqrt(c)
        return {'x': jax.random.normal(ks[0], (bs, c, t1), jnp.float32), 'mask': jnp.ones((bs, 1, t1), jnp.bool_), 'kv': jax.random.normal(ks[1], (bs, c, t2), jnp.float32), 'kv_mask': jnp.ones((bs, 1, t2), jnp.bool_), 'Wq': jax.random.normal(ks[2], (c, c), jnp.float32) * s, 'bq': jnp.zeros((c,), jnp.float32), 'Wk': jax.random.normal(ks[3], (c, c), jnp.float32) * s, 'bk': jnp.zeros((c,), jnp.float32), 'Wv': jax.random.normal(ks[4], (c, c), jnp.float32) * s, 'bv': jnp.zeros((c,), jnp.float32)}
    _L0_xattn_all = _L0_xattn_setup()
    _L0_xattn_in = {k: v for k, v in _L0_xattn_all.items() if k in ('Wq', 'bq', 'Wk', 'bk', 'Wv', 'bv')}
    del _L0_xattn_all

    def _L1_xattn_setup():
        import jax, jax.numpy as jnp
        import numpy as np
        E, H, L, B = (512, 32, 256, 4)
        S = E // H
        DM, DD = (32, 64)

        def _ln(x, w, b, eps=1e-05):
            m = x.mean(-1, keepdims=True)
            v = ((x - m) ** 2).mean(-1, keepdims=True)
            return (x - m) / jnp.sqrt(v + eps) * w + b

        def _block(x, state, ln1_w, ln1_b, ln2_w, ln2_b, maa_x, maa_w1, maa_w2, maa_stack, time_decay, td_w1, td_w2, u, Wr, Wk, Wv, Wg, Wo, gn_w, gn_b, ffn_maa_k, ffn_maa_r, Wfk, Wfr, Wfv):
            b, l, e = x.shape
            h = u.shape[0]
            s_ = e // h
            xa = _ln(x, ln1_w, ln1_b)
            sx = jnp.concatenate([state[:, 1:2] - xa[:, :1], xa[:, :-1] - xa[:, 1:]], axis=1)
            xxx = jnp.tanh((xa + sx * maa_x) @ maa_w1).reshape(b, l, 5, DM)
            xxx = jnp.einsum('blfd,fde->blfe', xxx, maa_w2)
            xm = xa[:, :, None] + sx[:, :, None] * (maa_stack + xxx)
            xk, xw, xv, xr, xg = (xm[:, :, j] for j in range(5))
            w = jnp.exp(-jnp.exp(time_decay + jnp.tanh(xw @ td_w1) @ td_w2)).reshape(b, l, h, s_)
            r = (xr @ Wr.T).reshape(b, l, h, s_)
            k = (xk @ Wk.T).reshape(b, l, h, s_)
            v = (xv @ Wv.T).reshape(b, l, h, s_)
            g = jax.nn.silu(xg @ Wg.T)
            s0 = state[:, 2:2 + s_].reshape(b, h, s_, s_)

            def step(s, rkvw):
                r_t, k_t, v_t, w_t = rkvw
                a = k_t[..., :, None] * v_t[..., None, :]
                out = jnp.einsum('bhi,bhij->bhj', r_t, u * a + s)
                s = a + w_t[..., :, None] * s
                return (s, out)
            rkvw = tuple((jnp.moveaxis(t, 1, 0) for t in (r, k, v, w)))
            _, out = jax.lax.scan(step, s0, rkvw)
            out = jnp.moveaxis(out, 0, 1).reshape(b, l, e)
            og = out.reshape(b, l, h, s_)
            m = og.mean(-1, keepdims=True)
            va = ((og - m) ** 2).mean(-1, keepdims=True)
            og = ((og - m) / jnp.sqrt(va + 1e-05)).reshape(b, l, e) * gn_w + gn_b
            x1 = x + og * g @ Wo.T
            xc = _ln(x1, ln2_w, ln2_b)
            sx2 = jnp.concatenate([state[:, 0:1] - xc[:, :1], xc[:, :-1] - xc[:, 1:]], axis=1)
            xk2 = xc + sx2 * ffn_maa_k
            xr2 = xc + sx2 * ffn_maa_r
            rr = jax.nn.sigmoid(xr2 @ Wfr.T)
            kk = jnp.square(jax.nn.relu(xk2 @ Wfk.T))
            return x1 + rr * (kk @ Wfv.T)
        key = jax.random.key(seed)
        ks = jax.random.split(key, 24)
        sc = 0.02
        d = {'x': jax.random.normal(ks[0], (B, L, E), jnp.float32), 'state': jax.random.normal(ks[1], (B, 2 + S, E), jnp.float32) * 0.1, 'ln1_w': jnp.ones((E,), jnp.float32), 'ln1_b': jnp.zeros((E,), jnp.float32), 'ln2_w': jnp.ones((E,), jnp.float32), 'ln2_b': jnp.zeros((E,), jnp.float32), 'maa_x': jax.random.normal(ks[2], (E,), jnp.float32) * 0.1, 'maa_w1': jax.random.normal(ks[3], (E, 5 * DM), jnp.float32) * sc, 'maa_w2': jax.random.normal(ks[4], (5, DM, E), jnp.float32) * sc, 'maa_stack': jax.random.normal(ks[5], (1, 5, E), jnp.float32) * 0.1, 'time_decay': jax.random.normal(ks[6], (E,), jnp.float32) * 0.5, 'td_w1': jax.random.normal(ks[7], (E, DD), jnp.float32) * sc, 'td_w2': jax.random.normal(ks[8], (DD, E), jnp.float32) * sc, 'u': jax.random.normal(ks[9], (H, S, 1), jnp.float32) * 0.1, 'Wr': jax.random.normal(ks[10], (E, E), jnp.float32) * sc, 'Wk': jax.random.normal(ks[11], (E, E), jnp.float32) * sc, 'Wv': jax.random.normal(ks[12], (E, E), jnp.float32) * sc, 'Wg': jax.random.normal(ks[13], (E, E), jnp.float32) * sc, 'Wo': jax.random.normal(ks[14], (E, E), jnp.float32) * sc, 'gn_w': jnp.ones((E,), jnp.float32), 'gn_b': jnp.zeros((E,), jnp.float32), 'ffn_maa_k': jax.random.normal(ks[15], (E,), jnp.float32) * 0.1, 'ffn_maa_r': jax.random.normal(ks[16], (E,), jnp.float32) * 0.1, 'Wfk': jax.random.normal(ks[17], (E, E), jnp.float32) * sc, 'Wfr': jax.random.normal(ks[18], (E, E), jnp.float32) * sc, 'Wfv': jax.random.normal(ks[19], (E, E), jnp.float32) * sc}
        return d
    _L1_xattn_all = _L1_xattn_setup()
    _L1_xattn_in = {k: v for k, v in _L1_xattn_all.items() if k in ('ln1_w', 'ln1_b', 'ln2_w', 'ln2_b', 'maa_x', 'maa_w1', 'maa_w2', 'maa_stack', 'time_decay', 'td_w1', 'td_w2', 'u', 'Wr', 'Wk', 'Wv', 'Wg', 'Wo', 'gn_w', 'gn_b', 'ffn_maa_k', 'ffn_maa_r', 'Wfk', 'Wfr', 'Wfv')}
    del _L1_xattn_all

    def _L2_xattn_setup():
        import jax, jax.numpy as jnp
        import numpy as np
        B, Q, S1, S2 = (4, 64, 512, 512)
        D, H, K, F = (512, 16, 128, 2048)
        LN_EPS = 1e-05

        def _layer_norm(x, scale, offset):
            mu = jnp.mean(x, axis=-1, keepdims=True)
            var = jnp.var(x, axis=-1, keepdims=True)
            return (x - mu) * jax.lax.rsqrt(var + LN_EPS) * scale + offset

        def _cross_attention(q_in, kv_in, wq, bq, wk, bk, wv, bv, wo, bo, bias_k, bias_v):
            b, q_len, _ = q_in.shape
            t = kv_in.shape[1]
            qh = (q_in @ wq + bq).reshape(b, q_len, H, K)
            kh = (kv_in @ wk + bk).reshape(b, t, H, K)
            vh = (kv_in @ wv + bv).reshape(b, t, H, K)
            kh = jnp.concatenate([kh, jnp.broadcast_to(bias_k, (b, 1, H, K))], axis=1)
            vh = jnp.concatenate([vh, jnp.broadcast_to(bias_v, (b, 1, H, K))], axis=1)
            scale = jnp.sqrt(jnp.asarray(K, q_in.dtype))
            logits = jnp.einsum('bqhk,bthk->bhqt', qh, kh) / scale
            weights = jax.nn.softmax(logits, axis=-1)
            ctx = jnp.einsum('bhqt,bthk->bqhk', weights, vh).reshape(b, q_len, H * K)
            return ctx @ wo + bo

        def _forward(x, xf_1, xf_2, ln1_scale, ln1_offset, wq1, bq1, wk1, bk1, wv1, bv1, wo1, bo1, bias_k1, bias_v1, ln2_scale, ln2_offset, wq2, bq2, wk2, bk2, wv2, bv2, wo2, bo2, bias_k2, bias_v2, ln_mlp_scale, ln_mlp_offset, w_fc1, b_fc1, w_fc2, b_fc2):
            res = x
            h = _layer_norm(x, ln1_scale, ln1_offset)
            x = res + _cross_attention(h, xf_1, wq1, bq1, wk1, bk1, wv1, bv1, wo1, bo1, bias_k1, bias_v1)
            res = x
            h = _layer_norm(x, ln2_scale, ln2_offset)
            x = res + _cross_attention(h, xf_2, wq2, bq2, wk2, bk2, wv2, bv2, wo2, bo2, bias_k2, bias_v2)
            h = _layer_norm(x, ln_mlp_scale, ln_mlp_offset)
            h = jax.nn.gelu(h @ w_fc1 + b_fc1, approximate=False) @ w_fc2 + b_fc2
            return x + h
        key = jax.random.key(seed)
        ks = iter(jax.random.split(key, 64))

        def rn(shape, s=0.02):
            return jax.random.normal(next(ks), shape, jnp.float32) * s
        inp = {'x': rn((B, Q, D), 1.0), 'xf_1': rn((B, S1, D), 1.0), 'xf_2': rn((B, S2, D), 1.0)}
        for i in (1, 2):
            inp[f'ln{i}_scale'] = jnp.ones((D,), jnp.float32)
            inp[f'ln{i}_offset'] = jnp.zeros((D,), jnp.float32)
            inp[f'wq{i}'] = rn((D, H * K))
            inp[f'bq{i}'] = jnp.zeros((H * K,), jnp.float32)
            inp[f'wk{i}'] = rn((D, H * K))
            inp[f'bk{i}'] = jnp.zeros((H * K,), jnp.float32)
            inp[f'wv{i}'] = rn((D, H * K))
            inp[f'bv{i}'] = jnp.zeros((H * K,), jnp.float32)
            inp[f'wo{i}'] = rn((H * K, D))
            inp[f'bo{i}'] = jnp.zeros((D,), jnp.float32)
            inp[f'bias_k{i}'] = rn((1, 1, H, K))
            inp[f'bias_v{i}'] = rn((1, 1, H, K))
        inp['ln_mlp_scale'] = jnp.ones((D,), jnp.float32)
        inp['ln_mlp_offset'] = jnp.zeros((D,), jnp.float32)
        inp['w_fc1'] = rn((D, F))
        inp['b_fc1'] = jnp.zeros((F,), jnp.float32)
        inp['w_fc2'] = rn((F, D))
        inp['b_fc2'] = jnp.zeros((D,), jnp.float32)
        return inp
    _L2_xattn_all = _L2_xattn_setup()
    _L2_xattn_in = {k: v for k, v in _L2_xattn_all.items() if k in ('ln1_scale', 'ln1_offset', 'wq1', 'bq1', 'wk1', 'bk1', 'wv1', 'bv1', 'wo1', 'bo1', 'bias_k1', 'bias_v1', 'ln2_scale', 'ln2_offset', 'wq2', 'bq2', 'wk2', 'bk2', 'wv2', 'bv2', 'wo2', 'bo2', 'bias_k2', 'bias_v2', 'ln_mlp_scale', 'ln_mlp_offset', 'w_fc1', 'b_fc1', 'w_fc2', 'b_fc2')}
    del _L2_xattn_all

    def _L3_xattn_setup():
        import jax, jax.numpy as jnp
        import numpy as np
        B, C, CI, N = (16, 256, 128, 512)
        EPS = 1e-05

        def _conv1x1(w, b, x):
            return jnp.einsum('oc,bcn->bon', w, x) + b[None, :, None]
        key = jax.random.key(seed)
        ks = jax.random.split(key, 14)
        s = 0.02
        return {'x': jax.random.normal(ks[0], (B, C, N), jnp.float32), 'x_2': jax.random.normal(ks[1], (B, C, N), jnp.float32), 'theta_w': jax.random.normal(ks[2], (CI, C), jnp.float32) * s, 'theta_b': jax.random.normal(ks[3], (CI,), jnp.float32) * s, 'phi_w': jax.random.normal(ks[4], (CI, C), jnp.float32) * s, 'phi_b': jax.random.normal(ks[5], (CI,), jnp.float32) * s, 'g_w': jax.random.normal(ks[6], (CI, C), jnp.float32) * s, 'g_b': jax.random.normal(ks[7], (CI,), jnp.float32) * s, 'w_w': jax.random.normal(ks[8], (C, CI), jnp.float32) * s, 'w_b': jax.random.normal(ks[9], (C,), jnp.float32) * s, 'bn_gamma': jax.random.normal(ks[10], (C,), jnp.float32), 'bn_beta': jax.random.normal(ks[11], (C,), jnp.float32), 'bn_mean': jax.random.normal(ks[12], (C,), jnp.float32), 'bn_var': jax.random.uniform(ks[13], (C,), jnp.float32, 0.5, 1.5)}
    _L3_xattn_all = _L3_xattn_setup()
    _L3_xattn_in = {k: v for k, v in _L3_xattn_all.items() if k in ('theta_w', 'theta_b', 'phi_w', 'phi_b', 'g_w', 'g_b', 'w_w', 'w_b', 'bn_gamma', 'bn_beta', 'bn_mean', 'bn_var')}
    del _L3_xattn_all
    return {'x': x, 'ctx_2048': ctx_2048, 'mask_Bx1x2048_bf1': mask_Bx1x2048_bf1, 'L0_xattn_Wq': _L0_xattn_in['Wq'], 'L0_xattn_bq': _L0_xattn_in['bq'], 'L0_xattn_Wk': _L0_xattn_in['Wk'], 'L0_xattn_bk': _L0_xattn_in['bk'], 'L0_xattn_Wv': _L0_xattn_in['Wv'], 'L0_xattn_bv': _L0_xattn_in['bv'], 'L1_xattn_ln1_w': _L1_xattn_in['ln1_w'], 'L1_xattn_ln1_b': _L1_xattn_in['ln1_b'], 'L1_xattn_ln2_w': _L1_xattn_in['ln2_w'], 'L1_xattn_ln2_b': _L1_xattn_in['ln2_b'], 'L1_xattn_maa_x': _L1_xattn_in['maa_x'], 'L1_xattn_maa_w1': _L1_xattn_in['maa_w1'], 'L1_xattn_maa_w2': _L1_xattn_in['maa_w2'], 'L1_xattn_maa_stack': _L1_xattn_in['maa_stack'], 'L1_xattn_time_decay': _L1_xattn_in['time_decay'], 'L1_xattn_td_w1': _L1_xattn_in['td_w1'], 'L1_xattn_td_w2': _L1_xattn_in['td_w2'], 'L1_xattn_u': _L1_xattn_in['u'], 'L1_xattn_Wr': _L1_xattn_in['Wr'], 'L1_xattn_Wk': _L1_xattn_in['Wk'], 'L1_xattn_Wv': _L1_xattn_in['Wv'], 'L1_xattn_Wg': _L1_xattn_in['Wg'], 'L1_xattn_Wo': _L1_xattn_in['Wo'], 'L1_xattn_gn_w': _L1_xattn_in['gn_w'], 'L1_xattn_gn_b': _L1_xattn_in['gn_b'], 'L1_xattn_ffn_maa_k': _L1_xattn_in['ffn_maa_k'], 'L1_xattn_ffn_maa_r': _L1_xattn_in['ffn_maa_r'], 'L1_xattn_Wfk': _L1_xattn_in['Wfk'], 'L1_xattn_Wfr': _L1_xattn_in['Wfr'], 'L1_xattn_Wfv': _L1_xattn_in['Wfv'], 'L2_xattn_ln1_scale': _L2_xattn_in['ln1_scale'], 'L2_xattn_ln1_offset': _L2_xattn_in['ln1_offset'], 'L2_xattn_wq1': _L2_xattn_in['wq1'], 'L2_xattn_bq1': _L2_xattn_in['bq1'], 'L2_xattn_wk1': _L2_xattn_in['wk1'], 'L2_xattn_bk1': _L2_xattn_in['bk1'], 'L2_xattn_wv1': _L2_xattn_in['wv1'], 'L2_xattn_bv1': _L2_xattn_in['bv1'], 'L2_xattn_wo1': _L2_xattn_in['wo1'], 'L2_xattn_bo1': _L2_xattn_in['bo1'], 'L2_xattn_bias_k1': _L2_xattn_in['bias_k1'], 'L2_xattn_bias_v1': _L2_xattn_in['bias_v1'], 'L2_xattn_ln2_scale': _L2_xattn_in['ln2_scale'], 'L2_xattn_ln2_offset': _L2_xattn_in['ln2_offset'], 'L2_xattn_wq2': _L2_xattn_in['wq2'], 'L2_xattn_bq2': _L2_xattn_in['bq2'], 'L2_xattn_wk2': _L2_xattn_in['wk2'], 'L2_xattn_bk2': _L2_xattn_in['bk2'], 'L2_xattn_wv2': _L2_xattn_in['wv2'], 'L2_xattn_bv2': _L2_xattn_in['bv2'], 'L2_xattn_wo2': _L2_xattn_in['wo2'], 'L2_xattn_bo2': _L2_xattn_in['bo2'], 'L2_xattn_bias_k2': _L2_xattn_in['bias_k2'], 'L2_xattn_bias_v2': _L2_xattn_in['bias_v2'], 'L2_xattn_ln_mlp_scale': _L2_xattn_in['ln_mlp_scale'], 'L2_xattn_ln_mlp_offset': _L2_xattn_in['ln_mlp_offset'], 'L2_xattn_w_fc1': _L2_xattn_in['w_fc1'], 'L2_xattn_b_fc1': _L2_xattn_in['b_fc1'], 'L2_xattn_w_fc2': _L2_xattn_in['w_fc2'], 'L2_xattn_b_fc2': _L2_xattn_in['b_fc2'], 'L3_xattn_theta_w': _L3_xattn_in['theta_w'], 'L3_xattn_theta_b': _L3_xattn_in['theta_b'], 'L3_xattn_phi_w': _L3_xattn_in['phi_w'], 'L3_xattn_phi_b': _L3_xattn_in['phi_b'], 'L3_xattn_g_w': _L3_xattn_in['g_w'], 'L3_xattn_g_b': _L3_xattn_in['g_b'], 'L3_xattn_w_w': _L3_xattn_in['w_w'], 'L3_xattn_w_b': _L3_xattn_in['w_b'], 'L3_xattn_bn_gamma': _L3_xattn_in['bn_gamma'], 'L3_xattn_bn_beta': _L3_xattn_in['bn_beta'], 'L3_xattn_bn_mean': _L3_xattn_in['bn_mean'], 'L3_xattn_bn_var': _L3_xattn_in['bn_var']}

def reference(x, ctx_2048, mask_Bx1x2048_bf1, L0_xattn_Wq, L0_xattn_bq, L0_xattn_Wk, L0_xattn_bk, L0_xattn_Wv, L0_xattn_bv, L1_xattn_ln1_w, L1_xattn_ln1_b, L1_xattn_ln2_w, L1_xattn_ln2_b, L1_xattn_maa_x, L1_xattn_maa_w1, L1_xattn_maa_w2, L1_xattn_maa_stack, L1_xattn_time_decay, L1_xattn_td_w1, L1_xattn_td_w2, L1_xattn_u, L1_xattn_Wr, L1_xattn_Wk, L1_xattn_Wv, L1_xattn_Wg, L1_xattn_Wo, L1_xattn_gn_w, L1_xattn_gn_b, L1_xattn_ffn_maa_k, L1_xattn_ffn_maa_r, L1_xattn_Wfk, L1_xattn_Wfr, L1_xattn_Wfv, L2_xattn_ln1_scale, L2_xattn_ln1_offset, L2_xattn_wq1, L2_xattn_bq1, L2_xattn_wk1, L2_xattn_bk1, L2_xattn_wv1, L2_xattn_bv1, L2_xattn_wo1, L2_xattn_bo1, L2_xattn_bias_k1, L2_xattn_bias_v1, L2_xattn_ln2_scale, L2_xattn_ln2_offset, L2_xattn_wq2, L2_xattn_bq2, L2_xattn_wk2, L2_xattn_bk2, L2_xattn_wv2, L2_xattn_bv2, L2_xattn_wo2, L2_xattn_bo2, L2_xattn_bias_k2, L2_xattn_bias_v2, L2_xattn_ln_mlp_scale, L2_xattn_ln_mlp_offset, L2_xattn_w_fc1, L2_xattn_b_fc1, L2_xattn_w_fc2, L2_xattn_b_fc2, L3_xattn_theta_w, L3_xattn_theta_b, L3_xattn_phi_w, L3_xattn_phi_b, L3_xattn_g_w, L3_xattn_g_b, L3_xattn_w_w, L3_xattn_w_b, L3_xattn_bn_gamma, L3_xattn_bn_beta, L3_xattn_bn_mean, L3_xattn_bn_var):
    import jax
    import jax.numpy as jnp

    def _L0_xattn_ref(x, mask, kv, kv_mask, Wq, bq, Wk, bk, Wv, bv):
        import jax, jax.numpy as jnp
        import numpy as np
        import math
        N_HEADS = 16
        EPS = 1e-05

        def _masked_instance_norm(x, mask):
            m = mask.astype(x.dtype)
            x = x * m
            n_valid = jnp.sum(m, axis=-1, keepdims=True)
            mean = jnp.sum(x, axis=-1, keepdims=True) / n_valid
            var = jnp.sum(x * x, axis=-1, keepdims=True) / n_valid - mean * mean
            x = (x - mean) / jnp.sqrt(jax.nn.relu(var) + EPS)
            return x * m
        bs, c, t1 = x.shape
        h = N_HEADS
        d = c // h
        scale = 1.0 / math.sqrt(d)
        q = jnp.einsum('oc,bct->bot', Wq, x) + bq[None, :, None]
        k = jnp.einsum('oc,bct->bot', Wk, kv) + bk[None, :, None]
        v = jnp.einsum('oc,bct->bot', Wv, kv) + bv[None, :, None]
        q = q.reshape(bs, h, d, t1).transpose(0, 1, 3, 2)
        k = k.reshape(bs, h, d, -1)
        v = v.reshape(bs, h, d, -1).transpose(0, 1, 3, 2)
        attn = jnp.einsum('bhqd,bhdk->bhqk', q * scale, k)
        attn = jnp.where(kv_mask[:, :, None, :], attn, -jnp.inf)
        attn = jax.nn.softmax(attn, axis=-1)
        mean = jnp.einsum('bhqk,bhkd->bhqd', attn, v)
        ex2 = jnp.einsum('bhqk,bhkd->bhqd', attn, v * v)
        std = jnp.sqrt(jax.nn.relu(ex2 - mean * mean))
        mean = mean.transpose(0, 1, 3, 2).reshape(bs, c, t1)
        std = std.transpose(0, 1, 3, 2).reshape(bs, c, t1)
        xn = _masked_instance_norm(x, mask)
        out = (xn * std + mean) * mask.astype(x.dtype)
        return out

    def _L1_xattn_ref(x, state, ln1_w, ln1_b, ln2_w, ln2_b, maa_x, maa_w1, maa_w2, maa_stack, time_decay, td_w1, td_w2, u, Wr, Wk, Wv, Wg, Wo, gn_w, gn_b, ffn_maa_k, ffn_maa_r, Wfk, Wfr, Wfv):
        import jax, jax.numpy as jnp
        import numpy as np
        E, H, L, B = (512, 32, 256, 4)
        S = E // H
        DM, DD = (32, 64)

        def _ln(x, w, b, eps=1e-05):
            m = x.mean(-1, keepdims=True)
            v = ((x - m) ** 2).mean(-1, keepdims=True)
            return (x - m) / jnp.sqrt(v + eps) * w + b

        def _block(x, state, ln1_w, ln1_b, ln2_w, ln2_b, maa_x, maa_w1, maa_w2, maa_stack, time_decay, td_w1, td_w2, u, Wr, Wk, Wv, Wg, Wo, gn_w, gn_b, ffn_maa_k, ffn_maa_r, Wfk, Wfr, Wfv):
            b, l, e = x.shape
            h = u.shape[0]
            s_ = e // h
            xa = _ln(x, ln1_w, ln1_b)
            sx = jnp.concatenate([state[:, 1:2] - xa[:, :1], xa[:, :-1] - xa[:, 1:]], axis=1)
            xxx = jnp.tanh((xa + sx * maa_x) @ maa_w1).reshape(b, l, 5, DM)
            xxx = jnp.einsum('blfd,fde->blfe', xxx, maa_w2)
            xm = xa[:, :, None] + sx[:, :, None] * (maa_stack + xxx)
            xk, xw, xv, xr, xg = (xm[:, :, j] for j in range(5))
            w = jnp.exp(-jnp.exp(time_decay + jnp.tanh(xw @ td_w1) @ td_w2)).reshape(b, l, h, s_)
            r = (xr @ Wr.T).reshape(b, l, h, s_)
            k = (xk @ Wk.T).reshape(b, l, h, s_)
            v = (xv @ Wv.T).reshape(b, l, h, s_)
            g = jax.nn.silu(xg @ Wg.T)
            s0 = state[:, 2:2 + s_].reshape(b, h, s_, s_)

            def step(s, rkvw):
                r_t, k_t, v_t, w_t = rkvw
                a = k_t[..., :, None] * v_t[..., None, :]
                out = jnp.einsum('bhi,bhij->bhj', r_t, u * a + s)
                s = a + w_t[..., :, None] * s
                return (s, out)
            rkvw = tuple((jnp.moveaxis(t, 1, 0) for t in (r, k, v, w)))
            _, out = jax.lax.scan(step, s0, rkvw)
            out = jnp.moveaxis(out, 0, 1).reshape(b, l, e)
            og = out.reshape(b, l, h, s_)
            m = og.mean(-1, keepdims=True)
            va = ((og - m) ** 2).mean(-1, keepdims=True)
            og = ((og - m) / jnp.sqrt(va + 1e-05)).reshape(b, l, e) * gn_w + gn_b
            x1 = x + og * g @ Wo.T
            xc = _ln(x1, ln2_w, ln2_b)
            sx2 = jnp.concatenate([state[:, 0:1] - xc[:, :1], xc[:, :-1] - xc[:, 1:]], axis=1)
            xk2 = xc + sx2 * ffn_maa_k
            xr2 = xc + sx2 * ffn_maa_r
            rr = jax.nn.sigmoid(xr2 @ Wfr.T)
            kk = jnp.square(jax.nn.relu(xk2 @ Wfk.T))
            return x1 + rr * (kk @ Wfv.T)
        return _block(x, state, ln1_w, ln1_b, ln2_w, ln2_b, maa_x, maa_w1, maa_w2, maa_stack, time_decay, td_w1, td_w2, u, Wr, Wk, Wv, Wg, Wo, gn_w, gn_b, ffn_maa_k, ffn_maa_r, Wfk, Wfr, Wfv)

    def _L2_xattn_ref(x, xf_1, xf_2, ln1_scale, ln1_offset, wq1, bq1, wk1, bk1, wv1, bv1, wo1, bo1, bias_k1, bias_v1, ln2_scale, ln2_offset, wq2, bq2, wk2, bk2, wv2, bv2, wo2, bo2, bias_k2, bias_v2, ln_mlp_scale, ln_mlp_offset, w_fc1, b_fc1, w_fc2, b_fc2):
        import jax, jax.numpy as jnp
        import numpy as np
        B, Q, S1, S2 = (4, 64, 512, 512)
        D, H, K, F = (512, 16, 128, 2048)
        LN_EPS = 1e-05

        def _layer_norm(x, scale, offset):
            mu = jnp.mean(x, axis=-1, keepdims=True)
            var = jnp.var(x, axis=-1, keepdims=True)
            return (x - mu) * jax.lax.rsqrt(var + LN_EPS) * scale + offset

        def _cross_attention(q_in, kv_in, wq, bq, wk, bk, wv, bv, wo, bo, bias_k, bias_v):
            b, q_len, _ = q_in.shape
            t = kv_in.shape[1]
            qh = (q_in @ wq + bq).reshape(b, q_len, H, K)
            kh = (kv_in @ wk + bk).reshape(b, t, H, K)
            vh = (kv_in @ wv + bv).reshape(b, t, H, K)
            kh = jnp.concatenate([kh, jnp.broadcast_to(bias_k, (b, 1, H, K))], axis=1)
            vh = jnp.concatenate([vh, jnp.broadcast_to(bias_v, (b, 1, H, K))], axis=1)
            scale = jnp.sqrt(jnp.asarray(K, q_in.dtype))
            logits = jnp.einsum('bqhk,bthk->bhqt', qh, kh) / scale
            weights = jax.nn.softmax(logits, axis=-1)
            ctx = jnp.einsum('bhqt,bthk->bqhk', weights, vh).reshape(b, q_len, H * K)
            return ctx @ wo + bo

        def _forward(x, xf_1, xf_2, ln1_scale, ln1_offset, wq1, bq1, wk1, bk1, wv1, bv1, wo1, bo1, bias_k1, bias_v1, ln2_scale, ln2_offset, wq2, bq2, wk2, bk2, wv2, bv2, wo2, bo2, bias_k2, bias_v2, ln_mlp_scale, ln_mlp_offset, w_fc1, b_fc1, w_fc2, b_fc2):
            res = x
            h = _layer_norm(x, ln1_scale, ln1_offset)
            x = res + _cross_attention(h, xf_1, wq1, bq1, wk1, bk1, wv1, bv1, wo1, bo1, bias_k1, bias_v1)
            res = x
            h = _layer_norm(x, ln2_scale, ln2_offset)
            x = res + _cross_attention(h, xf_2, wq2, bq2, wk2, bk2, wv2, bv2, wo2, bo2, bias_k2, bias_v2)
            h = _layer_norm(x, ln_mlp_scale, ln_mlp_offset)
            h = jax.nn.gelu(h @ w_fc1 + b_fc1, approximate=False) @ w_fc2 + b_fc2
            return x + h
        return _forward(x, xf_1, xf_2, ln1_scale, ln1_offset, wq1, bq1, wk1, bk1, wv1, bv1, wo1, bo1, bias_k1, bias_v1, ln2_scale, ln2_offset, wq2, bq2, wk2, bk2, wv2, bv2, wo2, bo2, bias_k2, bias_v2, ln_mlp_scale, ln_mlp_offset, w_fc1, b_fc1, w_fc2, b_fc2)

    def _L3_xattn_ref(x, x_2, theta_w, theta_b, phi_w, phi_b, g_w, g_b, w_w, w_b, bn_gamma, bn_beta, bn_mean, bn_var):
        import jax, jax.numpy as jnp
        import numpy as np
        B, C, CI, N = (16, 256, 128, 512)
        EPS = 1e-05

        def _conv1x1(w, b, x):
            return jnp.einsum('oc,bcn->bon', w, x) + b[None, :, None]
        g_x = _conv1x1(g_w, g_b, x_2).transpose(0, 2, 1)
        theta_x = _conv1x1(theta_w, theta_b, x).transpose(0, 2, 1)
        phi_x = _conv1x1(phi_w, phi_b, x_2)
        W = jnp.einsum('bnc,bcm->bnm', theta_x, phi_x) / phi_x.shape[-1]
        y = jnp.einsum('bnm,bmc->bnc', W, g_x).transpose(0, 2, 1)
        wy = _conv1x1(w_w, w_b, y)
        inv_std = jax.lax.rsqrt(bn_var + EPS)
        wy = bn_gamma[None, :, None] * (wy - bn_mean[None, :, None]) * inv_std[None, :, None] + bn_beta[None, :, None]
        return wy + x
    x = _L0_xattn_ref(x, mask_Bx1x2048_bf1, ctx_2048, mask_Bx1x2048_bf1, L0_xattn_Wq, L0_xattn_bq, L0_xattn_Wk, L0_xattn_bk, L0_xattn_Wv, L0_xattn_bv)
    x = _L1_xattn_ref(x, ctx_2048, L1_xattn_ln1_w, L1_xattn_ln1_b, L1_xattn_ln2_w, L1_xattn_ln2_b, L1_xattn_maa_x, L1_xattn_maa_w1, L1_xattn_maa_w2, L1_xattn_maa_stack, L1_xattn_time_decay, L1_xattn_td_w1, L1_xattn_td_w2, L1_xattn_u, L1_xattn_Wr, L1_xattn_Wk, L1_xattn_Wv, L1_xattn_Wg, L1_xattn_Wo, L1_xattn_gn_w, L1_xattn_gn_b, L1_xattn_ffn_maa_k, L1_xattn_ffn_maa_r, L1_xattn_Wfk, L1_xattn_Wfr, L1_xattn_Wfv)
    x = _L2_xattn_ref(x, ctx_2048, ctx_2048, L2_xattn_ln1_scale, L2_xattn_ln1_offset, L2_xattn_wq1, L2_xattn_bq1, L2_xattn_wk1, L2_xattn_bk1, L2_xattn_wv1, L2_xattn_bv1, L2_xattn_wo1, L2_xattn_bo1, L2_xattn_bias_k1, L2_xattn_bias_v1, L2_xattn_ln2_scale, L2_xattn_ln2_offset, L2_xattn_wq2, L2_xattn_bq2, L2_xattn_wk2, L2_xattn_bk2, L2_xattn_wv2, L2_xattn_bv2, L2_xattn_wo2, L2_xattn_bo2, L2_xattn_bias_k2, L2_xattn_bias_v2, L2_xattn_ln_mlp_scale, L2_xattn_ln_mlp_offset, L2_xattn_w_fc1, L2_xattn_b_fc1, L2_xattn_w_fc2, L2_xattn_b_fc2)
    x = _L3_xattn_ref(x, ctx_2048, L3_xattn_theta_w, L3_xattn_theta_b, L3_xattn_phi_w, L3_xattn_phi_b, L3_xattn_g_w, L3_xattn_g_b, L3_xattn_w_w, L3_xattn_w_b, L3_xattn_bn_gamma, L3_xattn_bn_beta, L3_xattn_bn_mean, L3_xattn_bn_var)
    return x

_drawn_inputs = setup_inputs


def setup_inputs(seed=0):
    import zlib

    import numpy as np

    out = dict(_drawn_inputs(seed))
    spreads = {'L0_xattn_bq': (0.0, 0.396),
     'L0_xattn_bk': (0.0, 2.0),
     'L0_xattn_bv': (0.0, 0.1),
     'L1_xattn_ln1_w': (1.0, 0.2),
     'L1_xattn_ln1_b': (0.0, 0.491),
     'L1_xattn_ln2_w': (1.0, 0.6),
     'L1_xattn_ln2_b': (0.0, 0.8),
     'L1_xattn_gn_w': (1.0, 0.6),
     'L1_xattn_gn_b': (0.0, 0.8),
     'L2_xattn_ln1_scale': (1.0, 0.6),
     'L2_xattn_ln1_offset': (0.0, 0.8),
     'L2_xattn_bq1': (0.0, 0.8),
     'L2_xattn_bk1': (0.0, 2.0),
     'L2_xattn_bv1': (0.0, 0.1),
     'L2_xattn_bo1': (0.0, 0.1),
     'L2_xattn_ln2_scale': (1.0, 0.6),
     'L2_xattn_ln2_offset': (0.0, 0.8),
     'L2_xattn_bq2': (0.0, 0.8),
     'L2_xattn_bk2': (0.0, 2.0),
     'L2_xattn_bv2': (0.0, 0.1),
     'L2_xattn_bo2': (0.0, 0.1),
     'L2_xattn_ln_mlp_scale': (1.0, 0.565),
     'L2_xattn_ln_mlp_offset': (0.0, 0.639),
     'L2_xattn_b_fc1': (0.0, 0.277),
     'L2_xattn_b_fc2': (0.0, 0.1)}
    factors = {'L1_xattn_maa_x': 8.0,
     'L1_xattn_maa_w1': 5.201,
     'L1_xattn_maa_w2': 5.165,
     'L1_xattn_td_w1': 8.0,
     'L1_xattn_td_w2': 8.0,
     'L1_xattn_u': 5.335,
     'L1_xattn_ffn_maa_k': 8.0,
     'L1_xattn_ffn_maa_r': 8.0,
     'L1_xattn_Wfr': 7.279,
     'L2_xattn_wq1': 6.5,
     'L2_xattn_wk1': 6.386,
     'L2_xattn_bias_k1': 64.0,
     'L2_xattn_bias_v1': 64.0,
     'L2_xattn_wq2': 6.307,
     'L2_xattn_wk2': 6.182,
     'L2_xattn_bias_k2': 64.0,
     'L2_xattn_bias_v2': 64.0,
     'L3_xattn_theta_w': 3.228,
     'L3_xattn_theta_b': 8.0,
     'L3_xattn_phi_w': 2.976,
     'L3_xattn_phi_b': 8.0,
     'L3_xattn_g_w': 3.274,
     'L3_xattn_g_b': 8.0,
     'L3_xattn_w_w': 3.01,
     'L3_xattn_w_b': 4.471}
    for name, (base, spread) in spreads.items():
        noise = np.random.default_rng([zlib.crc32(name.encode()), seed]).standard_normal(out[name].shape)
        drawn = base * np.exp(spread * noise) if base else spread * noise
        out[name] = jnp.asarray(drawn.astype(out[name].dtype))
    for name, factor in factors.items():
        out[name] = (out[name] * factor).astype(out[name].dtype)
    return out
```

```python
from contextlib import ExitStack

import concourse.bass as bass
from concourse import mybir

B, L, E = 8, 256, 512
P = 128
EC = E // P
LC = L // P
LN_EPS = 1e-5

H0, D0 = 16, L // 16
G0 = 4
HG = H0 // G0
CG = HG * D0
ROW_MASK, ROW_MAX = D0, D0 + 1
NEG = -1e30

F32 = mybir.dt.float32
U8 = mybir.dt.uint8
ALU = mybir.AluOpType
ACT = mybir.ActivationFunctionType
AX = mybir.AxisListType


AHEAD = 16


def start_ahead(eng, semaphores):
    for semaphore in semaphores:
        eng.sem_inc(semaphore, AHEAD)


def layer0(nc, x, xT, ctx, mask_row, mask_col, wqk, qkb, aug, wv, bv, mask_sel, ident_in, x1T):
    with ExitStack() as stack:
        def sb(name, shape, dt=F32):
            return stack.enter_context(nc.sbuf_tensor("a_" + name, shape, dt))

        sems = []

        def sem(name):
            sems.append(stack.enter_context(nc.semaphore("a_" + name)))
            return sems[-1]

        def dma_sem(name):
            return stack.enter_context(nc.semaphore("a_" + name))

        X = sb("x", [P, LC, E])
        C = sb("ctx", [P, LC, E])
        WQK = sb("wqk", [P, LC, 2, P])
        WV = sb("wv", [P, LC, CG])
        QKB = sb("qkb", [P, 2])
        AUG = sb("aug", [P, 2])
        BV = sb("bv", [1, CG])
        MSEL = sb("msel", [1, P])
        M8R = sb("m8r", [1, E], U8)
        MROW = sb("mrow", [1, E])
        M8C = sb("m8c", [P, EC], U8)
        MCOL = sb("mcol", [P, EC])
        XT = sb("xT", [P, EC, CG])
        XM = sb("xm", [P, EC, CG])
        XQ = sb("xq", [P, EC, CG])
        ID = sb("id", [P, P])
        ONES = sb("ones", [P, P])
        EPS = sb("eps", [P, 1])
        QA = sb("qa", [P, 2, E])
        KA = sb("ka", [P, 2, E])
        QB = sb("qb", [P, 2, 2])
        NM = sb("nm", [P, 2, HG * EC])
        NMT = sb("nmT", [HG * EC, 2, P])
        VA = sb("va", [P, 2, EC, HG, 2 * D0 + 1])
        EX = sb("ex", [P, 2, EC, E])
        U = sb("u", [P, EC, HG, 2 * D0 + 1])
        R = sb("r", [P, EC, HG, 1])
        MEAN = sb("mean", [P, EC, HG, D0])
        EX2 = sb("ex2", [P, EC, HG, D0])
        SQ = sb("sq", [P, EC, HG, D0])
        STD = sb("std", [P, EC, HG, D0])
        ST = sb("st", [P, 4, CG])
        RN = sb("rn", [P, 1])
        OUT = sb("out", [P, EC, CG])
        ps = stack.enter_context(nc.psum_tensor("a_ps", [P, 8, 512], F32))
        BQ, BK, BS, NBS, BO = 0, 1, 2, 4, 6

        consts_in, inputs_in = sem("consts_in"), sem("inputs_in")
        memset_done, inputs_used = sem("memset_done"), sem("inputs_used")
        prep_done, biased = sem("prep_done"), sem("biased")
        q_ready, k_ready, v_ready = sem("q_ready"), sem("k_ready"), sem("v_ready")
        qa_ready, ka_ready, va_ready, st_read = sem("qa_ready"), sem("ka_ready"), sem("va_ready"), sem("st_read")
        score_ready, score_max, score_exp = sem("score_ready"), sem("score_max"), sem("score_exp")
        nm_ready, nmT_ps, nmT_sb, max_in = sem("nm_ready"), sem("nmT_ps"), sem("nmT_sb"), dma_sem("max_in")
        probs_ready, o_ready, o_read = sem("probs_ready"), sem("o_ready"), sem("o_read")
        var_ready, std_ready, out_ready, out_stored = sem("var_ready"), sem("std_ready"), sem("out_ready"), dma_sem("out_stored")
        sq_ready, t_done = sem("sq_ready"), sem("t_done")
        passed, out_free = sem("passed"), sem("out_free")
        N_IN = 9 * 16
        NS = HG * EC
        block = stack.enter_context(nc.Block())

        @block.sync
        def _(sp):
            start_ahead(sp, sems)
            sp.dma_start(AUG[:, :], aug).then_inc(consts_in, 16)
            sp.dma_start(MSEL[:, :], mask_sel).then_inc(consts_in, 16)
            sp.dma_start(ID[:, :], ident_in).then_inc(consts_in, 16)
            with sp.Fori(0, B) as b:
                for g in range(G0):
                    it = b * G0 + g
                    sp.wait_ge(inputs_used, it * 2 + AHEAD)
                    sp.dma_start(X[:, :, :], x[b].rearrange("(k p) t -> p k t", p=P)).then_inc(inputs_in, 16)
                    sp.dma_start(C[:, :, :], ctx[b].rearrange("(k p) t -> p k t", p=P)).then_inc(inputs_in, 16)
                    sp.dma_start(WQK[:, :, :, :], wqk[g]).then_inc(inputs_in, 16)
                    sp.dma_start(WV[:, :, :], wv[g]).then_inc(inputs_in, 16)
                    sp.dma_start(QKB[:, :], qkb[g]).then_inc(inputs_in, 16)
                    sp.dma_start(BV[:, :], bv[g]).then_inc(inputs_in, 16)
                    sp.dma_start(M8R[:, :], mask_row[b]).then_inc(inputs_in, 16)
                    sp.dma_start(M8C[:, :], mask_col[b]).then_inc(inputs_in, 16)
                    sp.dma_start(XT[:, :, :], xT[b].rearrange("(k p) c -> p k c", p=P)[:, :, g * CG:(g + 1) * CG]).then_inc(inputs_in, 16)

        @block.gpsimd
        def _(pool):
            pool.memset(ONES[:, :], 1.0)
            pool.memset(EPS[:, :], LN_EPS)
            pool.memset(VA[:, :, :, :, 2 * D0:], 1.0).then_inc(memset_done, 1)
            with pool.Fori(0, B) as b:
                for g in range(G0):
                    it, s = b * G0 + g, g % 2
                    pool.wait_ge(nmT_sb, it + 1 + AHEAD)
                    pool.sem_inc(passed, 1)
                    for h in range(HG):
                        pool.dma_start(QA[32 * h + ROW_MAX:32 * h + ROW_MAX + 1, s, :],
                                       NMT[h * EC:(h + 1) * EC, s, :]).then_inc(max_in, 16)
                    pool.wait_ge(out_ready, it + 1 + AHEAD)
                    pool.sem_inc(passed, 1)
                    pool.dma_start(x1T[b][:, :, g * CG:(g + 1) * CG], OUT[:, :, :]).then_inc(out_stored, 16)
                    pool.wait_ge(out_stored, (it + 1) * 16)
                    pool.sem_inc(out_free, 1)
        @block.tensor
        def _(pe):
            pe.wait_ge(consts_in, 48 + AHEAD)
            pe.wait_ge(memset_done, 1 + AHEAD)
            with pe.Fori(0, B) as b:
                for g in range(G0):
                    it, s = b * G0 + g, g % 2
                    pe.wait_ge(inputs_in, (it + 1) * N_IN + AHEAD)
                    pe.wait_ge(prep_done, it + 1 + AHEAD)
                    pe.wait_ge(st_read, it + AHEAD)
                    pe.wait_ge(va_ready, it + AHEAD)
                    for k in range(LC):
                        mm = pe.matmul(ps[:, BQ, :], WQK[:, k, 0, :], X[:, k, :], start=(k == 0), stop=(k == LC - 1))
                    mm.then_inc(q_ready, 1)
                    for k in range(LC):
                        pe.matmul(ps[:, BK, :], WQK[:, k, 1, :], C[:, k, :], start=(k == 0), stop=False)
                    pe.matmul(ps[:, BK, :], MSEL[:, :], MROW[:, :], start=False, stop=True).then_inc(k_ready, 1)
                    pe.wait_ge(qa_ready, it + 1 + AHEAD)
                    pe.wait_ge(ka_ready, it + 1 + AHEAD)
                    for h in range(HG):
                        rows = slice(32 * h, 32 * h + ROW_MASK + 1)
                        for c in range(EC):
                            n = h * EC + c
                            if n < NBS:
                                pe.wait_ge(score_exp, it * NS + AHEAD)
                            else:
                                pe.wait_ge(score_max, it * NS + n - NBS + 1 + AHEAD)
                            pe.matmul(ps[:, BS + n % NBS, :], QA[rows, s, c * P:(c + 1) * P], KA[rows, s, :],
                                      start=True, stop=True).then_inc(score_ready, 1)
                    for c in range(EC):
                        for k in range(LC):
                            pe.matmul(ps[:, BQ, c * CG:(c + 1) * CG], C[:, k, c * P:(c + 1) * P], WV[:, k, :],
                                      start=(k == 0), stop=False, skip_group_check=True)
                        mm = pe.matmul(ps[:, BQ, c * CG:(c + 1) * CG], ONES[0:1, :], BV[:, :],
                                       start=False, stop=True, skip_group_check=True)
                    mm.then_inc(v_ready, 1)
                    for c in range(EC):
                        pe.matmul(ps[:, BK, 0:CG], ONES[:, :], XM[:, c, :], start=(c == 0), stop=(c == EC - 1),
                                  skip_group_check=True)
                    for c in range(EC):
                        pe.matmul(ps[:, BK, CG:2 * CG], ONES[:, :], XQ[:, c, :], start=(c == 0), stop=(c == EC - 1),
                                  skip_group_check=True)
                    for c in range(EC):
                        pe.matmul(ps[:, BK, 2 * CG:2 * CG + 1], ONES[:, :], MCOL[:, c:c + 1], start=(c == 0),
                                       stop=(c == EC - 1), skip_group_check=True)
                    
                    pe.wait_ge(nm_ready, it + 1 + AHEAD)
                    pe.transpose(ps[0:NS, BK, 256:256 + P], NM[:, s, :], ID[:, :]).then_inc(nmT_ps, 1)
                    pe.wait_ge(max_in, (it + 1) * HG * 16)
                    pe.wait_ge(va_ready, it + 1 + AHEAD)
                    for h in range(HG):
                        rows = slice(32 * h, 32 * h + ROW_MAX + 1)

                        def weighted(h):
                            for q in range(EC):
                                for k in range(EC):
                                    if q == 0:
                                        pe.wait_ge(probs_ready, it * NS + h * EC + k + 1 + AHEAD)
                                    if q == 0 and k == 0:
                                        if h < 2:
                                            pe.wait_ge(o_read, it * HG + AHEAD)
                                        else:
                                            pe.wait_ge(o_read, it * HG + h - 1 + AHEAD)
                                    mm = pe.matmul(ps[:, BO + h % 2, q * 33:(q + 1) * 33], EX[:, h % 2, k, q * P:(q + 1) * P],
                                                   VA[:, s, k, h, :], start=(k == 0), stop=(k == EC - 1),
                                                   skip_group_check=True)
                            mm.then_inc(o_ready, 1)

                        for k in range(EC):
                            n = h * EC + k
                            if n < NBS:
                                pe.wait_ge(score_max, (it + 1) * NS + AHEAD)
                            else:
                                pe.wait_ge(score_exp, it * NS + n - NBS + 1 + AHEAD)
                            pe.matmul(ps[:, BS + n % NBS, :], KA[rows, s, k * P:(k + 1) * P], QA[rows, s, :],
                                      start=True, stop=True).then_inc(t_done, 1)
                        if h > 0:
                            weighted(h - 1)
                    weighted(HG - 1)

        @block.scalar
        def _(act):
            act.wait_ge(memset_done, 1 + AHEAD)
            with act.Fori(0, B) as b:
                for g in range(G0):
                    it, s = b * G0 + g, g % 2
                    act.wait_ge(prep_done, it + 1 + AHEAD)
                    act.wait_ge(k_ready, it + 1 + AHEAD)
                    act.activation(KA[:, s, :], ps[:, BK, :], ACT.Identity, bias=QB[:, 0, 1:2]).then_inc(ka_ready, 1)
                    act.wait_ge(v_ready, it + 1 + AHEAD)
                    pv = ps[:, BQ, 0:EC * CG].rearrange("p (t h d) -> p t h d", t=EC, h=HG)
                    act.activation(VA[:, s, :, :, 0:D0], pv, ACT.Copy)
                    act.activation(VA[:, s, :, :, D0:2 * D0], pv, ACT.Square).then_inc(va_ready, 1)
                    for h in range(HG):
                        for k in range(EC):
                            n = h * EC + k
                            act.wait_ge(t_done, it * NS + n + 1 + AHEAD)
                            if k == 0:
                                if h < 2:
                                    act.wait_ge(o_ready, it * HG + AHEAD)
                                else:
                                    act.wait_ge(o_ready, it * HG + h - 1 + AHEAD)
                            act.activation(EX[:, h % 2, k, :], ps[:, BS + n % NBS, :], ACT.Exp)\
                               .then_inc(probs_ready, 1)
                            act.drain().then_inc(score_exp, 1)
                    act.wait_ge(var_ready, it + 1 + AHEAD)
                    act.activation(STD[:, :, :, :], EX2[:, :, :, :], ACT.Sqrt)
                    act.activation(ST[:, 3, :], ST[:, 2, :], ACT.Sqrt, bias=EPS[:, 0:1]).then_inc(std_ready, 1)

        @block.vector
        def _(dve):
            dve.wait_ge(consts_in, 48 + AHEAD)
            with dve.Fori(0, B) as b:
                for g in range(G0):
                    it, s = b * G0 + g, g % 2
                    dve.wait_ge(inputs_in, (it + 1) * N_IN + AHEAD)
                    dve.tensor_copy(MCOL[:, :], M8C[:, :])
                    dve.tensor_copy(MROW[:, :], M8R[:, :])
                    dve.tensor_tensor(QB[:, 0, :], QKB[:, :], AUG[:, :], ALU.add)
                    dve.drain()
                    dve.tensor_scalar(MROW[:, :], MROW[:, :], -NEG, NEG, ALU.mult, ALU.add)
                    dve.tensor_tensor(XM[:, :, :], XT[:, :, :], MCOL[:, :].unsqueeze(2).broadcast_to([P, EC, CG]), ALU.mult)
                    dve.drain()
                    dve.tensor_tensor(XQ[:, :, :], XM[:, :, :], XM[:, :, :], ALU.mult).then_inc(prep_done, 1)
                    dve.wait_ge(q_ready, it + 1 + AHEAD)
                    dve.tensor_scalar(QA[:, s, :], ps[:, BQ, :], QB[:, 0, 0:1], float(D0) ** -0.5, ALU.add, ALU.mult)\
                       .then_inc(qa_ready, 1)
                    for n in range(NS):
                        dve.wait_ge(score_ready, it * NS + n + 1 + AHEAD)
                        dve.tensor_reduce(NM[:, s, n:n + 1], ps[:, BS + n % NBS, :], AX.X, ALU.max, negate=True)\
                           .then_inc(score_max, 1)
                    dve.drain().then_inc(nm_ready, 1)
                    dve.wait_ge(nmT_ps, it + 1 + AHEAD)
                    dve.tensor_copy(NMT[:, s, :], ps[0:NS, BK, 256:256 + P]).then_inc(nmT_sb, 1)
                    dve.reciprocal(RN[:, :], ps[:, BK, 2 * CG:2 * CG + 1])
                    dve.drain()
                    dve.tensor_scalar(ST[:, 0, :], ps[:, BK, 0:CG], RN[:, 0:1], None, ALU.mult)
                    dve.tensor_scalar(ST[:, 1, :], ps[:, BK, CG:2 * CG], RN[:, 0:1], None, ALU.mult)
                    dve.drain()
                    dve.tensor_tensor(ST[:, 2, :], ST[:, 0, :], ST[:, 0, :], ALU.mult)
                    dve.drain()
                    dve.tensor_tensor(ST[:, 2, :], ST[:, 1, :], ST[:, 2, :], ALU.subtract)
                    dve.drain()
                    dve.tensor_scalar(ST[:, 2, :], ST[:, 2, :], 0.0, None, ALU.max).then_inc(st_read, 1)
                    for h in range(HG):
                        dve.wait_ge(o_ready, it * HG + h + 1 + AHEAD)
                        dve.tensor_copy(U[:, :, h, :], ps[:, BO + h % 2, 0:EC * 33].rearrange("p (q v) -> p q v", q=EC))\
                           .then_inc(o_read, 1)
                    dve.drain()
                    dve.reciprocal(R[:, :, :, :], U[:, :, :, 2 * D0:])
                    dve.drain()
                    for c in range(EC):
                        rb = R[:, c, :, :].broadcast_to([P, HG, D0])
                        dve.tensor_tensor(MEAN[:, c, :, :], U[:, c, :, 0:D0], rb, ALU.mult)
                        dve.tensor_tensor(EX2[:, c, :, :], U[:, c, :, D0:2 * D0], rb, ALU.mult)
                    dve.drain()
                    dve.tensor_tensor(SQ[:, :, :, :], MEAN[:, :, :, :], MEAN[:, :, :, :], ALU.mult)
                    dve.drain()
                    dve.tensor_tensor(EX2[:, :, :, :], EX2[:, :, :, :], SQ[:, :, :, :], ALU.subtract)
                    dve.drain()
                    dve.tensor_scalar(EX2[:, :, :, :], EX2[:, :, :, :], 0.0, None, ALU.max)
                    dve.drain().then_inc(var_ready, 1)
                    dve.tensor_tensor(XM[:, :, :], XM[:, :, :], ST[:, 0:1, :].broadcast_to([P, EC, CG]), ALU.subtract)
                    dve.wait_ge(std_ready, it + 1 + AHEAD)
                    dve.reciprocal(ST[:, 3, :], ST[:, 3, :])
                    dve.drain()
                    dve.tensor_tensor(XM[:, :, :], XM[:, :, :], ST[:, 3:4, :].broadcast_to([P, EC, CG]), ALU.mult)
                    dve.drain()
                    mb = MCOL[:, :].unsqueeze(2).broadcast_to([P, EC, CG])
                    dve.tensor_tensor(XM[:, :, :], XM[:, :, :], mb, ALU.mult)
                    dve.drain()
                    dve.tensor_tensor(XM[:, :, :], XM[:, :, :], STD[:, :, :, :].rearrange("p t h d -> p t (h d)"), ALU.mult)
                    dve.drain()
                    dve.tensor_tensor(XM[:, :, :], XM[:, :, :], MEAN[:, :, :, :].rearrange("p t h d -> p t (h d)"), ALU.add)
                    dve.drain()
                    dve.wait_ge(out_free, it + AHEAD)
                    dve.tensor_tensor(OUT[:, :, :], XM[:, :, :], mb, ALU.mult).then_inc(out_ready, 1)
                    dve.drain().then_inc(inputs_used, 2)

S1 = 16
DM, DD = 32, 64
(V_LN1W, V_LN1B, V_LN2W, V_LN2B, V_MAAX, V_STACK, V_TD, V_U, V_GNW, V_GNB, V_FK, V_FR) = \
    (0, 1, 2, 3, 4, 5, 10, 11, 12, 13, 14, 15)
NV1 = 16
W_K, W_V, W_R, W_G, W_O, W_FK, W_FR, W_FV = range(8)
MIX_K, MIX_W, MIX_V, MIX_R, MIX_G = range(5)


def layer1(nc, x1T, ctxT, s0, vecs, w8, maa_w1, maa_w2, td_w1, td_w2, sel, selT, blk, x2T):
    with ExitStack() as stack:
        def sb(name, shape, dt=F32):
            return stack.enter_context(nc.sbuf_tensor("b_" + name, shape, dt))

        sems = []

        def sem(name):
            sems.append(stack.enter_context(nc.semaphore("b_" + name)))
            return sems[-1]

        W = sb("w", [P, 8, EC, E])
        W1 = sb("w1", [P, EC, 5 * DM])
        W2A = sb("w2a", [4 * DM, E])
        W2B = sb("w2b", [DM, E])
        TW1 = sb("tw1", [P, EC, DD])
        TW2 = sb("tw2", [DD, E])
        SEL = sb("sel", [P, S1, P])
        SELT = sb("selT", [P, S1, P])
        BO = sb("bo", [P, P])
        BM = sb("bm", [P, P])
        VEC = sb("vec", [P, NV1, EC])
        MEANW = sb("meanw", [P, P])
        EPS = sb("eps", [P, 1])
        X = sb("x", [P, EC, L])
        CT = sb("ct", [P, EC, L])
        S0 = sb("s0", [P, EC, S1])
        XP = sb("xp", [P, EC, L + 1])
        SX = sb("sx", [P, EC, L])
        Z = sb("z", [P, EC, L])
        XC = sb("xc", [P, EC, L])
        SQ = sb("sq", [P, EC, L])
        SD = sb("sd", [P, L])
        XF = sb("xf", [P, 2, EC, L])
        KT, VT, RT, WT, GT, TH, BV, OG = [sb(n, [P, EC, L]) for n in ("kt", "vt", "rt", "wt", "gt", "th", "bv", "og")]
        T0 = sb("t0", [P, L])
        T1 = sb("t1", [DM, L])
        TW = sb("tw", [DD, L])
        A = sb("a", [P, 4, L])
        Y = sb("y", [P, 4, L])
        RC = sb("rc", [P, L])
        SB = sb("sb", [P, S1, L + 1])
        ps = stack.enter_context(nc.psum_tensor("b_ps", [P, 8, 512], F32))

        def pair(bank):
            return ps[:, bank:bank + 2, :].rearrange("p a (c t) -> p (a c) t", c=2)

        PF, PA, PB, SM0, SM1 = pair(0), pair(2), pair(4), ps[:, 6, 0:L], ps[:, 7, 0:L]

        weights_in, x_in, x_used, memset_done = sem("weights_in"), sem("x_in"), sem("x_used"), sem("memset_done")
        ln_in, mean_ps, xc_ready, sq_ready, var_ps, sd_ready = [sem(n) for n in ("ln_in", "mean_ps", "xc_ready", "sq_ready", "var_ps", "sd_ready")]
        z_ready, h_ps, t_ready = sem("z_ready"), sem("h_ps"), sem("t_ready")
        mix_ps, mix_read, mix_ready, proj_ps, proj_read = [sem(n) for n in ("mix_ps", "mix_read", "mix_ready", "proj_ps", "proj_read")]
        tw_ps, tw_ready, w_ready, th_ready = sem("tw_ps"), sem("tw_ready"), sem("w_ready"), sem("th_ready")
        rku_ready, bonus_ps, bonus_read = sem("rku_ready"), sem("bonus_ps"), sem("bonus_read")
        vb_ps, vb_read, s_ready, s_used, y_ready, y_used, o_ps, o_read = [sem(n) for n in ("vb_ps", "vb_read", "s_ready", "s_used", "y_ready", "y_used", "o_ps", "o_read")]
        og_ready, gm_ps, gc_ready, gq_ready, gv_ps, gd_ready = [sem(n) for n in ("og_ready", "gm_ps", "gc_ready", "gq_ready", "gv_ps", "gd_ready")]
        gated, wo_ps, x1_ready = sem("gated"), sem("wo_ps"), sem("x1_ready")
        ffn_in, ffr_ps, ffk_ps, rr_ready, kk_ready, kk2_ready, ffv_ps = [sem(n) for n in ("ffn_in", "ffr_ps", "ffk_ps", "rr_ready", "kk_ready", "kk2_ready", "ffv_ps")]
        out_ready, out_stored = sem("out_ready"), sem("out_stored")
        passed = sem("passed")
        NLN = 2
        block = stack.enter_context(nc.Block())

        @block.sync
        def _(sp):
            start_ahead(sp, sems)
            for dst, src in ((W[:, :, :, :], w8), (W1[:, :, :], maa_w1), (W2A[:, :], maa_w2[0:4 * DM]), (W2B[:, :], maa_w2[4 * DM:]),
                             (TW1[:, :, :], td_w1), (TW2[:, :], td_w2), (SEL[:, :, :], sel), (SELT[:, :, :], selT),
                             (BO[:, :], blk[0]), (BM[:, :], blk[1]), (VEC[:, :, :], vecs)):
                sp.dma_start(dst, src).then_inc(weights_in, 16)
            with sp.Fori(0, B) as b:
                sp.wait_ge(x_used, b + AHEAD)
                sp.dma_start(X[:, :, :], x1T[b]).then_inc(x_in, 16)
                sp.dma_start(CT[:, :, :], ctxT[b].rearrange("(k p) c -> p k c", p=P)).then_inc(x_in, 16)
                sp.dma_start(S0[:, :, :], s0[b]).then_inc(x_in, 16)
                sp.wait_ge(out_ready, b + 1 + AHEAD)
                sp.dma_start(x2T[b], OG[:, :, :]).then_inc(out_stored, 16)
            sp.wait_ge(out_stored, 16 * B + AHEAD)
        def project(pe, out, w, src):
            for o in range(EC):
                for k in range(EC):
                    mm = pe.matmul(out[:, o, :], W[:, w, k, o * P:(o + 1) * P], src[:, k, :], start=(k == 0),
                                   stop=(k == EC - 1), skip_group_check=True)
            return mm

        @block.tensor
        def _(pe):
            pe.wait_ge(weights_in, 16 * 11 + AHEAD)
            pe.wait_ge(memset_done, 1 + AHEAD)
            def norm(n, src):
                pe.wait_ge(ln_in, n + 1 + AHEAD)
                for k in range(EC):
                    mm = pe.matmul(SM0, MEANW[:, :], src[:, k, :], start=(k == 0), stop=(k == EC - 1))
                mm.then_inc(mean_ps, 1)
                pe.wait_ge(sq_ready, n + 1 + AHEAD)
                for k in range(EC):
                    mm = pe.matmul(SM1, MEANW[:, :], SQ[:, k, :], start=(k == 0), stop=(k == EC - 1))
                mm.then_inc(var_ps, 1)

            with pe.Fori(0, B) as b:
                norm(b * NLN, X)
                pe.wait_ge(z_ready, b + 1 + AHEAD)
                for k in range(EC):
                    pe.matmul(SM0, W1[:, k, 0:P], Z[:, k, :], start=(k == 0), stop=(k == EC - 1))
                for k in range(EC):
                    mm = pe.matmul(SM1[0:DM, :], W1[:, k, P:], Z[:, k, :], start=(k == 0), stop=(k == EC - 1))
                mm.then_inc(h_ps, 1)
                pe.wait_ge(t_ready, b + 1 + AHEAD)
                def mix(f):
                    if f > 0:
                        pe.wait_ge(mix_read, b * 5 + f + AHEAD)
                    for o in range(EC):
                        if f < 4:
                            lo, hi = W2A[f * DM:(f + 1) * DM, o * P:(o + 1) * P], T0[f * DM:(f + 1) * DM, :]
                        else:
                            lo, hi = W2B[:, o * P:(o + 1) * P], T1[:, :]
                        mm = pe.matmul(PF[:, o, :], lo, hi, start=True, stop=True)
                    mm.then_inc(mix_ps, 1)

                mix(0)
                for f in range(5):
                    if f < 4:
                        mix(f + 1)
                    pe.wait_ge(mix_ready, b * 5 + f + 1 + AHEAD)
                    if f >= 2:
                        pe.wait_ge(proj_read, b * 5 + f - 1 + AHEAD)
                    dst = PA if f % 2 == 0 else PB
                    if f == MIX_W:
                        for k in range(EC):
                            mm = pe.matmul(SM0[0:DD, :], TW1[:, k, :], XF[:, f % 2, k, :], start=(k == 0), stop=(k == EC - 1))
                        mm.then_inc(tw_ps, 1)
                        pe.wait_ge(tw_ready, b + 1 + AHEAD)
                        for o in range(EC):
                            mm = pe.matmul(dst[:, o, :], TW2[:, o * P:(o + 1) * P], TW[:, :], start=True, stop=True)
                    else:
                        mm = project(pe, dst, {MIX_K: W_K, MIX_V: W_V, MIX_R: W_R, MIX_G: W_G}[f], XF[:, f % 2])
                    mm.then_inc(proj_ps, 1)
                pe.wait_ge(rku_ready, b + 1 + AHEAD)
                pe.wait_ge(proj_read, b * 5 + 5 + AHEAD)
                for o in range(EC):
                    mm = pe.matmul(PA[:, o, :], BO[:, :], Z[:, o, :], start=True, stop=True)
                mm.then_inc(bonus_ps, 1)
                pe.wait_ge(bonus_read, b + 1 + AHEAD)
                pe.sem_inc(passed, 1)
                with pe.Fori(0, EC) as c:
                    st = b * EC + c
                    pe.wait_ge(o_read, st + AHEAD)
                    def spread(j):
                        if j >= 4:
                            pe.wait_ge(vb_read, st * S1 + j - 3 + AHEAD)
                        else:
                            pe.wait_ge(vb_read, st * S1 + AHEAD)
                        pe.matmul(ps[:, j % 4, 0:L], SEL[:, j, :], VT[:, c, :], start=True, stop=True).then_inc(vb_ps, 1)

                    for j in range(3):
                        spread(j)
                    for j in range(S1):
                        if j + 3 < S1:
                            spread(j + 3)
                        pe.wait_ge(y_ready, st * S1 + j + 1 + AHEAD)
                        pe.matmul(SM0, SELT[:, j, :], Y[:, j % 4, :], start=(j == 0), stop=(j == S1 - 1)).then_inc(y_used, 1)
                pe.wait_ge(og_ready, b + 1 + AHEAD)
                for o in range(EC):
                    mm = pe.matmul(PA[:, o, :], BM[:, :], OG[:, o, :], start=True, stop=True)
                mm.then_inc(gm_ps, 1)
                pe.wait_ge(gq_ready, b + 1 + AHEAD)
                for o in range(EC):
                    mm = pe.matmul(PB[:, o, :], BM[:, :], SQ[:, o, :], start=True, stop=True)
                mm.then_inc(gv_ps, 1)
                pe.wait_ge(gated, b + 1 + AHEAD)
                project(pe, PA, W_O, Z).then_inc(wo_ps, 1)
                norm(b * NLN + 1, X)
                pe.wait_ge(ffn_in, b + 1 + AHEAD)
                project(pe, PA, W_FR, XF[:, 0]).then_inc(ffr_ps, 1)
                project(pe, PB, W_FK, XF[:, 1]).then_inc(ffk_ps, 1)
                pe.wait_ge(kk2_ready, b + 1 + AHEAD)
                pe.wait_ge(rr_ready, b + 1 + AHEAD)
                project(pe, PA, W_FV, KT).then_inc(ffv_ps, 1)

        @block.scalar
        def _(act):
            act.wait_ge(weights_in, 16 * 11 + AHEAD)
            act.wait_ge(memset_done, 1 + AHEAD)
            def norm(n):
                act.wait_ge(xc_ready, n + 1 + AHEAD)
                act.activation(SQ[:, :, :], XC[:, :, :], ACT.Square).then_inc(sq_ready, 1)
                act.wait_ge(var_ps, n + 1 + AHEAD)
                act.activation(SD[:, :], SM1, ACT.Sqrt, bias=EPS[:, 0:1]).then_inc(sd_ready, 1)

            with act.Fori(0, B) as b:
                norm(b * NLN)
                act.wait_ge(h_ps, b + 1 + AHEAD)
                act.activation(T0[:, :], SM0, ACT.Tanh)
                act.activation(T1[:, :], SM1[0:DM, :], ACT.Tanh).then_inc(t_ready, 1)
                act.wait_ge(proj_ps, b * 5 + 1 + AHEAD)
                act.activation(KT[:, :, :], PA, ACT.Copy).then_inc(proj_read, 1)
                act.wait_ge(tw_ps, b + 1 + AHEAD)
                act.activation(TW[:, :], SM0[0:DD, :], ACT.Tanh).then_inc(tw_ready, 1)
                act.wait_ge(proj_ps, b * 5 + 2 + AHEAD)
                for o in range(EC):
                    act.activation(TH[:, o, :], PB[:, o, :], ACT.Exp, bias=VEC[:, V_TD, o:o + 1])
                act.drain().then_inc(proj_read, 1)
                act.activation(WT[:, :, :], TH[:, :, :], ACT.Exp, scale=-1.0).then_inc(w_ready, 1)
                act.wait_ge(proj_ps, b * 5 + 3 + AHEAD)
                act.activation(VT[:, :, :], PA, ACT.Copy).then_inc(proj_read, 1)
                act.wait_ge(proj_ps, b * 5 + 4 + AHEAD)
                act.activation(RT[:, :, :], PB, ACT.Copy).then_inc(proj_read, 1)
                act.wait_ge(proj_ps, b * 5 + 5 + AHEAD)
                act.activation(TH[:, :, :], PA, ACT.Tanh, scale=0.5).then_inc(th_ready, 1)
                act.wait_ge(gc_ready, b + 1 + AHEAD)
                act.activation(SQ[:, :, :], XC[:, :, :], ACT.Square).then_inc(gq_ready, 1)
                act.wait_ge(gv_ps, b + 1 + AHEAD)
                act.activation(TH[:, :, :], PB, ACT.Sqrt, bias=EPS[:, 0:1]).then_inc(gd_ready, 1)
                norm(b * NLN + 1)
                act.wait_ge(ffr_ps, b + 1 + AHEAD)
                act.activation(RT[:, :, :], PA, ACT.Tanh, scale=0.5).then_inc(rr_ready, 1)
                act.wait_ge(ffk_ps, b + 1 + AHEAD)
                act.activation(KT[:, :, :], PB, ACT.Relu).then_inc(kk_ready, 1)

        @block.gpsimd
        def _(pool):
            pool.memset(MEANW[:, :], 1.0 / E)
            pool.memset(EPS[:, :], LN_EPS).then_inc(memset_done, 1)
            with pool.Fori(0, B) as b:
                with pool.Fori(0, EC) as c:
                    st = b * EC + c
                    for j in range(S1):
                        pool.wait_ge(s_ready, st * S1 + j + 1 + AHEAD)
                        if j >= 4:
                            pool.wait_ge(y_used, st * S1 + j - 3 + AHEAD)
                        else:
                            pool.wait_ge(y_used, st * S1 + AHEAD)
                        pool.tensor_tensor(Y[:, j % 4, :], SB[:, j, 0:L], RC[:, :], ALU.mult).then_inc(y_ready, 1)
                pool.wait_ge(kk_ready, b + 1 + AHEAD)
                pool.tensor_tensor(KT[:, :, :], KT[:, :, :], KT[:, :, :], ALU.mult).then_inc(kk2_ready, 1)

        @block.vector
        def _(dve):
            dve.wait_ge(weights_in, 16 * 11 + AHEAD)
            def vec(v, o):
                return VEC[:, v, o:o + 1]

            def norm(n, src, w, bias, prev_col):
                dve.wait_ge(mean_ps, n + 1 + AHEAD)
                dve.tensor_tensor(XC[:, :, :], src[:, :, :], SM0.unsqueeze(1).broadcast_to([P, EC, L]), ALU.subtract)\
                   .then_inc(xc_ready, 1)
                dve.tensor_copy(XP[:, :, 0:1], CT[:, :, prev_col:prev_col + 1])
                dve.wait_ge(sd_ready, n + 1 + AHEAD)
                dve.reciprocal(SD[:, :], SD[:, :])
                dve.drain()
                dve.tensor_tensor(XC[:, :, :], XC[:, :, :], SD[:, :].unsqueeze(1).broadcast_to([P, EC, L]), ALU.mult)
                dve.drain()
                for o in range(EC):
                    dve.tensor_scalar(XP[:, o, 1:L + 1], XC[:, o, :], vec(w, o), vec(bias, o), ALU.mult, ALU.add)
                dve.drain()
                dve.tensor_tensor(SX[:, :, :], XP[:, :, 0:L], XP[:, :, 1:L + 1], ALU.subtract)
                dve.drain()

            with dve.Fori(0, B) as b:
                dve.wait_ge(x_in, (b + 1) * 48 + AHEAD)
                dve.sem_inc(ln_in, 1)
                norm(b * NLN, X, V_LN1W, V_LN1B, 1)
                for o in range(EC):
                    dve.scalar_tensor_tensor(Z[:, o, :], SX[:, o, :], vec(V_MAAX, o), XP[:, o, 1:L + 1], ALU.mult, ALU.add)
                dve.drain().then_inc(z_ready, 1)
                for f in range(5):
                    dve.wait_ge(mix_ps, b * 5 + f + 1 + AHEAD)
                    if f >= 2:
                        dve.wait_ge(proj_ps, b * 5 + f - 1 + AHEAD)
                    for o in range(EC):
                        dve.scalar_tensor_tensor(XF[:, f % 2, o, :], PF[:, o, :], vec(V_STACK + f, o), SX[:, o, :], ALU.add, ALU.mult)
                    dve.drain().then_inc(mix_read, 1)
                    dve.tensor_tensor(XF[:, f % 2], XF[:, f % 2], XP[:, :, 1:L + 1], ALU.add).then_inc(mix_ready, 1)
                dve.wait_ge(th_ready, b + 1 + AHEAD)
                dve.tensor_scalar(TH[:, :, :], TH[:, :, :], 0.5, 0.5, ALU.mult, ALU.add)
                dve.drain()
                dve.tensor_tensor(GT[:, :, :], TH[:, :, :], PA, ALU.mult).then_inc(proj_read, 1)
                dve.tensor_tensor(Z[:, :, :], RT[:, :, :], KT[:, :, :], ALU.mult)
                dve.drain()
                for o in range(EC):
                    dve.tensor_scalar(Z[:, o, :], Z[:, o, :], vec(V_U, o), None, ALU.mult)
                dve.drain().then_inc(rku_ready, 1)
                dve.wait_ge(bonus_ps, b + 1 + AHEAD)
                dve.tensor_tensor(BV[:, :, :], VT[:, :, :], PA, ALU.mult).then_inc(bonus_read, 1)
                dve.wait_ge(w_ready, b + 1 + AHEAD)
                dve.wait_ge(out_stored, b * 16 + AHEAD)
                dve.sem_inc(passed, 1)
                with dve.Fori(0, EC) as c:
                    st = b * EC + c
                    dve.wait_ge(y_ready, st * S1 + AHEAD)
                    dve.tensor_copy(SB[:, :, 0:1], S0[:, c, :].unsqueeze(2))
                    dve.tensor_copy(RC[:, :], RT[:, c, :])
                    for j in range(S1):
                        dve.wait_ge(vb_ps, st * S1 + j + 1 + AHEAD)
                        dve.tensor_tensor(A[:, j % 4, :], KT[:, c, :], ps[:, j % 4, 0:L], ALU.mult).then_inc(vb_read, 1)
                        if j > 0:
                            dve.wait_ge(vb_read, st * S1 + j + AHEAD)
                            dve.tensor_tensor_scan(SB[:, j - 1, 1:L + 1], WT[:, c, :], A[:, (j - 1) % 4, :], S0[:, c, j - 1:j], ALU.mult, ALU.add)\
                               .then_inc(s_ready, 1)
                    dve.drain()
                    dve.tensor_tensor_scan(SB[:, S1 - 1, 1:L + 1], WT[:, c, :], A[:, (S1 - 1) % 4, :], S0[:, c, S1 - 1:S1], ALU.mult, ALU.add)\
                       .then_inc(s_ready, 1)
                    dve.wait_ge(y_used, (st + 1) * S1 + AHEAD)
                    dve.tensor_tensor(OG[:, c, :], BV[:, c, :], SM0, ALU.add).then_inc(o_read, 1)
                dve.drain().then_inc(og_ready, 1)
                dve.wait_ge(gm_ps, b + 1 + AHEAD)
                dve.tensor_tensor(XC[:, :, :], OG[:, :, :], PA, ALU.subtract).then_inc(gc_ready, 1)
                dve.wait_ge(gd_ready, b + 1 + AHEAD)
                dve.reciprocal(TH[:, :, :], TH[:, :, :])
                dve.drain()
                dve.tensor_tensor(XC[:, :, :], XC[:, :, :], TH[:, :, :], ALU.mult)
                dve.drain()
                for o in range(EC):
                    dve.tensor_scalar(XC[:, o, :], XC[:, o, :], vec(V_GNW, o), vec(V_GNB, o), ALU.mult, ALU.add)
                dve.drain()
                dve.tensor_tensor(Z[:, :, :], XC[:, :, :], GT[:, :, :], ALU.mult).then_inc(gated, 1)
                dve.wait_ge(wo_ps, b + 1 + AHEAD)
                dve.tensor_tensor(X[:, :, :], X[:, :, :], PA, ALU.add).then_inc(ln_in, 1)
                dve.drain()
                norm(b * NLN + 1, X, V_LN2W, V_LN2B, 0)
                for o in range(EC):
                    dve.scalar_tensor_tensor(XF[:, 0, o, :], SX[:, o, :], vec(V_FR, o), XP[:, o, 1:L + 1], ALU.mult, ALU.add)
                    dve.scalar_tensor_tensor(XF[:, 1, o, :], SX[:, o, :], vec(V_FK, o), XP[:, o, 1:L + 1], ALU.mult, ALU.add)
                dve.drain().then_inc(ffn_in, 1)
                dve.wait_ge(rr_ready, b + 1 + AHEAD)
                dve.tensor_scalar(RT[:, :, :], RT[:, :, :], 0.5, 0.5, ALU.mult, ALU.add)
                dve.drain()
                dve.wait_ge(ffv_ps, b + 1 + AHEAD)
                dve.tensor_tensor(OG[:, :, :], RT[:, :, :], PA, ALU.mult)
                dve.drain()
                dve.tensor_tensor(OG[:, :, :], OG[:, :, :], X[:, :, :], ALU.add).then_inc(out_ready, 1)
                dve.drain().then_inc(x_used, 1)

H2, K2, F2 = 16, 128, 2048
N2 = 2 * L
FC2 = F2 // P
PACK = 3 * EC * P + 3 + 2 * P
(V2_NW, V2_NB, V2_BO) = range(3)


def layer2(nc, x2T, ctxT, packs, downs, fc1, vec2, ident_in, x3T):
    with ExitStack() as stack:
        def sb(name, shape, dt=F32):
            return stack.enter_context(nc.sbuf_tensor("c_" + name, shape, dt))

        sems = []

        def sem(name):
            sems.append(stack.enter_context(nc.semaphore("c_" + name)))
            return sems[-1]

        def dma_sem(name):
            return stack.enter_context(nc.semaphore("c_" + name))

        X = sb("x", [P, EC, N2])
        CT = sb("ct", [P, EC, N2])
        H = sb("h", [P, EC, N2])
        SQ = sb("sq", [P, EC, N2])
        SD = sb("sd", [P, N2])
        ID = sb("id", [P, P])
        MEANW = sb("meanw", [P, P])
        ONES = sb("ones", [1, P])
        EPS = sb("eps", [P, 1])
        VEC = sb("vec", [P, 3, 3, EC])
        PK = sb("pk", [P, 2, PACK])
        WD = sb("wd", [P, 2, H2, P])
        W1 = sb("w1", [P, 2, EC * P + 1])
        QT = sb("qt", [P, 2, N2])
        KT = sb("kt", [P, 2, 2, L + 1])
        V = sb("v", [P, 2, 4, P])
        NM = sb("nm", [P, 4])
        RS = sb("rs", [P, 4])
        PR = sb("pr", [P, 4, L + 1])
        PT = sb("pt", [P, 2, 2, L])
        PTB = sb("ptb", [1, N2])
        G = sb("g", [P, FC2, N2])
        ps = stack.enter_context(nc.psum_tensor("c_ps", [P, 8, 512], F32))
        BQ, BK, BV, BS, BT, BC = 0, 1, 2, 3, 5, 7

        names = """consts_in x_in ct_in x_used memset_done ln_in mean_ps xc_ready sq_ready var_ps sd_ready h_ready
            pack_used q_ps k_ps v_ps q_ready k_ready v_ready s_ps max_ready exp_ready p_ready t_ps t_ready tb_ps tb_ready
            c_ps c_ready down_ps x_ready fc_used fc_ps fc_ready out_stored passed out_free"""
        S = {n: dma_sem(n) if n == "out_stored" else sem(n) for n in names.split()}
        (consts_in, x_in, ct_in, x_used, memset_done, ln_in, mean_ps, xc_ready, sq_ready, var_ps, sd_ready, h_ready,
         pack_used, q_ps, k_ps, v_ps, q_ready, k_ready, v_ready, s_ps, max_ready, exp_ready, p_ready, t_ps, t_ready, tb_ps,
         tb_ready, c_ps, c_ready, down_ps, x_ready, fc_used, fc_ps, fc_ready, out_stored, passed, out_free) = [S[n] for n in names.split()]
        pack_in = [sem(f"pack_in{i}") for i in range(2)]
        down_in = [dma_sem(f"down_in{i}") for i in range(2)]
        fc_in = [dma_sem(f"fc_in{i}") for i in range(2)]
        NPAIR = B // 2
        block = stack.enter_context(nc.Block())

        def weights(u, which):
            return PK[:, u, which * EC * P:(which + 1) * EC * P].rearrange("p (k m) -> p k m", k=EC)

        def column(u, i):
            return PK[:, u, 3 * EC * P + i:3 * EC * P + i + 1]

        def row(u, i):
            at = 3 * EC * P + 3 + i * P
            return PK[0:1, u, at:at + P]

        @block.sync
        def _(sp):
            start_ahead(sp, sems)
            sp.dma_start(ID[:, :], ident_in).then_inc(consts_in, 16)
            sp.dma_start(VEC[:, :, :, :], vec2).then_inc(consts_in, 16)
            with sp.Fori(0, NPAIR) as b:
                sp.wait_ge(out_free, b + AHEAD)
                for i in range(2):
                    sp.dma_start(X[:, :, i * L:(i + 1) * L], x2T[b * 2 + i]).then_inc(x_in, 16)
                sp.wait_ge(x_used, b + AHEAD)
                for i in range(2):
                    sp.dma_start(CT[:, :, i * L:(i + 1) * L], ctxT[b * 2 + i].rearrange("(k p) c -> p k c", p=P)).then_inc(ct_in, 16)
                with sp.Fori(0, 2) as a:
                    with sp.Fori(0, H2 // 2) as h:
                        for u in range(2):
                            n = (b * 2 + a) * (H2 // 2) + h
                            sp.wait_ge(pack_used, n * 2 + u + AHEAD)
                            sp.dma_start(PK[:, u, :], packs[a * H2 + h * 2 + u]).then_inc(pack_in[u], 16)

        @block.gpsimd
        def _(pool):
            pool.memset(MEANW[:, :], 1.0 / E)
            pool.memset(ONES[:, :], 1.0)
            pool.memset(EPS[:, :], LN_EPS).then_inc(memset_done, 1)
            with pool.Fori(0, NPAIR) as b:
                def down(n, layer):
                    for d in range(EC):
                        pool.wait_ge(down_ps, n * EC + max(d - 1, 0) + AHEAD)
                        pool.sem_inc(passed, 1)
                        pool.dma_start(WD[:, d % 2], downs[layer * EC + d]).then_inc(down_in[d % 2], 16)

                with pool.Fori(0, 2) as a:
                    down(b * 3 + a, a)
                with pool.Fori(0, FC2 // 2) as f:
                    for u in range(2):
                        pool.wait_ge(fc_used, b * FC2 + f * 2 + u + AHEAD)
                        pool.sem_inc(passed, 1)
                        pool.dma_start(W1[:, u, :], fc1[f * 2 + u]).then_inc(fc_in[u], 16)
                down(b * 3 + 2, 2)
                pool.wait_ge(x_ready, (b * 3 + 3) * EC + AHEAD)
                pool.sem_inc(passed, 1)
                for i in range(2):
                    pool.dma_start(x3T[b * 2 + i], X[:, :, i * L:(i + 1) * L]).then_inc(out_stored, 16)
                pool.wait_ge(out_stored, (b + 1) * 32)
                pool.sem_inc(out_free, 1)
        @block.tensor
        def _(pe):
            pe.wait_ge(consts_in, 32 + AHEAD)
            pe.wait_ge(memset_done, 1 + AHEAD)
            def norm(n):
                pe.wait_ge(ln_in, n + 1 + AHEAD)
                for k in range(EC):
                    mm = pe.matmul(ps[:, BQ, :], MEANW[:, :], X[:, k, :], start=(k == 0), stop=(k == EC - 1))
                mm.then_inc(mean_ps, 1)
                pe.wait_ge(sq_ready, n + 1 + AHEAD)
                for k in range(EC):
                    mm = pe.matmul(ps[:, BK, :], MEANW[:, :], SQ[:, k, :], start=(k == 0), stop=(k == EC - 1))
                mm.then_inc(var_ps, 1)

            def down(n):
                for d in range(EC):
                    pe.wait_ge(down_in[d % 2], (n * 2 + d // 2 + 1) * 16)
                    pe.wait_ge(x_ready, n * EC + max(d - 1, 0) + AHEAD)
                    for h in range(H2):
                        mm = pe.matmul(ps[:, BV + d % 2, :], WD[:, d % 2, h, :], G[:, h, :], start=(h == 0), stop=(h == H2 - 1))
                    mm.then_inc(down_ps, 1)

            with pe.Fori(0, NPAIR) as b:
                with pe.Fori(0, 2) as a:
                    norm(b * 3 + a)
                    pe.wait_ge(ct_in, (b + 1) * 32 + AHEAD)
                    pe.sem_inc(passed, 1)
                    pe.wait_ge(h_ready, b * 3 + a + 1 + AHEAD)
                    pe.sem_inc(passed, 1)
                    with pe.Fori(0, H2 // 2) as h:
                        for u in range(2):
                            n = ((b * 2 + a) * (H2 // 2) + h) * 2 + u
                            pe.wait_ge(pack_in[u], ((b * 2 + a) * (H2 // 2) + h + 1) * 16 + AHEAD)
                            pe.wait_ge(q_ready, n + AHEAD)
                            for k in range(EC):
                                mm = pe.matmul(ps[:, BQ, :], weights(u, 0)[:, k, :], H[:, k, :], start=(k == 0), stop=(k == EC - 1))
                            mm.then_inc(q_ps, 1)
                            pe.wait_ge(k_ready, n + AHEAD)
                            for k in range(EC):
                                mm = pe.matmul(ps[:, BK, :], weights(u, 1)[:, k, :], CT[:, k, :], start=(k == 0), stop=(k == EC - 1))
                            mm.then_inc(k_ps, 1)
                            pe.wait_ge(v_ready, n + AHEAD)
                            for t in range(4):
                                for k in range(EC):
                                    pe.matmul(ps[:, BV, t * P:(t + 1) * P], CT[:, k, t * P:(t + 1) * P], weights(u, 2)[:, k, :],
                                              start=(k == 0), stop=False, skip_group_check=True)
                                mm = pe.matmul(ps[:, BV, t * P:(t + 1) * P], ONES[:, :], row(u, 0), start=False, stop=True, skip_group_check=True)
                            mm.then_inc(v_ps, 1)
                            pe.wait_ge(q_ready, n + 1 + AHEAD)
                            pe.wait_ge(k_ready, n + 1 + AHEAD)
                            for i in range(4):
                                pe.wait_ge(exp_ready, n * 4 + max(i - 1, 0) + AHEAD)
                                pe.matmul(ps[:, BS + i % 2, 0:L + 1], QT[:, u, i * P:(i + 1) * P], KT[:, u, i // 2, :], start=True, stop=True)\
                                  .then_inc(s_ps, 1)
                            pe.wait_ge(v_ready, n + 1 + AHEAD)
                            for i in range(2):
                                pe.wait_ge(p_ready, n * 4 + 2 * i + 2 + AHEAD)
                                pe.wait_ge(t_ready, n * 2 + i + AHEAD)
                                for t in range(2):
                                    for q in range(2):
                                        mm = pe.transpose(ps[:, BT, t * L + q * P:t * L + (q + 1) * P], PR[:, 2 * i + q, t * P:(t + 1) * P], ID[:, :])
                                mm.then_inc(t_ps, 1)
                                if i == 0:
                                    pe.wait_ge(tb_ready, n + AHEAD)
                                for q in range(2):
                                    mm = pe.transpose(ps[0:1, BT + 1, i * L + q * P:i * L + (q + 1) * P], PR[:, 2 * i + q, L:L + 1], ID[:, :])
                            mm.then_inc(tb_ps, 1)
                            pe.wait_ge(c_ready, n + AHEAD)
                            pe.wait_ge(tb_ready, n + 1 + AHEAD)
                            for i in range(2):
                                pe.wait_ge(t_ready, n * 2 + i + 1 + AHEAD)
                                for t in range(2):
                                    pe.matmul(ps[:, BC, i * L:(i + 1) * L], V[:, u, 2 * i + t, :], PT[:, i, t, :], start=(t == 0), stop=False, skip_group_check=True)
                                mm = pe.matmul(ps[:, BC, i * L:(i + 1) * L], row(u, 1), PTB[:, i * L:(i + 1) * L], start=False, stop=True, skip_group_check=True)
                            mm.then_inc(c_ps, 1)
                    pe.wait_ge(c_ready, (b * 2 + a + 1) * H2 + AHEAD)
                    down(b * 3 + a)
                norm(b * 3 + 2)
                pe.wait_ge(h_ready, b * 3 + 3 + AHEAD)
                pe.sem_inc(passed, 1)
                with pe.Fori(0, FC2 // 2) as f:
                    for u in range(2):
                        n = b * FC2 + f * 2 + u
                        pe.wait_ge(fc_in[u], (b * (FC2 // 2) + f + 1) * 16)
                        pe.wait_ge(fc_used, n + AHEAD)
                        for k in range(EC):
                            mm = pe.matmul(ps[:, BT + u, :], W1[:, u, k * P:(k + 1) * P], H[:, k, :], start=(k == 0), stop=(k == EC - 1))
                        mm.then_inc(fc_ps, 1)
                pe.wait_ge(fc_ready, (b + 1) * FC2 + AHEAD)
                down(b * 3 + 2)

        @block.scalar
        def _(act):
            act.sem_inc(fc_used, 1)
            act.wait_ge(memset_done, 1 + AHEAD)
            def norm(n):
                act.wait_ge(xc_ready, n + 1 + AHEAD)
                act.activation(SQ[:, :, :], H[:, :, :], ACT.Square).then_inc(sq_ready, 1)
                act.wait_ge(var_ps, n + 1 + AHEAD)
                act.activation(SD[:, :], ps[:, BK, :], ACT.Sqrt, bias=EPS[:, 0:1]).then_inc(sd_ready, 1)

            with act.Fori(0, NPAIR) as b:
                with act.Fori(0, 2) as a:
                    norm(b * 3 + a)
                    with act.Fori(0, H2 // 2) as h:
                        for u in range(2):
                            n = ((b * 2 + a) * (H2 // 2) + h) * 2 + u
                            act.wait_ge(pack_in[u], ((b * 2 + a) * (H2 // 2) + h + 1) * 16 + AHEAD)
                            act.wait_ge(k_ps, n + 1 + AHEAD)
                            act.activation(KT[:, u, :, 0:L], ps[:, BK, :].rearrange("p (i t) -> p i t", i=2), ACT.Identity, bias=column(u, 1))
                            act.activation(KT[:, u, :, L:], column(u, 2).unsqueeze(1).broadcast_to([P, 2, 1]), ACT.Copy)\
                               .then_inc(k_ready, 1)
                            act.wait_ge(v_ps, n + 1 + AHEAD)
                            act.activation(V[:, u, :, :], ps[:, BV, :].rearrange("p (t m) -> p t m", t=4), ACT.Copy).then_inc(v_ready, 1)
                            for i in range(4):
                                act.wait_ge(max_ready, n * 4 + i + 1 + AHEAD)
                                act.wait_ge(tb_ps, n + AHEAD)
                                act.activation(PR[:, i, :], ps[:, BS + i % 2, 0:L + 1], ACT.Exp, bias=NM[:, i:i + 1], accum_out=RS[:, i:i + 1])\
                                   .then_inc(exp_ready, 1)
                            act.wait_ge(c_ps, n + 1 + AHEAD)
                            act.sem_inc(passed, 1)
                            act.activation(G[:, h * 2 + u, :], ps[:, BC, :], ACT.Copy).then_inc(c_ready, 1)
                norm(b * 3 + 2)
                with act.Fori(0, FC2 // 2) as f:
                    for u in range(2):
                        n = b * FC2 + f * 2 + u
                        act.wait_ge(fc_in[u], (b * (FC2 // 2) + f + 1) * 16)
                        act.wait_ge(fc_ps, n + 1 + AHEAD)
                        act.sem_inc(passed, 1)
                        act.activation(G[:, f * 2 + u, :], ps[:, BT + u, :], ACT.Gelu, bias=W1[:, u, EC * P:]).then_inc(fc_ready, 1)
                        act.drain().then_inc(fc_used, 1)

        @block.vector
        def _(dve):
            dve.sem_inc(pack_used, 1)
            dve.wait_ge(consts_in, 32 + AHEAD)
            def norm(n, v):
                dve.wait_ge(mean_ps, n + 1 + AHEAD)
                dve.tensor_tensor(H[:, :, :], X[:, :, :], ps[:, BQ:BQ + 1, :].broadcast_to([P, EC, N2]), ALU.subtract).then_inc(xc_ready, 1)
                dve.wait_ge(sd_ready, n + 1 + AHEAD)
                dve.reciprocal(SD[:, :], SD[:, :])
                dve.drain()
                dve.tensor_tensor(H[:, :, :], H[:, :, :], SD[:, :].unsqueeze(1).broadcast_to([P, EC, N2]), ALU.mult)
                dve.drain()
                for o in range(EC):
                    mm = dve.tensor_scalar(H[:, o, :], H[:, o, :], VEC[:, v, V2_NW, o:o + 1], VEC[:, v, V2_NB, o:o + 1], ALU.mult, ALU.add)
                dve.drain().then_inc(h_ready, 1)

            def down(n, v):
                for d in range(EC):
                    dve.wait_ge(down_ps, n * EC + d + 1 + AHEAD)
                    dve.scalar_tensor_tensor(X[:, d, :], ps[:, BV + d % 2, :], VEC[:, v, V2_BO, d:d + 1], X[:, d, :], ALU.add, ALU.add)\
                       .then_inc(x_ready, 1)

            with dve.Fori(0, NPAIR) as b:
                dve.wait_ge(x_in, (b + 1) * 32 + AHEAD)
                dve.sem_inc(ln_in, 1)
                with dve.Fori(0, 2) as a:
                    norm(b * 3 + a, a)
                    with dve.Fori(0, H2 // 2) as h:
                        for u in range(2):
                            n = ((b * 2 + a) * (H2 // 2) + h) * 2 + u
                            dve.wait_ge(q_ps, n + 1 + AHEAD)
                            dve.tensor_scalar(QT[:, u, :], ps[:, BQ, :], column(u, 0), float(K2) ** -0.5, ALU.add, ALU.mult).then_inc(q_ready, 1)
                            for i in range(4):
                                dve.wait_ge(s_ps, n * 4 + i + 1 + AHEAD)
                                dve.tensor_reduce(NM[:, i:i + 1], ps[:, BS + i % 2, 0:L + 1], AX.X, ALU.max, negate=True).then_inc(max_ready, 1)
                            for i in range(4):
                                dve.wait_ge(exp_ready, n * 4 + i + 1 + AHEAD)
                                dve.reciprocal(RS[:, i:i + 1], RS[:, i:i + 1])
                                dve.drain()
                                dve.tensor_scalar(PR[:, i, :], PR[:, i, :], RS[:, i:i + 1], None, ALU.mult).then_inc(p_ready, 1)
                            for i in range(2):
                                dve.wait_ge(t_ps, n * 2 + i + 1 + AHEAD)
                                dve.wait_ge(c_ps, n + AHEAD)
                                dve.tensor_copy(PT[:, i, :, :], ps[:, BT, :].rearrange("p (t q) -> p t q", t=2)).then_inc(t_ready, 1)
                            dve.wait_ge(tb_ps, n + 1 + AHEAD)
                            dve.tensor_copy(PTB[:, :], ps[0:1, BT + 1, :]).then_inc(tb_ready, 1)
                            dve.wait_ge(c_ps, n + 1 + AHEAD)
                            dve.sem_inc(pack_used, 1)
                    down(b * 3 + a, a)
                    dve.drain().then_inc(ln_in, 1)
                norm(b * 3 + 2, 2)
                down(b * 3 + 2, 2)
                dve.drain().then_inc(x_used, 1)

CI = 128
(V3_TB, V3_WB, V3_GAMMA, V3_BETA, V3_MEAN, V3_VAR) = (0, 1, 3, 5, 7, 9)
NV3 = 11


def layer3(nc, x3T, ctx, theta_w, pg_w, pg_b, w_w, vec3, ident_in, out):
    with ExitStack() as stack:
        def sb(name, shape, dt=F32):
            return stack.enter_context(nc.sbuf_tensor("d_" + name, shape, dt))

        sems = []

        def sem(name):
            sems.append(stack.enter_context(nc.semaphore("d_" + name)))
            return sems[-1]

        WT = sb("wt", [P, LC, CI])
        WPG = sb("wpg", [P, LC, 2 * CI])
        BPG = sb("bpg", [1, 2 * CI])
        WW = sb("ww", [P, L])
        VEC = sb("vec", [P, NV3])
        ID = sb("id", [P, P])
        ONES = sb("ones", [1, P])
        EPS = sb("eps", [P, 1])
        BN = sb("bn", [P, 2, 2])
        XT = sb("xt", [P, EC, L])
        C = sb("c", [P, LC, E])
        X = sb("x", [P, LC, E])
        PG = sb("pg", [P, EC, 2 * CI])
        M = sb("m", [P, CI])
        TH = sb("th", [P, E])
        Y = sb("y", [P, E])
        O = sb("o", [P, LC, E])
        ps = stack.enter_context(nc.psum_tensor("d_ps", [P, 8, 512], F32))
        names = "consts_in memset_done bn_sqrt bn_in x_in in_used x_ps x_ready pg_ps pg_ready m_ps m_ready th_ps th_ready y_ps y_ready o_ps o_read out_ready out_stored".split()
        (consts_in, memset_done, bn_sqrt, bn_in, x_in, in_used, x_ps, x_ready, pg_ps, pg_ready, m_ps, m_ready, th_ps, th_ready,
         y_ps, y_ready, o_ps, o_read, out_ready, out_stored) = [sem(n) for n in names]
        block = stack.enter_context(nc.Block())

        @block.sync
        def _(sp):
            start_ahead(sp, sems)
            for dst, src in ((WT[:, :, :], theta_w), (WPG[:, :, :], pg_w), (BPG[:, :], pg_b), (WW[:, :], w_w), (VEC[:, :], vec3), (ID[:, :], ident_in)):
                sp.dma_start(dst, src).then_inc(consts_in, 16)
            with sp.Fori(0, B) as b:
                sp.wait_ge(in_used, b + AHEAD)
                sp.dma_start(XT[:, :, :], x3T[b]).then_inc(x_in, 16)
                sp.dma_start(C[:, :, :], ctx[b].rearrange("(k p) t -> p k t", p=P)).then_inc(x_in, 16)
                sp.wait_ge(out_ready, b + 1 + AHEAD)
                sp.dma_start(out[b].rearrange("(k p) t -> p k t", p=P), O[:, :, :]).then_inc(out_stored, 16)
            sp.wait_ge(out_stored, 16 * B + AHEAD)
        @block.gpsimd
        def _(pool):
            pool.memset(ONES[:, :], 1.0)
            pool.memset(EPS[:, :], LN_EPS).then_inc(memset_done, 1)

        @block.tensor
        def _(pe):
            pe.wait_ge(consts_in, 96 + AHEAD)
            pe.wait_ge(memset_done, 1 + AHEAD)
            with pe.Fori(0, B) as b:
                pe.wait_ge(x_in, (b + 1) * 32 + AHEAD)
                pe.wait_ge(o_read, b + AHEAD)
                for c in range(LC):
                    for k in range(EC):
                        mm = pe.transpose(ps[:, c, k * P:(k + 1) * P], XT[:, k, c * P:(c + 1) * P], ID[:, :])
                mm.then_inc(x_ps, 1)
                for m in range(EC):
                    for k in range(LC):
                        pe.matmul(ps[:, 2 + m // 2, (m % 2) * L:(m % 2 + 1) * L], C[:, k, m * P:(m + 1) * P], WPG[:, k, :],
                                  start=(k == 0), stop=False, skip_group_check=True)
                    mm = pe.matmul(ps[:, 2 + m // 2, (m % 2) * L:(m % 2 + 1) * L], ONES[:, :], BPG[:, :], start=False, stop=True,
                                   skip_group_check=True)
                mm.then_inc(pg_ps, 1)
                pe.wait_ge(x_ready, b + 1 + AHEAD)
                for k in range(LC):
                    mm = pe.matmul(ps[:, 5, :], WT[:, k, :], X[:, k, :], start=(k == 0), stop=(k == LC - 1))
                mm.then_inc(th_ps, 1)
                pe.wait_ge(pg_ready, b + 1 + AHEAD)
                for m in range(EC):
                    mm = pe.matmul(ps[:, 4, 0:CI], PG[:, m, 0:CI], PG[:, m, CI:], start=(m == 0), stop=(m == EC - 1))
                mm.then_inc(m_ps, 1)
                pe.wait_ge(m_ready, b + 1 + AHEAD)
                pe.wait_ge(th_ready, b + 1 + AHEAD)
                pe.matmul(ps[:, 6, :], M[:, :], TH[:, :], start=True, stop=True).then_inc(y_ps, 1)
                pe.wait_ge(y_ready, b + 1 + AHEAD)
                for c in range(LC):
                    mm = pe.matmul(ps[:, 2 + c, :], WW[:, c * P:(c + 1) * P], Y[:, :], start=True, stop=True)
                mm.then_inc(o_ps, 1)

        @block.scalar
        def _(act):
            act.wait_ge(memset_done, 1 + AHEAD)
            act.wait_ge(consts_in, 96 + AHEAD)
            act.activation(BN[:, 0, :], VEC[:, V3_VAR:V3_VAR + 2], ACT.Sqrt, bias=EPS[:, 0:1]).then_inc(bn_sqrt, 1)
            with act.Fori(0, B) as b:
                act.wait_ge(pg_ps, b + 1 + AHEAD)
                act.activation(PG[:, :, :], ps[:, 2:4, :].rearrange("p a (c t) -> p (a c) t", c=2), ACT.Copy).then_inc(pg_ready, 1)
                act.wait_ge(th_ps, b + 1 + AHEAD)
                act.activation(TH[:, :], ps[:, 5, :], ACT.Identity, bias=VEC[:, V3_TB:V3_TB + 1]).then_inc(th_ready, 1)
                act.wait_ge(y_ps, b + 1 + AHEAD)
                act.activation(Y[:, :], ps[:, 6, :], ACT.Copy).then_inc(y_ready, 1)

        @block.vector
        def _(dve):
            dve.wait_ge(bn_sqrt, 1 + AHEAD)
            dve.reciprocal(BN[:, 0, :], BN[:, 0, :])
            dve.tensor_tensor(BN[:, 1, :], VEC[:, V3_WB:V3_WB + 2], VEC[:, V3_MEAN:V3_MEAN + 2], ALU.subtract)
            dve.drain()
            dve.tensor_tensor(BN[:, 0, :], BN[:, 0, :], VEC[:, V3_GAMMA:V3_GAMMA + 2], ALU.mult)
            dve.drain()
            dve.tensor_tensor(BN[:, 1, :], BN[:, 1, :], BN[:, 0, :], ALU.mult)
            dve.drain()
            dve.tensor_tensor(BN[:, 1, :], BN[:, 1, :], VEC[:, V3_BETA:V3_BETA + 2], ALU.add)
            with dve.Fori(0, B) as b:
                dve.wait_ge(x_ps, b + 1 + AHEAD)
                dve.tensor_copy(X[:, :, :], ps[:, 0:2, :]).then_inc(x_ready, 1)
                dve.wait_ge(m_ps, b + 1 + AHEAD)
                dve.tensor_scalar(M[:, :], ps[:, 4, 0:CI], 1.0 / E, None, ALU.mult).then_inc(m_ready, 1)
                dve.wait_ge(o_ps, b + 1 + AHEAD)
                dve.wait_ge(out_stored, b * 16 + AHEAD)
                for c in range(LC):
                    dve.tensor_scalar(O[:, c, :], ps[:, 2 + c, :], BN[:, 0, c:c + 1], BN[:, 1, c:c + 1], ALU.mult, ALU.add)
                dve.drain().then_inc(o_read, 1)
                dve.tensor_tensor(O[:, :, :], O[:, :, :], X[:, :, :], ALU.add).then_inc(out_ready, 1)
                dve.drain().then_inc(in_used, 1)


def _l0(I):
    import numpy as np
    f=np.ascontiguousarray
    def pad(W):
        z=np.zeros((4,4,32,256),np.float32); z[:,:,:16,:]=W.reshape(4,4,16,256)
        return z.reshape(4,128,2,128).transpose(0,3,2,1)
    def padb(b):
        z=np.zeros((4,4,32),np.float32); z[:,:,:16]=b.reshape(4,4,16); return z.reshape(4,128)
    wqk=f(np.stack([pad(I['L0_xattn_Wq']),pad(I['L0_xattn_Wk'])],axis=3))
    qkb=f(np.stack([padb(I['L0_xattn_bq']),padb(I['L0_xattn_bk'])],axis=2))
    aug=np.zeros((4,32,2),np.float32); aug[:,16,0]=4.0; aug[:,17,1]=1.0
    ms=np.zeros((4,32),np.float32); ms[:,16]=1.0
    wv=f(I['L0_xattn_Wv'].reshape(4,64,2,128).transpose(0,3,2,1))
    m=I['mask_Bx1x2048_bf1'].view(np.uint8)
    return dict(x=I['x'],xT=f(I['x'].transpose(0,2,1)),ctx=I['ctx_2048'],mask_row=f(m),mask_col=f(m.reshape(8,4,128).transpose(0,2,1)),
      wqk=wqk,qkb=qkb,aug=aug.reshape(128,2),wv=wv,bv=f(I['L0_xattn_bv'].reshape(4,1,64)),mask_sel=ms.reshape(1,128),ident_in=np.eye(128,dtype=np.float32))


def _l1(I):
    import numpy as np
    f=np.ascontiguousarray
    c=I['ctx_2048']
    s0=f(c[:,2:18].reshape(8,4,128,16).transpose(0,2,1,3))
    n=lambda k:I['L1_xattn_'+k].reshape(-1,512)
    v=np.concatenate([n('ln1_w'),n('ln1_b'),n('ln2_w'),n('ln2_b'),n('maa_x'),n('maa_stack'),n('time_decay'),n('u'),n('gn_w'),n('gn_b'),n('ffn_maa_k'),n('ffn_maa_r')])
    vecs=f(v.reshape(16,4,128).transpose(2,0,1))
    w8=f(np.stack([I['L1_xattn_'+k].T.reshape(4,128,512).transpose(1,0,2) for k in ('Wk','Wv','Wr','Wg','Wo','Wfk','Wfr','Wfv')],axis=1))
    sel=np.zeros((8,16,16,8,16),np.float32)
    for h in range(8):
        for j in range(16): sel[h,j,j,h,:]=1
    sel=sel.reshape(128,16,128)
    blk=np.kron(np.eye(8,dtype=np.float32),np.ones((16,16),np.float32))
    return dict(ctxT=f(c.transpose(0,2,1)),s0=s0,vecs=vecs,w8=w8,maa_w1=f(I['L1_xattn_maa_w1'].reshape(4,128,160).transpose(1,0,2)),
      maa_w2=I['L1_xattn_maa_w2'].reshape(160,512),td_w1=f(I['L1_xattn_td_w1'].reshape(4,128,64).transpose(1,0,2)),td_w2=I['L1_xattn_td_w2'],
      sel=sel,selT=f(sel.transpose(2,1,0)),blk=f(np.stack([blk,blk/16])))


def _l2(I):
    import numpy as np
    f=np.ascontiguousarray; g=lambda k:I['L2_xattn_'+k]
    def hd(W): return W.reshape(4,128,16,128).transpose(2,1,0,3).reshape(16,128,512)
    packs=[];downs=[]
    for i in '12':
        z=np.zeros((16,128,3+256),np.float32)
        z[:,:,0]=g('bq'+i).reshape(16,128); z[:,:,1]=g('bk'+i).reshape(16,128); z[:,:,2]=g('bias_k'+i).reshape(16,128)
        z[:,0,3:131]=g('bv'+i).reshape(16,128); z[:,0,131:]=g('bias_v'+i).reshape(16,128)
        packs.append(np.concatenate([hd(g('wq'+i)),hd(g('wk'+i)),hd(g('wv'+i)),z],axis=2))
    for W in (g('wo1'),g('wo2'),g('w_fc2')):
        downs.append(W.reshape(16,128,4,128).transpose(2,1,0,3))
    fc1=np.concatenate([hd(g('w_fc1')),g('b_fc1').reshape(16,128,1)],axis=2)
    v=np.stack([np.stack([g('ln1_scale'),g('ln1_offset'),g('bo1')]),np.stack([g('ln2_scale'),g('ln2_offset'),g('bo2')]),np.stack([g('ln_mlp_scale'),g('ln_mlp_offset'),g('b_fc2')])])
    return dict(packs=f(np.concatenate(packs)),downs=f(np.concatenate(downs)),fc1=f(fc1),vec2=f(v.reshape(3,3,4,128).transpose(3,0,1,2)),ident_in=np.eye(128,dtype=np.float32))


def _l3(I):
    import numpy as np
    f=np.ascontiguousarray; g=lambda k:I['L3_xattn_'+k]
    def ci(W): return W.reshape(128,2,128).transpose(2,1,0)
    v=np.concatenate([g('theta_b').reshape(1,128)]+[g(k).reshape(2,128) for k in ('w_b','bn_gamma','bn_beta','bn_mean','bn_var')]).T
    return dict(theta_w=f(ci(g('theta_w'))),pg_w=f(np.concatenate([ci(g('phi_w')),ci(g('g_w'))],axis=2)),pg_b=np.concatenate([g('phi_b'),g('g_b')]).reshape(1,256),w_w=f(g('w_w').T),vec3=f(v),ident_in=np.eye(128,dtype=np.float32),ctx=I['ctx_2048'])


def build(nc, io, out):
    def scratch(name):
        return nc.dram_tensor(name, [B, P, EC, L], F32).ap()

    x1T, x2T, x3T = scratch("x1T"), scratch("x2T"), scratch("x3T")
    layer0(nc, x=io["x"], xT=io["xT"], ctx=io["ctx"], mask_row=io["mask_row"], mask_col=io["mask_col"], wqk=io["wqk"], qkb=io["qkb"],
           aug=io["aug"], wv=io["wv"], bv=io["bv"], mask_sel=io["mask_sel"], ident_in=io["ident_in"], x1T=x1T)
    layer1(nc, x1T=x1T, ctxT=io["ctxT"], s0=io["s0"], vecs=io["vecs"], w8=io["w8"], maa_w1=io["maa_w1"], maa_w2=io["maa_w2"],
           td_w1=io["td_w1"], td_w2=io["td_w2"], sel=io["sel"], selT=io["selT"], blk=io["blk"], x2T=x2T)
    layer2(nc, x2T=x2T, ctxT=io["ctxT"], packs=io["packs"], downs=io["downs"], fc1=io["fc1"], vec2=io["vec2"],
           ident_in=io["ident_in"], x3T=x3T)
    layer3(nc, x3T=x3T, ctx=io["ctx"], theta_w=io["theta_w"], pg_w=io["pg_w"], pg_b=io["pg_b"], w_w=io["w_w"], vec3=io["vec3"],
           ident_in=io["ident_in"], out=out)


def kernel(**inputs):
    import numpy as np
    import concourse.bacc as bacc
    from concourse.bass_utils import run_bass_kernel_spmd

    I = {k: np.asarray(v) for k, v in inputs.items()}
    arrays = {}
    for part in (_l0(I), _l1(I), _l2(I), _l3(I)):
        arrays.update(part)
    arrays = {k: np.ascontiguousarray(v) for k, v in arrays.items()}
    nc = bacc.Bacc("TRN2", target_bir_lowering=False, num_devices=1)
    io = {k: nc.dram_tensor("in_" + k, a.shape, mybir.dt.from_np(a.dtype), kind="ExternalInput").ap() for k, a in arrays.items()}
    out = nc.dram_tensor("out", (B, L, E), F32, kind="ExternalOutput").ap()
    build(nc, io, out)
    r = run_bass_kernel_spmd(nc, [{"in_" + k: a for k, a in arrays.items()}], core_ids=[0])
    return r.results[0]["out"]
```

```python
from contextlib import ExitStack

import concourse.bass as bass
from concourse import mybir

B, L, E = 8, 256, 512
P = 128
EC = E // P
LC = L // P
LN_EPS = 1e-5

H0, D0 = 16, L // 16
G0 = 4
HG = H0 // G0
CG = HG * D0
ROW_MASK, ROW_MAX = D0, D0 + 1
V2C = 2 * D0
VW = 3 * V2C + 1
MAX_FROM, MAX_RATE = 3, 2
NEG = -1e30

F32 = mybir.dt.float32
U8 = mybir.dt.uint8
F32R = mybir.dt.float32r
F16 = mybir.dt.float16
BF16 = mybir.dt.bfloat16
ALU = mybir.AluOpType
ACT = mybir.ActivationFunctionType
AX = mybir.AxisListType


AHEAD = 128


def start_ahead(eng, semaphores):
    for semaphore in semaphores:
        eng.sem_inc(semaphore, AHEAD)


def layer0(nc, x, xT, ctx, mask_row, mask_col, wqk, qkb, aug, wv, bv, mask_sel, ident_in, x1T):
    with ExitStack() as stack:
        def sb(name, shape, dt=F32):
            return stack.enter_context(nc.sbuf_tensor("a_" + name, shape, dt))

        sems = []

        def sem(name):
            sems.append(nc.alloc_semaphore("a_" + name))
            return sems[-1]

        def dma_sem(name):
            return stack.enter_context(nc.semaphore("a_" + name))

        WH = sb("wh", [P, G0, LC, 2, P], F32R)
        WL = sb("wl", [P, G0, LC, 2, P], F32R)
        WVH = sb("wvh", [P, LC, L], F32R)
        WVL = sb("wvl", [P, LC, L], F32R)
        QKB = sb("qkb", [P, 2, G0])
        AUG = sb("aug", [P, 2, G0])
        BVB = sb("bvb", [P, L])
        MSEL = sb("msel", [P, P])
        MSELR = sb("mselr", [P, P], F32R)
        M8R = sb("m8r", [P, E], U8)
        MBRR = sb("mbrr", [P, E], F32R)
        M8C = sb("m8c", [P, EC], U8)
        MCOL = sb("mcol", [P, EC])
        X = sb("x", [P, LC, E])
        C = sb("ctx", [P, LC, E])
        XH = sb("xh", [P, LC, E], F32R)
        XL = sb("xl", [P, LC, E], F32R)
        CH = sb("ch", [P, LC, E], F32R)
        CL = sb("cl", [P, LC, E], F32R)
        XT = sb("xT", [P, EC, L])
        XM = sb("xm", [P, EC, L])
        XQ = sb("xq", [P, EC, L])
        ID = sb("id", [P, P])
        ONES = sb("ones", [P, P])
        EPS = sb("eps", [P, 1])
        QF = sb("qf", [P, E])
        KF = sb("kf", [P, E])
        QH = sb("qh", [P, 2, E], F32R)
        QL = sb("ql", [P, 2, E], F32R)
        KK = sb("kk", [P, 2, 2, E], F32R)
        QM = sb("qm", [P, HG, E], F32R)
        KM = sb("km", [P, 2, HG, 2, E], F32R)
        NM = sb("nm", [P, 2, HG * EC])
        NMT = sb("nmT", [HG * EC, 2, P], F32R)
        VF = sb("vf", [P, EC, H0, V2C])
        VA = sb("va", [P, EC, H0, VW], BF16)
        EX = sb("ex", [P, 4, E])
        EH = sb("eh", [P, 2, EC, E], F16)
        EL = sb("el", [P, 2, EC, E], F16)
        U = sb("u", [P, 2, EC, HG, V2C])
        DEN = sb("den", [P, 2, EC, HG, 1])
        MEAN = sb("mean", [P, EC, L])
        VAR = sb("var", [P, EC, L])
        MSQ = sb("msq", [P, EC, HG, D0])
        ST = sb("st", [P, 4, L])
        RN = sb("rn", [P, 1])
        OUT = XQ
        WQK = EX[:, :, :].rearrange("p a (b c d) -> p a b c d", b=LC, c=2)
        WV = XQ[:, 0:LC, :]
        ps = stack.enter_context(nc.psum_tensor("a_ps", [P, 8, 512], F32))
        BQ, BK, BM, BT, BO = 0, 1, 2, 4, 6

        consts_in, inputs_in, stats_x_in, memset_done, inputs_read, stats_read = [sem(n) for n in ("consts_in", "inputs_in", "stats_x_in", "memset_done", "inputs_read", "stats_read")]
        xc_high, xc_split, weights_split, stats_in = sem("xc_high"), sem("xc_split"), sem("weights_split"), sem("stats_in")
        q_ps, k_ps, qf_ready, kf_ready, qh_ready, kh_ready, qk_split = [sem(n) for n in ("q_ps", "k_ps", "qf_ready", "kf_ready", "qh_ready", "kh_ready", "qk_split")]
        v_ps, vf_ready, v_square, v_split, st_ps, st_read, sq_ready = [sem(n) for n in ("v_ps", "vf_ready", "v_square", "v_split", "st_ps", "st_read", "sq_ready")]
        qm_in, km_in_even, km_in_odd, m_ps, m_read, nm_ready, nmT_ps, nmT_sb, max_in = [sem(n) for n in ("qm_in", "km_in", "km_in_odd", "m_ps", "m_read", "nm_ready", "nmT_ps", "nmT_sb", "max_in")]
        t_ps, ex_ready, eh_ready, el_dve, el_pool, o_ps, o_read = [sem(n) for n in ("t_ps", "ex_ready", "eh_ready", "el_dve", "el_pool", "o_ps", "o_read")]
        den_ready, u_read, var_x, var_v, std_ready, rstd_ready = [sem(n) for n in ("den_ready", "u_read", "var_x", "var_v", "std_ready", "rstd_ready")]
        out_free, out_stored, passed, out_ready = sem("out_free"), dma_sem("out_stored"), sem("passed"), sem("out_ready")
        km_in = (km_in_even, km_in_odd)
        N_IN, N_STATS, N_HEADS = 3 * 16, 2 * 16, HG * 16
        NS = HG * EC
        NE = NS // 2
        stack.callback(nc.all_engine_barrier)
        stack.callback(lambda: nc.clear_and_free_semaphores(sems))
        block = stack.enter_context(nc.Block())

        def tiles_beside(n):
            first = (n - MAX_FROM) * MAX_RATE
            return range(first, first + MAX_RATE) if 0 <= first < NS else range(0)

        TURN_AT = MAX_FROM + NS // MAX_RATE
        STATS_AT, MOMENTS_AT = 3, 7
        PROJECT_AT = TURN_AT + 2

        def after(b, g):
            return (b, g + 1) if g + 1 < G0 else (b + 1, 0)

        @block.sync
        def _(sp):
            start_ahead(sp, sems)

            def load_inputs(b):
                sp.wait_ge(inputs_read, b + AHEAD)
                sp.sem_inc(passed, 1)
                sp.dma_start(X[:, :, :], x[b].rearrange("(k p) t -> p k t", p=P)).then_inc(inputs_in, 16)
                sp.dma_start(C[:, :, :], ctx[b].rearrange("(k p) t -> p k t", p=P)).then_inc(inputs_in, 16)
                sp.dma_start(M8R[:, :], mask_row[b]).then_inc(inputs_in, 16)

            def load_statistics(b):
                sp.wait_ge(stats_read, b + AHEAD)
                sp.sem_inc(passed, 1)
                sp.dma_start(M8C[:, :], mask_col[b]).then_inc(stats_x_in, 16)
                sp.dma_start(XT[:, :, :], xT[b].rearrange("(k p) c -> p k c", p=P)).then_inc(stats_x_in, 16)

            def spread(b, g):
                it, s = b * G0 + g, g % 2
                sp.wait_ge(m_ps, it * NS + AHEAD)
                sp.sem_inc(passed, 1)
                sp.wait_ge(qh_ready, it + 1 + AHEAD)
                for h in range(HG):
                    rows = slice(32 * h, 32 * h + 32)
                    sp.dma_start(QM[rows, h, :].bitcast(F32), QH[rows, s, :].bitcast(F32)).then_inc(qm_in, 16)
                sp.wait_ge(t_ps, (it - 1) * NS + AHEAD)
                sp.sem_inc(passed, 1)
                sp.wait_ge(qk_split, it + 1 + AHEAD)
                for h in range(HG):
                    rows = slice(32 * h, 32 * h + 32)
                    sp.dma_start(KM[rows, s, h, :, :].bitcast(F32), KK[rows, s, :, :].bitcast(F32)).then_inc(km_in[s], 16)
                sp.wait_ge(nmT_sb, it + 1 + AHEAD)
                for h in range(HG):
                    sp.dma_start(QH[32 * h + ROW_MAX:32 * h + ROW_MAX + 1, s, :].bitcast(F32),
                                 NMT[h * EC:(h + 1) * EC, s, :].bitcast(F32)).then_inc(max_in, 16)

            for dst, src in ((WQK, wqk), (WV, wv), (QKB[:, :, :], qkb), (AUG[:, :, :], aug), (BVB[:, :], bv),
                             (MSEL[:, :], mask_sel), (ID[:, :], ident_in)):
                sp.dma_start(dst, src).then_inc(consts_in, 16)
            load_inputs(0)
            sp.wait_ge(memset_done, 1 + AHEAD)
            sp.sem_inc(passed, 1)
            spread(0, 0)
            load_statistics(0)
            spread(0, 1)
            spread(0, 2)
            with sp.Fori(0, B - 1) as b:
                load_inputs(b + 1)
                for g in (2, 3):
                    spread(*after(b, g))
                load_statistics(b + 1)
                for g in (0, 1):
                    spread(*after(b + 1, g))
            spread(B - 1, 3)

        @block.gpsimd
        def _(pool):
            pool.memset(QM[:, :, :].bitcast(F32), 0.0)
            pool.memset(ONES[:, :], 1.0)
            pool.memset(EPS[:, :], LN_EPS)
            pool.memset(VA[:, :, :, 0:1], 1.0)
            pool.memset(KM[:, :, :, :, :].bitcast(F32), 0.0).then_inc(memset_done, 1)

            def group_moments(b, g):
                it, s = b * G0 + g, g % 2
                cols = slice(g * HG * D0, (g + 1) * HG * D0)
                mean = MEAN[:, :, cols].rearrange("p c (h d) -> p c h d", h=HG)
                var = VAR[:, :, cols].rearrange("p c (h d) -> p c h d", h=HG)
                pool.wait_ge(den_ready, it + 1 + AHEAD)
                pool.sem_inc(passed, 1)
                for c in range(EC):
                    pool.tensor_tensor(U[:, s, c, :, :], U[:, s, c, :, :], DEN[:, s, c, :, :].broadcast_to([P, HG, V2C]), ALU.mult)
                pool.drain()
                pool.tensor_copy(mean, U[:, s, :, :, 0:D0])
                pool.tensor_tensor(MSQ[:, :, :, :], U[:, s, :, :, 0:D0], U[:, s, :, :, 0:D0], ALU.mult)
                pool.drain()
                pool.tensor_tensor(var, U[:, s, :, :, D0:], MSQ[:, :, :, :], ALU.subtract).then_inc(u_read, 1)
                pool.drain()
                if g == G0 - 1:
                    pool.tensor_scalar(VAR[:, :, :], VAR[:, :, :], 0.0, None, ALU.max).then_inc(var_v, 1)
                    pool.drain()

            def centre(b):
                pool.wait_ge(var_x, b + 1 + AHEAD)
                pool.sem_inc(passed, 1)
                pool.tensor_tensor(XM[:, :, :], XM[:, :, :], ST[:, 0:1, :].broadcast_to([P, EC, L]), ALU.subtract)
                pool.drain()

            def scale(b):
                pool.wait_ge(rstd_ready, b + 1 + AHEAD)
                pool.sem_inc(passed, 1)
                pool.tensor_tensor(XM[:, :, :], XM[:, :, :], ST[:, 3:4, :].broadcast_to([P, EC, L]), ALU.mult)
                pool.drain()

            def spread_out(b):
                pool.tensor_tensor(XM[:, :, :], XM[:, :, :], VAR[:, :, :], ALU.mult)
                pool.drain()

            def shift(b):
                pool.tensor_tensor(XM[:, :, :], XM[:, :, :], MEAN[:, :, :], ALU.add)
                pool.drain()

            def store(b):
                for c in range(EC):
                    pool.tensor_scalar(OUT[:, c, :], XM[:, c, :], MCOL[:, c:c + 1], None, ALU.mult)
                pool.drain().then_inc(out_ready, 1)
                pool.dma_start(x1T[b], OUT[:, :, :]).then_inc(out_stored, 16)

            def group(b, g, prior):
                it = b * G0 + g
                for h in range(HG):
                    for k in range(1, EC, 2):
                        n = h * EC + k
                        pool.wait_ge(eh_ready, it * NS + n + 1 + AHEAD)
                        pool.sem_inc(passed, 1)
                        pool.tensor_tensor(EL[:, h % 2, k, :], EX[:, n % 4, :], EH[:, h % 2, k, :], ALU.subtract).then_inc(el_pool, 1)
                    if g == 0 and h == 1 and prior is not None:
                        group_moments(prior, G0 - 1)
                    if g == 0 and h == 3 and prior is not None:
                        scale(prior)
                    if g == 1 and h == 0 and prior is not None:
                        spread_out(prior)
                        shift(prior)
                    if g == 1 and h == 1 and prior is not None:
                        store(prior)
                    if g == 1 and h == 1:
                        group_moments(b, 0)
                    if g == 1 and h == 3 and prior is not None:
                        pool.wait_ge(out_stored, (prior + 1) * 16)
                        pool.sem_inc(out_free, 1)
                    if g >= 2 and h == 1:
                        group_moments(b, g - 1)
                    if g == 3 and h == 3:
                        centre(b)

            group(0, 0, None)
            group(0, 1, None)
            with pool.Fori(0, B - 1) as b:
                group(b, 2, None)
                group(b, 3, None)
                group(b + 1, 0, b)
                group(b + 1, 1, b)
            group(B - 1, 2, None)
            group(B - 1, 3, None)
            group_moments(B - 1, G0 - 1)
            scale(B - 1)
            spread_out(B - 1)
            shift(B - 1)
            store(B - 1)
            pool.wait_ge(out_stored, B * 16)

        @block.tensor
        def _(pe):
            pe.wait_ge(memset_done, 1 + AHEAD)
            pe.wait_ge(weights_split, 1 + AHEAD)

            def project_queries(b, g):
                it = b * G0 + g
                if g == 0:
                    pe.wait_ge(xc_split, b + 1 + AHEAD)
                pe.wait_ge(nmT_sb, it + AHEAD)
                for k in range(LC):
                    pe.matmul(ps[:, BQ, :], WH[:, g, k, 0, :], XH[:, k, :], start=(k == 0), stop=False)
                    pe.matmul(ps[:, BQ, :], WH[:, g, k, 0, :], XL[:, k, :], start=False, stop=False)
                    mm = pe.matmul(ps[:, BQ, :], WL[:, g, k, 0, :], XH[:, k, :], start=False, stop=(k == LC - 1))
                mm.then_inc(q_ps, 1)

            def project_keys(b, g):
                pe.wait_ge(kf_ready, b * G0 + g + AHEAD)
                for k in range(LC):
                    pe.matmul(ps[:, BK, :], WH[:, g, k, 1, :], CH[:, k, :], start=(k == 0), stop=False)
                    pe.matmul(ps[:, BK, :], WH[:, g, k, 1, :], CL[:, k, :], start=False, stop=False)
                    pe.matmul(ps[:, BK, :], WL[:, g, k, 1, :], CH[:, k, :], start=False, stop=False)
                pe.matmul(ps[:, BK, :], MSELR[:, :], MBRR[:, :], start=False, stop=True).then_inc(k_ps, 1)

            def values(b):
                pe.wait_ge(eh_ready, b * G0 * NS + AHEAD)
                for c in range(EC):
                    out = ps[:, BT + c // 2, (c % 2) * L:(c % 2 + 1) * L]
                    for k in range(LC):
                        cols = slice(c * P, (c + 1) * P)
                        pe.matmul(out, CH[:, k, cols], WVH[:, k, :], start=(k == 0), stop=False, skip_group_check=True)
                        pe.matmul(out, CH[:, k, cols], WVL[:, k, :], start=False, stop=False, skip_group_check=True)
                        mm = pe.matmul(out, CL[:, k, cols], WVH[:, k, :], start=False, stop=(k == LC - 1), skip_group_check=True)
                mm.then_inc(v_ps, 1)

            def statistics(b, last):
                pe.wait_ge(stats_in, b + 1 + AHEAD)
                pe.wait_ge(sq_ready, b + 1 + AHEAD)
                pe.wait_ge(kf_ready, (b + 1) * G0 + (0 if last else 1) + AHEAD)
                pe.wait_ge(nmT_sb, (b + 1) * G0 + AHEAD)
                for c in range(EC):
                    pe.matmul(ps[:, BK, 0:L], ONES[:, :], XM[:, c, :], start=(c == 0), stop=(c == EC - 1), skip_group_check=True)
                for c in range(EC):
                    pe.matmul(ps[:, BK, L:2 * L], ONES[:, :], XQ[:, c, :], start=(c == 0), stop=(c == EC - 1), skip_group_check=True)
                for c in range(EC):
                    mm = pe.matmul(ps[:, BQ, 0:1], ONES[:, :], MCOL[:, c:c + 1], start=(c == 0), stop=(c == EC - 1))
                mm.then_inc(st_ps, 1)

            def maxima(b, g, n):
                it, s = b * G0 + g, g % 2
                if n == 0:
                    pe.wait_ge(qm_in, (it + 1) * N_HEADS + AHEAD)
                    pe.wait_ge(kh_ready, it + 1 + AHEAD)
                pe.wait_ge(m_read, it * NS + n - 1 + AHEAD)
                h, c = divmod(n, EC)
                pe.matmul(ps[:, BM + n % 2, :], QM[:, h, c * P:(c + 1) * P], KK[:, s, 0, :], start=True, stop=True).then_inc(m_ps, 1)

            def turn_maxima(b, g):
                it, s = b * G0 + g, g % 2
                pe.wait_ge(nm_ready, it + 1 + AHEAD)
                pe.wait_ge(qf_ready, it + 1 + AHEAD)
                if g == 0:
                    pe.wait_ge(st_read, b + AHEAD)
                pe.transpose(ps[0:NS, BQ, 128:128 + P], NM[:, s, :], ID[:, :]).then_inc(nmT_ps, 1)

            def scores(b, g, n):
                it, s = b * G0 + g, g % 2
                h, k = divmod(n, EC)
                if n == 0:
                    pe.wait_ge(max_in, (it + 1) * N_HEADS + AHEAD)
                    pe.wait_ge(km_in[s], (b * (G0 // 2) + g // 2 + 1) * N_HEADS + AHEAD)
                pe.wait_ge(eh_ready, it * NS + n - 1 + AHEAD)
                if g == 0 and n == 0:
                    pe.wait_ge(vf_ready, b + 1 + AHEAD)
                cols = slice(k * P, (k + 1) * P)
                pe.matmul(ps[:, BT + n % 2, :], KM[:, s, h, 0, cols], QH[:, s, :], start=True, stop=False)
                pe.matmul(ps[:, BT + n % 2, :], KM[:, s, h, 0, cols], QL[:, s, :], start=False, stop=False)
                pe.matmul(ps[:, BT + n % 2, :], KM[:, s, h, 1, cols], QH[:, s, :], start=False, stop=True).then_inc(t_ps, 1)

            def weighted(b, g, h, q):
                it = b * G0 + g
                if q == 0:
                    if g == 0 and h == 0:
                        pe.wait_ge(v_split, b + 1 + AHEAD)
                    pe.wait_ge(o_read, it * HG + h - 1 + AHEAD)
                    pe.wait_ge(el_dve, it * NE + (h + 1) * EC // 2 + AHEAD)
                    pe.wait_ge(el_pool, it * NE + (h + 1) * EC // 2 + AHEAD)
                for k in range(EC):
                    out = ps[:, BO + h % 2, q * VW:(q + 1) * VW]
                    cols = slice(q * P, (q + 1) * P)
                    pe.matmul(out, EH[:, h % 2, k, cols], VA[:, k, g * HG + h, :], start=(k == 0), stop=False, skip_group_check=True)
                    mm = pe.matmul(out[:, 0:VW - V2C], EL[:, h % 2, k, cols], VA[:, k, g * HG + h, 0:VW - V2C], start=False,
                                   stop=(k == EC - 1), skip_group_check=True)
                if q == EC - 1:
                    mm.then_inc(o_ps, 1)

            def group(b, g, left=2):
                for n in range(NS):
                    h, k = divmod(n, EC)
                    if left:
                        for m in tiles_beside(n):
                            maxima(*after(b, g), m)
                        if n == TURN_AT:
                            turn_maxima(*after(b, g))
                    scores(b, g, n)
                    if g == G0 - 1 and n == STATS_AT:
                        statistics(b, left == 0)
                    if left > 1 and n == PROJECT_AT:
                        project_queries(*after(*after(b, g)))
                    if left > 1 and n == PROJECT_AT + 1:
                        project_keys(*after(*after(b, g)))
                    if h == 0:
                        previous(b, g, k)
                    else:
                        weighted(b, g, h - 1, k)

            def previous(b, g, q):
                if g == 0 and b is FIRST:
                    return
                if g > 0:
                    weighted(b, g - 1, HG - 1, q)
                else:
                    weighted(b - 1, G0 - 1, HG - 1, q)

            FIRST = 0
            project_queries(0, 0)
            project_keys(0, 0)
            values(0)
            for n in range(NS):
                maxima(0, 0, n)
            turn_maxima(0, 0)
            project_queries(0, 1)
            project_keys(0, 1)
            group(0, 0)
            group(0, 1)
            with pe.Fori(0, B - 1) as b:
                group(b, 2)
                group(b, 3)
                values(b + 1)
                group(b + 1, 0)
                group(b + 1, 1)
            group(B - 1, 2, left=1)
            group(B - 1, 3, left=0)
            for q in range(EC):
                weighted(B - 1, G0 - 1, HG - 1, q)

        @block.scalar
        def _(act):
            act.wait_ge(memset_done, 1 + AHEAD)

            def queries(b, g):
                it = b * G0 + g
                act.wait_ge(q_ps, it + 1 + AHEAD)
                act.wait_ge(qk_split, it + AHEAD)
                act.activation(QF[:, :], ps[:, BQ, :], ACT.Identity, bias=QKB[:, 0, g:g + 1], scale=float(D0) ** -0.5).then_inc(qf_ready, 1)

            def keys(b, g):
                it = b * G0 + g
                act.wait_ge(k_ps, it + 1 + AHEAD)
                act.activation(KF[:, :], ps[:, BK, :], ACT.Identity, bias=QKB[:, 1, g:g + 1]).then_inc(kf_ready, 1)

            def cut(b):
                act.wait_ge(inputs_in, (b + 1) * N_IN + AHEAD)
                act.wait_ge(k_ps, b * G0 + AHEAD)
                act.wait_ge(v_ps, b + AHEAD)
                act.activation(XH[:, :, :], X[:, :, :], ACT.Copy)
                act.activation(CH[:, :, :], C[:, :, :], ACT.Copy).then_inc(xc_high, 1)

            def group(b, g, left=2, prior=None):
                it = b * G0 + g
                for h in range(HG):
                    for k in range(EC):
                        n = h * EC + k
                        act.wait_ge(t_ps, it * NS + n + 1 + AHEAD)
                        if k == 0:
                            act.wait_ge(o_ps, it * HG + h - 1 + AHEAD)
                        act.wait_ge(el_pool if k % 2 else el_dve, it * NE + n // 2 - 1 + AHEAD)
                        act.activation(EX[:, n % 4, :], ps[:, BT + n % 2, :], ACT.Exp).then_inc(ex_ready, 1)
                        act.activation(EH[:, h % 2, k, :], ps[:, BT + n % 2, :], ACT.Exp).then_inc(eh_ready, 1)
                        if left > 1 and n == PROJECT_AT:
                            queries(*after(*after(b, g)))
                        if left > 1 and n == PROJECT_AT + 1:
                            keys(*after(*after(b, g)))
                    if g == 0 and h == 0:
                        act.wait_ge(vf_ready, b + 1 + AHEAD)
                        act.activation(VF[:, :, :, D0:], VF[:, :, :, 0:D0], ACT.Square)
                        act.drain()
                        act.wait_ge(o_ps, b * H0 + AHEAD)
                        act.activation(VA[:, :, :, 1:1 + V2C], VF[:, :, :, :], ACT.Copy).then_inc(v_square, 1)
                    if g == 2 and h == 1:
                        act.wait_ge(stats_in, b + 1 + AHEAD)
                        act.wait_ge(out_free, b + AHEAD)
                        act.activation(XQ[:, :, :], XM[:, :, :], ACT.Square).then_inc(sq_ready, 1)
                    if g == 2 and h == 0 and left > 1:
                        cut(b + 1)
                    if g == 0 and h == 2 and prior is not None:
                        roots(prior)

            def roots(b):
                act.wait_ge(var_x, b + 1 + AHEAD)
                act.activation(ST[:, 3, :], ST[:, 2, :], ACT.Sqrt, bias=EPS[:, 0:1])
                act.wait_ge(var_v, b + 1 + AHEAD)
                act.activation(VAR[:, :, :], VAR[:, :, :], ACT.Sqrt).then_inc(std_ready, 1)

            act.wait_ge(weights_split, 1 + AHEAD)
            cut(0)
            queries(0, 0)
            keys(0, 0)
            queries(0, 1)
            keys(0, 1)
            group(0, 0)
            group(0, 1)
            with act.Fori(0, B - 1) as b:
                group(b, 2)
                group(b, 3)
                group(b + 1, 0, prior=b)
                group(b + 1, 1)
            group(B - 1, 2, left=1)
            group(B - 1, 3, left=0)
            roots(B - 1)

        @block.vector
        def _(dve):
            dve.wait_ge(consts_in, 7 * 16 + AHEAD)
            for full, high, low in ((WQK, WH[:, :, :, :, :], WL[:, :, :, :, :]), (WV, WVH[:, :, :], WVL[:, :, :])):
                dve.tensor_copy(high, full)
                dve.drain()
                dve.tensor_tensor(low, full, high, ALU.subtract)
            dve.tensor_copy(MSELR[:, :], MSEL[:, :])
            dve.tensor_tensor(QKB[:, :, :], QKB[:, :, :], AUG[:, :, :], ALU.add)
            dve.drain()
            dve.tensor_scalar(QKB[:, 0, :], QKB[:, 0, :], float(D0) ** -0.5, None, ALU.mult).then_inc(weights_split, 1)

            def split(b, g):
                it, s = b * G0 + g, g % 2
                dve.wait_ge(t_ps, (it - 1) * NS + AHEAD)
                dve.wait_ge(km_in[s], (b * (G0 // 2) + g // 2) * N_HEADS + AHEAD)
                dve.wait_ge(qf_ready, it + 1 + AHEAD)
                dve.tensor_copy(QH[:, s, :], QF[:, :]).then_inc(qh_ready, 1)
                dve.wait_ge(kf_ready, it + 1 + AHEAD)
                dve.tensor_copy(KK[:, s, 0, :], KF[:, :]).then_inc(kh_ready, 1)
                dve.wait_ge(qh_ready, it + 1 + AHEAD)
                dve.tensor_tensor(QL[:, s, :], QF[:, :], QH[:, s, :], ALU.subtract)
                dve.wait_ge(kh_ready, it + 1 + AHEAD)
                dve.tensor_tensor(KK[:, s, 1, :], KF[:, :], KK[:, s, 0, :], ALU.subtract).then_inc(qk_split, 1)

            def take_max(b, g, n):
                it, s = b * G0 + g, g % 2
                dve.wait_ge(m_ps, it * NS + n + 1 + AHEAD)
                dve.tensor_reduce(NM[:, s, n:n + 1], ps[:, BM + n % 2, :], AX.X, ALU.max, negate=True).then_inc(m_read, 1)
                if n == NS - 1:
                    dve.drain().then_inc(nm_ready, 1)

            def turned_maxima(b, g):
                it, s = b * G0 + g, g % 2
                dve.wait_ge(nmT_ps, it + 1 + AHEAD)
                dve.wait_ge(max_in, (it - 1) * N_HEADS + AHEAD)
                dve.tensor_copy(NMT[:, s, :], ps[0:NS, BQ, 128:128 + P]).then_inc(nmT_sb, 1)

            def sums(b, g, h):
                it, s = b * G0 + g, g % 2
                if h == 0:
                    dve.wait_ge(u_read, it - 1 + AHEAD)
                dve.wait_ge(o_ps, it * HG + h + 1 + AHEAD)
                tile = ps[:, BO + h % 2, 0:EC * VW].rearrange("p (q v) -> p q v", q=EC)
                dve.reciprocal(DEN[:, s, :, h, :], tile[:, :, 0:1])
                dve.tensor_reduce(U[:, s, :, h, :], tile[:, :, 1:].rearrange("p q (a v) -> p q v a", a=3), AX.X, ALU.add)\
                   .then_inc(o_read, 1)
                if h == HG - 1:
                    dve.drain().then_inc(den_ready, 1)

            def cut(b):
                dve.wait_ge(inputs_in, (b + 1) * N_IN + AHEAD)
                dve.wait_ge(k_ps, b * G0 + AHEAD)
                dve.wait_ge(v_ps, b + AHEAD)
                dve.tensor_scalar(MBRR[:, :], M8R[:, :], -NEG, NEG, ALU.mult, ALU.add)
                dve.wait_ge(xc_high, b + 1 + AHEAD)
                dve.tensor_tensor(XL[:, :, :], X[:, :, :], XH[:, :, :], ALU.subtract)
                dve.tensor_tensor(CL[:, :, :], C[:, :, :], CH[:, :, :], ALU.subtract).then_inc(xc_split, 1)
                dve.drain().then_inc(inputs_read, 1)

            def take_values(b):
                dve.wait_ge(v_ps, b + 1 + AHEAD)
                dve.wait_ge(v_split, b + AHEAD)
                dve.tensor_tensor(VF[:, :, :, 0:D0], ps[:, BT:BT + 2, :].rearrange("p a (c h d) -> p (a c) h d", c=2, h=H0),
                                  BVB[:, :].rearrange("p (h d) -> p h d", h=H0).unsqueeze(1).broadcast_to([P, EC, H0, D0]), ALU.add)\
                   .then_inc(vf_ready, 1)

            def cut_values(b):
                dve.wait_ge(v_square, b + 1 + AHEAD)
                dve.tensor_tensor(VF[:, :, :, :], VF[:, :, :, :], VA[:, :, :, 1:1 + V2C], ALU.subtract)
                dve.drain()
                dve.tensor_copy(VA[:, :, :, 1 + V2C:1 + 2 * V2C], VF[:, :, :, :])
                dve.drain()
                dve.tensor_tensor(VA[:, :, :, 1 + 2 * V2C:], VF[:, :, :, :], VA[:, :, :, 1 + V2C:1 + 2 * V2C], ALU.subtract).then_inc(v_split, 1)

            def mask_x(b):
                dve.wait_ge(stats_x_in, (b + 1) * N_STATS + AHEAD)
                dve.wait_ge(out_ready, b + AHEAD)
                dve.tensor_copy(MCOL[:, :], M8C[:, :])
                dve.drain()
                for c in range(EC):
                    dve.tensor_scalar(XM[:, c, :], XT[:, c, :], MCOL[:, c:c + 1], None, ALU.mult)
                dve.drain().then_inc(stats_in, 1)
                dve.sem_inc(stats_read, 1)

            def moments(b):
                dve.wait_ge(st_ps, b + 1 + AHEAD)
                dve.reciprocal(RN[:, :], ps[:, BQ, 0:1])
                dve.drain()
                dve.tensor_scalar(ST[:, 0, :], ps[:, BK, 0:L], RN[:, 0:1], None, ALU.mult)
                dve.tensor_scalar(ST[:, 1, :], ps[:, BK, L:2 * L], RN[:, 0:1], None, ALU.mult)
                dve.drain().then_inc(st_read, 1)
                dve.tensor_tensor(ST[:, 2, :], ST[:, 0, :], ST[:, 0, :], ALU.mult)
                dve.drain()
                dve.tensor_tensor(ST[:, 2, :], ST[:, 1, :], ST[:, 2, :], ALU.subtract)
                dve.drain()
                dve.tensor_scalar(ST[:, 2, :], ST[:, 2, :], 0.0, None, ALU.max).then_inc(var_x, 1)

            def low_part(b, g, n):
                if n % 2 == 0:
                    dve.wait_ge(eh_ready, (b * G0 + g) * NS + n + 1 + AHEAD)
                    dve.tensor_tensor(EL[:, (n // EC) % 2, n % EC, :], EX[:, n % 4, :], EH[:, (n // EC) % 2, n % EC, :], ALU.subtract)\
                       .then_inc(el_dve, 1)

            def group(b, g, left=2, prior=None):
                if left:
                    split(*after(b, g))
                for n in range(NS):
                    h, k = divmod(n, EC)
                    if left:
                        for m in tiles_beside(n):
                            take_max(*after(b, g), m)
                        if n == TURN_AT:
                            turned_maxima(*after(b, g))
                    if g == G0 - 1 and n == MOMENTS_AT:
                        moments(b)
                    if n > 0:
                        low_part(b, g, n - 1)
                    if g == 0 and n == 4:
                        cut_values(b)
                    if g == 1 and n == 13:
                        mask_x(b)
                    if g == 2 and n == 4 and left > 1:
                        cut(b + 1)
                    if g == 0 and n == 13 and prior is not None:
                        inverse_root(prior)
                    if k == 0 and h > 1:
                        sums(b, g, h - 2)
                    if k == 0 and h == 1 and (g > 0 or prior is not None):
                        sums(b if g > 0 else prior, g - 1 if g > 0 else G0 - 1, HG - 1)
                low_part(b, g, NS - 1)
                sums(b, g, HG - 2)

            def inverse_root(b):
                dve.wait_ge(std_ready, b + 1 + AHEAD)
                dve.reciprocal(ST[:, 3, :], ST[:, 3, :]).then_inc(rstd_ready, 1)

            cut(0)
            split(0, 0)
            take_values(0)
            for n in range(NS):
                take_max(0, 0, n)
            turned_maxima(0, 0)
            group(0, 0)
            group(0, 1)
            with dve.Fori(0, B - 1) as b:
                group(b, 2)
                group(b, 3)
                take_values(b + 1)
                group(b + 1, 0, prior=b)
                group(b + 1, 1)
            group(B - 1, 2, left=1)
            group(B - 1, 3, left=0)
            sums(B - 1, G0 - 1, HG - 1)
            inverse_root(B - 1)

S1 = 16
DM, DD = 32, 64
(V_LN1W, V_LN1B, V_LN2W, V_LN2B, V_MAAX, V_STACK, V_TD, V_U, V_GNW, V_GNB, V_FK, V_FR) = \
    (0, 1, 2, 3, 4, 5, 10, 11, 12, 13, 14, 15)
NV1 = 16
W_K, W_V, W_R, W_G, W_O, W_FK, W_FR, W_FV = range(8)
MIX_K, MIX_W, MIX_V, MIX_R, MIX_G = range(5)


def layer1(nc, x1T, ctxT, s0, vecs, w8, maa_w1, maa_w2, td_w1, td_w2, sel, selT, blk, x2T):
    with ExitStack() as stack:
        def sb(name, shape, dt=F32):
            return stack.enter_context(nc.sbuf_tensor("b_" + name, shape, dt))

        sems = []

        def sem(name):
            sems.append(stack.enter_context(nc.semaphore("b_" + name)))
            return sems[-1]

        W = sb("w", [P, 8, EC, E])
        W1 = sb("w1", [P, EC, 5 * DM])
        W2A = sb("w2a", [4 * DM, E])
        W2B = sb("w2b", [DM, E])
        TW1 = sb("tw1", [P, EC, DD])
        TW2 = sb("tw2", [DD, E])
        SEL = sb("sel", [P, S1, P])
        SELT = sb("selT", [P, S1, P])
        BO = sb("bo", [P, P])
        BM = sb("bm", [P, P])
        VEC = sb("vec", [P, NV1, EC])
        MEANW = sb("meanw", [P, P])
        EPS = sb("eps", [P, 1])
        X = sb("x", [P, EC, L])
        CT = sb("ct", [P, EC, L])
        S0 = sb("s0", [P, EC, S1])
        XP = sb("xp", [P, EC, L + 1])
        SX = sb("sx", [P, EC, L])
        Z = sb("z", [P, EC, L])
        XC = sb("xc", [P, EC, L])
        SQ = sb("sq", [P, EC, L])
        SD = sb("sd", [P, L])
        XF = sb("xf", [P, 2, EC, L])
        KT, VT, RT, WT, GT, TH, BV, OG = [sb(n, [P, EC, L]) for n in ("kt", "vt", "rt", "wt", "gt", "th", "bv", "og")]
        T0 = sb("t0", [P, L])
        T1 = sb("t1", [DM, L])
        TW = sb("tw", [DD, L])
        A = sb("a", [P, 4, L])
        Y = sb("y", [P, 4, L])
        RC = sb("rc", [P, L])
        SB = sb("sb", [P, S1, L + 1])
        ps = stack.enter_context(nc.psum_tensor("b_ps", [P, 8, 512], F32))

        def pair(bank):
            return ps[:, bank:bank + 2, :].rearrange("p a (c t) -> p (a c) t", c=2)

        PF, PA, PB, SM0, SM1 = pair(0), pair(2), pair(4), ps[:, 6, 0:L], ps[:, 7, 0:L]

        weights_in, x_in, x_used, memset_done = sem("weights_in"), sem("x_in"), sem("x_used"), sem("memset_done")
        ln_in, mean_ps, xc_ready, sq_ready, var_ps, sd_ready = [sem(n) for n in ("ln_in", "mean_ps", "xc_ready", "sq_ready", "var_ps", "sd_ready")]
        z_ready, h_ps, t_ready = sem("z_ready"), sem("h_ps"), sem("t_ready")
        mix_ps, mix_read, mix_ready, proj_ps, proj_read = [sem(n) for n in ("mix_ps", "mix_read", "mix_ready", "proj_ps", "proj_read")]
        tw_ps, tw_ready, w_ready, th_ready = sem("tw_ps"), sem("tw_ready"), sem("w_ready"), sem("th_ready")
        rku_ready, bonus_ps, bonus_read = sem("rku_ready"), sem("bonus_ps"), sem("bonus_read")
        vb_ps, vb_read, s_ready, s_used, y_ready, y_used, o_ps, o_read = [sem(n) for n in ("vb_ps", "vb_read", "s_ready", "s_used", "y_ready", "y_used", "o_ps", "o_read")]
        og_ready, gm_ps, gc_ready, gq_ready, gv_ps, gd_ready = [sem(n) for n in ("og_ready", "gm_ps", "gc_ready", "gq_ready", "gv_ps", "gd_ready")]
        gated, wo_ps, x1_ready = sem("gated"), sem("wo_ps"), sem("x1_ready")
        ffn_in, ffr_ps, ffk_ps, rr_ready, kk_ready, kk2_ready, ffv_ps = [sem(n) for n in ("ffn_in", "ffr_ps", "ffk_ps", "rr_ready", "kk_ready", "kk2_ready", "ffv_ps")]
        out_ready, out_stored = sem("out_ready"), sem("out_stored")
        passed = sem("passed")
        NLN = 2
        block = stack.enter_context(nc.Block())

        @block.sync
        def _(sp):
            start_ahead(sp, sems)
            for dst, src in ((W[:, :, :, :], w8), (W1[:, :, :], maa_w1), (W2A[:, :], maa_w2[0:4 * DM]), (W2B[:, :], maa_w2[4 * DM:]),
                             (TW1[:, :, :], td_w1), (TW2[:, :], td_w2), (SEL[:, :, :], sel), (SELT[:, :, :], selT),
                             (BO[:, :], blk[0]), (BM[:, :], blk[1]), (VEC[:, :, :], vecs)):
                sp.dma_start(dst, src).then_inc(weights_in, 16)
            with sp.Fori(0, B) as b:
                sp.wait_ge(x_used, b + AHEAD)
                sp.dma_start(X[:, :, :], x1T[b]).then_inc(x_in, 16)
                sp.dma_start(CT[:, :, :], ctxT[b].rearrange("(k p) c -> p k c", p=P)).then_inc(x_in, 16)
                sp.dma_start(S0[:, :, :], s0[b]).then_inc(x_in, 16)
                sp.wait_ge(out_ready, b + 1 + AHEAD)
                sp.dma_start(x2T[b], OG[:, :, :]).then_inc(out_stored, 16)
            sp.wait_ge(out_stored, 16 * B + AHEAD)
        def project(pe, out, w, src):
            for o in range(EC):
                for k in range(EC):
                    mm = pe.matmul(out[:, o, :], W[:, w, k, o * P:(o + 1) * P], src[:, k, :], start=(k == 0),
                                   stop=(k == EC - 1), skip_group_check=True)
            return mm

        @block.tensor
        def _(pe):
            pe.wait_ge(weights_in, 16 * 11 + AHEAD)
            pe.wait_ge(memset_done, 1 + AHEAD)
            def norm(n, src):
                pe.wait_ge(ln_in, n + 1 + AHEAD)
                for k in range(EC):
                    mm = pe.matmul(SM0, MEANW[:, :], src[:, k, :], start=(k == 0), stop=(k == EC - 1))
                mm.then_inc(mean_ps, 1)
                pe.wait_ge(sq_ready, n + 1 + AHEAD)
                for k in range(EC):
                    mm = pe.matmul(SM1, MEANW[:, :], SQ[:, k, :], start=(k == 0), stop=(k == EC - 1))
                mm.then_inc(var_ps, 1)

            with pe.Fori(0, B) as b:
                norm(b * NLN, X)
                pe.wait_ge(z_ready, b + 1 + AHEAD)
                for k in range(EC):
                    pe.matmul(SM0, W1[:, k, 0:P], Z[:, k, :], start=(k == 0), stop=(k == EC - 1))
                for k in range(EC):
                    mm = pe.matmul(SM1[0:DM, :], W1[:, k, P:], Z[:, k, :], start=(k == 0), stop=(k == EC - 1))
                mm.then_inc(h_ps, 1)
                pe.wait_ge(t_ready, b + 1 + AHEAD)
                def mix(f):
                    if f > 0:
                        pe.wait_ge(mix_read, b * 5 + f + AHEAD)
                    for o in range(EC):
                        if f < 4:
                            lo, hi = W2A[f * DM:(f + 1) * DM, o * P:(o + 1) * P], T0[f * DM:(f + 1) * DM, :]
                        else:
                            lo, hi = W2B[:, o * P:(o + 1) * P], T1[:, :]
                        mm = pe.matmul(PF[:, o, :], lo, hi, start=True, stop=True)
                    mm.then_inc(mix_ps, 1)

                mix(0)
                for f in range(5):
                    if f < 4:
                        mix(f + 1)
                    pe.wait_ge(mix_ready, b * 5 + f + 1 + AHEAD)
                    if f >= 2:
                        pe.wait_ge(proj_read, b * 5 + f - 1 + AHEAD)
                    dst = PA if f % 2 == 0 else PB
                    if f == MIX_W:
                        for k in range(EC):
                            mm = pe.matmul(SM0[0:DD, :], TW1[:, k, :], XF[:, f % 2, k, :], start=(k == 0), stop=(k == EC - 1))
                        mm.then_inc(tw_ps, 1)
                        pe.wait_ge(tw_ready, b + 1 + AHEAD)
                        for o in range(EC):
                            mm = pe.matmul(dst[:, o, :], TW2[:, o * P:(o + 1) * P], TW[:, :], start=True, stop=True)
                    else:
                        mm = project(pe, dst, {MIX_K: W_K, MIX_V: W_V, MIX_R: W_R, MIX_G: W_G}[f], XF[:, f % 2])
                    mm.then_inc(proj_ps, 1)
                pe.wait_ge(rku_ready, b + 1 + AHEAD)
                pe.wait_ge(proj_read, b * 5 + 5 + AHEAD)
                for o in range(EC):
                    mm = pe.matmul(PA[:, o, :], BO[:, :], Z[:, o, :], start=True, stop=True)
                mm.then_inc(bonus_ps, 1)
                pe.wait_ge(bonus_read, b + 1 + AHEAD)
                pe.sem_inc(passed, 1)
                with pe.Fori(0, EC) as c:
                    st = b * EC + c
                    pe.wait_ge(o_read, st + AHEAD)
                    def spread(j):
                        if j >= 4:
                            pe.wait_ge(vb_read, st * S1 + j - 3 + AHEAD)
                        else:
                            pe.wait_ge(vb_read, st * S1 + AHEAD)
                        pe.matmul(ps[:, j % 4, 0:L], SEL[:, j, :], VT[:, c, :], start=True, stop=True).then_inc(vb_ps, 1)

                    for j in range(3):
                        spread(j)
                    for j in range(S1):
                        if j + 3 < S1:
                            spread(j + 3)
                        pe.wait_ge(y_ready, st * S1 + j + 1 + AHEAD)
                        pe.matmul(SM0, SELT[:, j, :], Y[:, j % 4, :], start=(j == 0), stop=(j == S1 - 1)).then_inc(y_used, 1)
                pe.wait_ge(og_ready, b + 1 + AHEAD)
                for o in range(EC):
                    mm = pe.matmul(PA[:, o, :], BM[:, :], OG[:, o, :], start=True, stop=True)
                mm.then_inc(gm_ps, 1)
                pe.wait_ge(gq_ready, b + 1 + AHEAD)
                for o in range(EC):
                    mm = pe.matmul(PB[:, o, :], BM[:, :], SQ[:, o, :], start=True, stop=True)
                mm.then_inc(gv_ps, 1)
                pe.wait_ge(gated, b + 1 + AHEAD)
                project(pe, PA, W_O, Z).then_inc(wo_ps, 1)
                norm(b * NLN + 1, X)
                pe.wait_ge(ffn_in, b + 1 + AHEAD)
                project(pe, PA, W_FR, XF[:, 0]).then_inc(ffr_ps, 1)
                project(pe, PB, W_FK, XF[:, 1]).then_inc(ffk_ps, 1)
                pe.wait_ge(kk2_ready, b + 1 + AHEAD)
                pe.wait_ge(rr_ready, b + 1 + AHEAD)
                project(pe, PA, W_FV, KT).then_inc(ffv_ps, 1)

        @block.scalar
        def _(act):
            act.wait_ge(weights_in, 16 * 11 + AHEAD)
            act.wait_ge(memset_done, 1 + AHEAD)
            def norm(n):
                act.wait_ge(xc_ready, n + 1 + AHEAD)
                act.activation(SQ[:, :, :], XC[:, :, :], ACT.Square).then_inc(sq_ready, 1)
                act.wait_ge(var_ps, n + 1 + AHEAD)
                act.activation(SD[:, :], SM1, ACT.Sqrt, bias=EPS[:, 0:1]).then_inc(sd_ready, 1)

            with act.Fori(0, B) as b:
                norm(b * NLN)
                act.wait_ge(h_ps, b + 1 + AHEAD)
                act.activation(T0[:, :], SM0, ACT.Tanh)
                act.activation(T1[:, :], SM1[0:DM, :], ACT.Tanh).then_inc(t_ready, 1)
                act.wait_ge(proj_ps, b * 5 + 1 + AHEAD)
                act.activation(KT[:, :, :], PA, ACT.Copy).then_inc(proj_read, 1)
                act.wait_ge(tw_ps, b + 1 + AHEAD)
                act.activation(TW[:, :], SM0[0:DD, :], ACT.Tanh).then_inc(tw_ready, 1)
                act.wait_ge(proj_ps, b * 5 + 2 + AHEAD)
                for o in range(EC):
                    act.activation(TH[:, o, :], PB[:, o, :], ACT.Exp, bias=VEC[:, V_TD, o:o + 1])
                act.drain().then_inc(proj_read, 1)
                act.activation(WT[:, :, :], TH[:, :, :], ACT.Exp, scale=-1.0).then_inc(w_ready, 1)
                act.wait_ge(proj_ps, b * 5 + 3 + AHEAD)
                act.activation(VT[:, :, :], PA, ACT.Copy).then_inc(proj_read, 1)
                act.wait_ge(proj_ps, b * 5 + 4 + AHEAD)
                act.activation(RT[:, :, :], PB, ACT.Copy).then_inc(proj_read, 1)
                act.wait_ge(proj_ps, b * 5 + 5 + AHEAD)
                act.activation(TH[:, :, :], PA, ACT.Tanh, scale=0.5).then_inc(th_ready, 1)
                act.wait_ge(gc_ready, b + 1 + AHEAD)
                act.activation(SQ[:, :, :], XC[:, :, :], ACT.Square).then_inc(gq_ready, 1)
                act.wait_ge(gv_ps, b + 1 + AHEAD)
                act.activation(TH[:, :, :], PB, ACT.Sqrt, bias=EPS[:, 0:1]).then_inc(gd_ready, 1)
                norm(b * NLN + 1)
                act.wait_ge(ffr_ps, b + 1 + AHEAD)
                act.activation(RT[:, :, :], PA, ACT.Tanh, scale=0.5).then_inc(rr_ready, 1)
                act.wait_ge(ffk_ps, b + 1 + AHEAD)
                act.activation(KT[:, :, :], PB, ACT.Relu).then_inc(kk_ready, 1)

        @block.gpsimd
        def _(pool):
            pool.memset(MEANW[:, :], 1.0 / E)
            pool.memset(EPS[:, :], LN_EPS).then_inc(memset_done, 1)
            with pool.Fori(0, B) as b:
                with pool.Fori(0, EC) as c:
                    st = b * EC + c
                    for j in range(S1):
                        pool.wait_ge(s_ready, st * S1 + j + 1 + AHEAD)
                        if j >= 4:
                            pool.wait_ge(y_used, st * S1 + j - 3 + AHEAD)
                        else:
                            pool.wait_ge(y_used, st * S1 + AHEAD)
                        pool.tensor_tensor(Y[:, j % 4, :], SB[:, j, 0:L], RC[:, :], ALU.mult).then_inc(y_ready, 1)
                pool.wait_ge(kk_ready, b + 1 + AHEAD)
                pool.tensor_tensor(KT[:, :, :], KT[:, :, :], KT[:, :, :], ALU.mult).then_inc(kk2_ready, 1)

        @block.vector
        def _(dve):
            dve.wait_ge(weights_in, 16 * 11 + AHEAD)
            def vec(v, o):
                return VEC[:, v, o:o + 1]

            def norm(n, src, w, bias, prev_col):
                dve.wait_ge(mean_ps, n + 1 + AHEAD)
                dve.tensor_tensor(XC[:, :, :], src[:, :, :], SM0.unsqueeze(1).broadcast_to([P, EC, L]), ALU.subtract)\
                   .then_inc(xc_ready, 1)
                dve.tensor_copy(XP[:, :, 0:1], CT[:, :, prev_col:prev_col + 1])
                dve.wait_ge(sd_ready, n + 1 + AHEAD)
                dve.reciprocal(SD[:, :], SD[:, :])
                dve.drain()
                dve.tensor_tensor(XC[:, :, :], XC[:, :, :], SD[:, :].unsqueeze(1).broadcast_to([P, EC, L]), ALU.mult)
                dve.drain()
                for o in range(EC):
                    dve.tensor_scalar(XP[:, o, 1:L + 1], XC[:, o, :], vec(w, o), vec(bias, o), ALU.mult, ALU.add)
                dve.drain()
                dve.tensor_tensor(SX[:, :, :], XP[:, :, 0:L], XP[:, :, 1:L + 1], ALU.subtract)
                dve.drain()

            with dve.Fori(0, B) as b:
                dve.wait_ge(x_in, (b + 1) * 48 + AHEAD)
                dve.sem_inc(ln_in, 1)
                norm(b * NLN, X, V_LN1W, V_LN1B, 1)
                for o in range(EC):
                    dve.scalar_tensor_tensor(Z[:, o, :], SX[:, o, :], vec(V_MAAX, o), XP[:, o, 1:L + 1], ALU.mult, ALU.add)
                dve.drain().then_inc(z_ready, 1)
                for f in range(5):
                    dve.wait_ge(mix_ps, b * 5 + f + 1 + AHEAD)
                    if f >= 2:
                        dve.wait_ge(proj_ps, b * 5 + f - 1 + AHEAD)
                    for o in range(EC):
                        dve.scalar_tensor_tensor(XF[:, f % 2, o, :], PF[:, o, :], vec(V_STACK + f, o), SX[:, o, :], ALU.add, ALU.mult)
                    dve.drain().then_inc(mix_read, 1)
                    dve.tensor_tensor(XF[:, f % 2], XF[:, f % 2], XP[:, :, 1:L + 1], ALU.add).then_inc(mix_ready, 1)
                dve.wait_ge(th_ready, b + 1 + AHEAD)
                dve.tensor_scalar(TH[:, :, :], TH[:, :, :], 0.5, 0.5, ALU.mult, ALU.add)
                dve.drain()
                dve.tensor_tensor(GT[:, :, :], TH[:, :, :], PA, ALU.mult).then_inc(proj_read, 1)
                dve.tensor_tensor(Z[:, :, :], RT[:, :, :], KT[:, :, :], ALU.mult)
                dve.drain()
                for o in range(EC):
                    dve.tensor_scalar(Z[:, o, :], Z[:, o, :], vec(V_U, o), None, ALU.mult)
                dve.drain().then_inc(rku_ready, 1)
                dve.wait_ge(bonus_ps, b + 1 + AHEAD)
                dve.tensor_tensor(BV[:, :, :], VT[:, :, :], PA, ALU.mult).then_inc(bonus_read, 1)
                dve.wait_ge(w_ready, b + 1 + AHEAD)
                dve.wait_ge(out_stored, b * 16 + AHEAD)
                dve.sem_inc(passed, 1)
                with dve.Fori(0, EC) as c:
                    st = b * EC + c
                    dve.wait_ge(y_ready, st * S1 + AHEAD)
                    dve.tensor_copy(SB[:, :, 0:1], S0[:, c, :].unsqueeze(2))
                    dve.tensor_copy(RC[:, :], RT[:, c, :])
                    for j in range(S1):
                        dve.wait_ge(vb_ps, st * S1 + j + 1 + AHEAD)
                        dve.tensor_tensor(A[:, j % 4, :], KT[:, c, :], ps[:, j % 4, 0:L], ALU.mult).then_inc(vb_read, 1)
                        if j > 0:
                            dve.wait_ge(vb_read, st * S1 + j + AHEAD)
                            dve.tensor_tensor_scan(SB[:, j - 1, 1:L + 1], WT[:, c, :], A[:, (j - 1) % 4, :], S0[:, c, j - 1:j], ALU.mult, ALU.add)\
                               .then_inc(s_ready, 1)
                    dve.drain()
                    dve.tensor_tensor_scan(SB[:, S1 - 1, 1:L + 1], WT[:, c, :], A[:, (S1 - 1) % 4, :], S0[:, c, S1 - 1:S1], ALU.mult, ALU.add)\
                       .then_inc(s_ready, 1)
                    dve.wait_ge(y_used, (st + 1) * S1 + AHEAD)
                    dve.tensor_tensor(OG[:, c, :], BV[:, c, :], SM0, ALU.add).then_inc(o_read, 1)
                dve.drain().then_inc(og_ready, 1)
                dve.wait_ge(gm_ps, b + 1 + AHEAD)
                dve.tensor_tensor(XC[:, :, :], OG[:, :, :], PA, ALU.subtract).then_inc(gc_ready, 1)
                dve.wait_ge(gd_ready, b + 1 + AHEAD)
                dve.reciprocal(TH[:, :, :], TH[:, :, :])
                dve.drain()
                dve.tensor_tensor(XC[:, :, :], XC[:, :, :], TH[:, :, :], ALU.mult)
                dve.drain()
                for o in range(EC):
                    dve.tensor_scalar(XC[:, o, :], XC[:, o, :], vec(V_GNW, o), vec(V_GNB, o), ALU.mult, ALU.add)
                dve.drain()
                dve.tensor_tensor(Z[:, :, :], XC[:, :, :], GT[:, :, :], ALU.mult).then_inc(gated, 1)
                dve.wait_ge(wo_ps, b + 1 + AHEAD)
                dve.tensor_tensor(X[:, :, :], X[:, :, :], PA, ALU.add).then_inc(ln_in, 1)
                dve.drain()
                norm(b * NLN + 1, X, V_LN2W, V_LN2B, 0)
                for o in range(EC):
                    dve.scalar_tensor_tensor(XF[:, 0, o, :], SX[:, o, :], vec(V_FR, o), XP[:, o, 1:L + 1], ALU.mult, ALU.add)
                    dve.scalar_tensor_tensor(XF[:, 1, o, :], SX[:, o, :], vec(V_FK, o), XP[:, o, 1:L + 1], ALU.mult, ALU.add)
                dve.drain().then_inc(ffn_in, 1)
                dve.wait_ge(rr_ready, b + 1 + AHEAD)
                dve.tensor_scalar(RT[:, :, :], RT[:, :, :], 0.5, 0.5, ALU.mult, ALU.add)
                dve.drain()
                dve.wait_ge(ffv_ps, b + 1 + AHEAD)
                dve.tensor_tensor(OG[:, :, :], RT[:, :, :], PA, ALU.mult)
                dve.drain()
                dve.tensor_tensor(OG[:, :, :], OG[:, :, :], X[:, :, :], ALU.add).then_inc(out_ready, 1)
                dve.drain().then_inc(x_used, 1)

H2, K2, F2 = 16, 128, 2048
N2 = 2 * L
FC2 = F2 // P
PACK = 3 * EC * P + 3 + 2 * P
(V2_NW, V2_NB, V2_BO) = range(3)


def layer2(nc, x2T, ctxT, packs, downs, fc1, vec2, ident_in, x3T):
    with ExitStack() as stack:
        def sb(name, shape, dt=F32):
            return stack.enter_context(nc.sbuf_tensor("c_" + name, shape, dt))

        sems = []

        def sem(name):
            sems.append(stack.enter_context(nc.semaphore("c_" + name)))
            return sems[-1]

        def dma_sem(name):
            return stack.enter_context(nc.semaphore("c_" + name))

        X = sb("x", [P, EC, N2])
        CT = sb("ct", [P, EC, N2])
        H = sb("h", [P, EC, N2])
        SQ = sb("sq", [P, EC, N2])
        SD = sb("sd", [P, N2])
        ID = sb("id", [P, P])
        MEANW = sb("meanw", [P, P])
        ONES = sb("ones", [1, P])
        EPS = sb("eps", [P, 1])
        VEC = sb("vec", [P, 3, 3, EC])
        PK = sb("pk", [P, 2, PACK])
        WD = sb("wd", [P, 2, H2, P])
        W1 = sb("w1", [P, 2, EC * P + 1])
        QT = sb("qt", [P, 2, N2])
        KT = sb("kt", [P, 2, 2, L + 1])
        V = sb("v", [P, 2, 4, P])
        NM = sb("nm", [P, 4])
        RS = sb("rs", [P, 4])
        PR = sb("pr", [P, 4, L + 1])
        PT = sb("pt", [P, 2, 2, L])
        PTB = sb("ptb", [1, N2])
        G = sb("g", [P, FC2, N2])
        ps = stack.enter_context(nc.psum_tensor("c_ps", [P, 8, 512], F32))
        BQ, BK, BV, BS, BT, BC = 0, 1, 2, 3, 5, 7

        names = """consts_in x_in ct_in x_used memset_done ln_in mean_ps xc_ready sq_ready var_ps sd_ready h_ready
            pack_used q_ps k_ps v_ps q_ready k_ready v_ready s_ps max_ready exp_ready p_ready t_ps t_ready tb_ps tb_ready
            c_ps c_ready down_ps x_ready fc_used fc_ps fc_ready out_stored passed out_free"""
        S = {n: dma_sem(n) if n == "out_stored" else sem(n) for n in names.split()}
        (consts_in, x_in, ct_in, x_used, memset_done, ln_in, mean_ps, xc_ready, sq_ready, var_ps, sd_ready, h_ready,
         pack_used, q_ps, k_ps, v_ps, q_ready, k_ready, v_ready, s_ps, max_ready, exp_ready, p_ready, t_ps, t_ready, tb_ps,
         tb_ready, c_ps, c_ready, down_ps, x_ready, fc_used, fc_ps, fc_ready, out_stored, passed, out_free) = [S[n] for n in names.split()]
        pack_in = [sem(f"pack_in{i}") for i in range(2)]
        down_in = [dma_sem(f"down_in{i}") for i in range(2)]
        fc_in = [dma_sem(f"fc_in{i}") for i in range(2)]
        NPAIR = B // 2
        block = stack.enter_context(nc.Block())

        def weights(u, which):
            return PK[:, u, which * EC * P:(which + 1) * EC * P].rearrange("p (k m) -> p k m", k=EC)

        def column(u, i):
            return PK[:, u, 3 * EC * P + i:3 * EC * P + i + 1]

        def row(u, i):
            at = 3 * EC * P + 3 + i * P
            return PK[0:1, u, at:at + P]

        @block.sync
        def _(sp):
            start_ahead(sp, sems)
            sp.dma_start(ID[:, :], ident_in).then_inc(consts_in, 16)
            sp.dma_start(VEC[:, :, :, :], vec2).then_inc(consts_in, 16)
            with sp.Fori(0, NPAIR) as b:
                sp.wait_ge(out_free, b + AHEAD)
                for i in range(2):
                    sp.dma_start(X[:, :, i * L:(i + 1) * L], x2T[b * 2 + i]).then_inc(x_in, 16)
                sp.wait_ge(x_used, b + AHEAD)
                for i in range(2):
                    sp.dma_start(CT[:, :, i * L:(i + 1) * L], ctxT[b * 2 + i].rearrange("(k p) c -> p k c", p=P)).then_inc(ct_in, 16)
                with sp.Fori(0, 2) as a:
                    with sp.Fori(0, H2 // 2) as h:
                        for u in range(2):
                            n = (b * 2 + a) * (H2 // 2) + h
                            sp.wait_ge(pack_used, n * 2 + u + AHEAD)
                            sp.dma_start(PK[:, u, :], packs[a * H2 + h * 2 + u]).then_inc(pack_in[u], 16)

        @block.gpsimd
        def _(pool):
            pool.memset(MEANW[:, :], 1.0 / E)
            pool.memset(ONES[:, :], 1.0)
            pool.memset(EPS[:, :], LN_EPS).then_inc(memset_done, 1)
            with pool.Fori(0, NPAIR) as b:
                def down(n, layer):
                    for d in range(EC):
                        pool.wait_ge(down_ps, n * EC + max(d - 1, 0) + AHEAD)
                        pool.sem_inc(passed, 1)
                        pool.dma_start(WD[:, d % 2], downs[layer * EC + d]).then_inc(down_in[d % 2], 16)

                with pool.Fori(0, 2) as a:
                    down(b * 3 + a, a)
                with pool.Fori(0, FC2 // 2) as f:
                    for u in range(2):
                        pool.wait_ge(fc_used, b * FC2 + f * 2 + u + AHEAD)
                        pool.sem_inc(passed, 1)
                        pool.dma_start(W1[:, u, :], fc1[f * 2 + u]).then_inc(fc_in[u], 16)
                down(b * 3 + 2, 2)
                pool.wait_ge(x_ready, (b * 3 + 3) * EC + AHEAD)
                pool.sem_inc(passed, 1)
                for i in range(2):
                    pool.dma_start(x3T[b * 2 + i], X[:, :, i * L:(i + 1) * L]).then_inc(out_stored, 16)
                pool.wait_ge(out_stored, (b + 1) * 32)
                pool.sem_inc(out_free, 1)
        @block.tensor
        def _(pe):
            pe.wait_ge(consts_in, 32 + AHEAD)
            pe.wait_ge(memset_done, 1 + AHEAD)
            def norm(n):
                pe.wait_ge(ln_in, n + 1 + AHEAD)
                for k in range(EC):
                    mm = pe.matmul(ps[:, BQ, :], MEANW[:, :], X[:, k, :], start=(k == 0), stop=(k == EC - 1))
                mm.then_inc(mean_ps, 1)
                pe.wait_ge(sq_ready, n + 1 + AHEAD)
                for k in range(EC):
                    mm = pe.matmul(ps[:, BK, :], MEANW[:, :], SQ[:, k, :], start=(k == 0), stop=(k == EC - 1))
                mm.then_inc(var_ps, 1)

            def down(n):
                for d in range(EC):
                    pe.wait_ge(down_in[d % 2], (n * 2 + d // 2 + 1) * 16)
                    pe.wait_ge(x_ready, n * EC + max(d - 1, 0) + AHEAD)
                    for h in range(H2):
                        mm = pe.matmul(ps[:, BV + d % 2, :], WD[:, d % 2, h, :], G[:, h, :], start=(h == 0), stop=(h == H2 - 1))
                    mm.then_inc(down_ps, 1)

            with pe.Fori(0, NPAIR) as b:
                with pe.Fori(0, 2) as a:
                    norm(b * 3 + a)
                    pe.wait_ge(ct_in, (b + 1) * 32 + AHEAD)
                    pe.sem_inc(passed, 1)
                    pe.wait_ge(h_ready, b * 3 + a + 1 + AHEAD)
                    pe.sem_inc(passed, 1)
                    with pe.Fori(0, H2 // 2) as h:
                        for u in range(2):
                            n = ((b * 2 + a) * (H2 // 2) + h) * 2 + u
                            pe.wait_ge(pack_in[u], ((b * 2 + a) * (H2 // 2) + h + 1) * 16 + AHEAD)
                            pe.wait_ge(q_ready, n + AHEAD)
                            for k in range(EC):
                                mm = pe.matmul(ps[:, BQ, :], weights(u, 0)[:, k, :], H[:, k, :], start=(k == 0), stop=(k == EC - 1))
                            mm.then_inc(q_ps, 1)
                            pe.wait_ge(k_ready, n + AHEAD)
                            for k in range(EC):
                                mm = pe.matmul(ps[:, BK, :], weights(u, 1)[:, k, :], CT[:, k, :], start=(k == 0), stop=(k == EC - 1))
                            mm.then_inc(k_ps, 1)
                            pe.wait_ge(v_ready, n + AHEAD)
                            for t in range(4):
                                for k in range(EC):
                                    pe.matmul(ps[:, BV, t * P:(t + 1) * P], CT[:, k, t * P:(t + 1) * P], weights(u, 2)[:, k, :],
                                              start=(k == 0), stop=False, skip_group_check=True)
                                mm = pe.matmul(ps[:, BV, t * P:(t + 1) * P], ONES[:, :], row(u, 0), start=False, stop=True, skip_group_check=True)
                            mm.then_inc(v_ps, 1)
                            pe.wait_ge(q_ready, n + 1 + AHEAD)
                            pe.wait_ge(k_ready, n + 1 + AHEAD)
                            for i in range(4):
                                pe.wait_ge(exp_ready, n * 4 + max(i - 1, 0) + AHEAD)
                                pe.matmul(ps[:, BS + i % 2, 0:L + 1], QT[:, u, i * P:(i + 1) * P], KT[:, u, i // 2, :], start=True, stop=True)\
                                  .then_inc(s_ps, 1)
                            pe.wait_ge(v_ready, n + 1 + AHEAD)
                            for i in range(2):
                                pe.wait_ge(p_ready, n * 4 + 2 * i + 2 + AHEAD)
                                pe.wait_ge(t_ready, n * 2 + i + AHEAD)
                                for t in range(2):
                                    for q in range(2):
                                        mm = pe.transpose(ps[:, BT, t * L + q * P:t * L + (q + 1) * P], PR[:, 2 * i + q, t * P:(t + 1) * P], ID[:, :])
                                mm.then_inc(t_ps, 1)
                                if i == 0:
                                    pe.wait_ge(tb_ready, n + AHEAD)
                                for q in range(2):
                                    mm = pe.transpose(ps[0:1, BT + 1, i * L + q * P:i * L + (q + 1) * P], PR[:, 2 * i + q, L:L + 1], ID[:, :])
                            mm.then_inc(tb_ps, 1)
                            pe.wait_ge(c_ready, n + AHEAD)
                            pe.wait_ge(tb_ready, n + 1 + AHEAD)
                            for i in range(2):
                                pe.wait_ge(t_ready, n * 2 + i + 1 + AHEAD)
                                for t in range(2):
                                    pe.matmul(ps[:, BC, i * L:(i + 1) * L], V[:, u, 2 * i + t, :], PT[:, i, t, :], start=(t == 0), stop=False, skip_group_check=True)
                                mm = pe.matmul(ps[:, BC, i * L:(i + 1) * L], row(u, 1), PTB[:, i * L:(i + 1) * L], start=False, stop=True, skip_group_check=True)
                            mm.then_inc(c_ps, 1)
                    pe.wait_ge(c_ready, (b * 2 + a + 1) * H2 + AHEAD)
                    down(b * 3 + a)
                norm(b * 3 + 2)
                pe.wait_ge(h_ready, b * 3 + 3 + AHEAD)
                pe.sem_inc(passed, 1)
                with pe.Fori(0, FC2 // 2) as f:
                    for u in range(2):
                        n = b * FC2 + f * 2 + u
                        pe.wait_ge(fc_in[u], (b * (FC2 // 2) + f + 1) * 16)
                        pe.wait_ge(fc_used, n + AHEAD)
                        for k in range(EC):
                            mm = pe.matmul(ps[:, BT + u, :], W1[:, u, k * P:(k + 1) * P], H[:, k, :], start=(k == 0), stop=(k == EC - 1))
                        mm.then_inc(fc_ps, 1)
                pe.wait_ge(fc_ready, (b + 1) * FC2 + AHEAD)
                down(b * 3 + 2)

        @block.scalar
        def _(act):
            act.sem_inc(fc_used, 1)
            act.wait_ge(memset_done, 1 + AHEAD)
            def norm(n):
                act.wait_ge(xc_ready, n + 1 + AHEAD)
                act.activation(SQ[:, :, :], H[:, :, :], ACT.Square).then_inc(sq_ready, 1)
                act.wait_ge(var_ps, n + 1 + AHEAD)
                act.activation(SD[:, :], ps[:, BK, :], ACT.Sqrt, bias=EPS[:, 0:1]).then_inc(sd_ready, 1)

            with act.Fori(0, NPAIR) as b:
                with act.Fori(0, 2) as a:
                    norm(b * 3 + a)
                    with act.Fori(0, H2 // 2) as h:
                        for u in range(2):
                            n = ((b * 2 + a) * (H2 // 2) + h) * 2 + u
                            act.wait_ge(pack_in[u], ((b * 2 + a) * (H2 // 2) + h + 1) * 16 + AHEAD)
                            act.wait_ge(k_ps, n + 1 + AHEAD)
                            act.activation(KT[:, u, :, 0:L], ps[:, BK, :].rearrange("p (i t) -> p i t", i=2), ACT.Identity, bias=column(u, 1))
                            act.activation(KT[:, u, :, L:], column(u, 2).unsqueeze(1).broadcast_to([P, 2, 1]), ACT.Copy)\
                               .then_inc(k_ready, 1)
                            act.wait_ge(v_ps, n + 1 + AHEAD)
                            act.activation(V[:, u, :, :], ps[:, BV, :].rearrange("p (t m) -> p t m", t=4), ACT.Copy).then_inc(v_ready, 1)
                            for i in range(4):
                                act.wait_ge(max_ready, n * 4 + i + 1 + AHEAD)
                                act.wait_ge(tb_ps, n + AHEAD)
                                act.activation(PR[:, i, :], ps[:, BS + i % 2, 0:L + 1], ACT.Exp, bias=NM[:, i:i + 1], accum_out=RS[:, i:i + 1])\
                                   .then_inc(exp_ready, 1)
                            act.wait_ge(c_ps, n + 1 + AHEAD)
                            act.sem_inc(passed, 1)
                            act.activation(G[:, h * 2 + u, :], ps[:, BC, :], ACT.Copy).then_inc(c_ready, 1)
                norm(b * 3 + 2)
                with act.Fori(0, FC2 // 2) as f:
                    for u in range(2):
                        n = b * FC2 + f * 2 + u
                        act.wait_ge(fc_in[u], (b * (FC2 // 2) + f + 1) * 16)
                        act.wait_ge(fc_ps, n + 1 + AHEAD)
                        act.sem_inc(passed, 1)
                        act.activation(G[:, f * 2 + u, :], ps[:, BT + u, :], ACT.Gelu, bias=W1[:, u, EC * P:]).then_inc(fc_ready, 1)
                        act.drain().then_inc(fc_used, 1)

        @block.vector
        def _(dve):
            dve.sem_inc(pack_used, 1)
            dve.wait_ge(consts_in, 32 + AHEAD)
            def norm(n, v):
                dve.wait_ge(mean_ps, n + 1 + AHEAD)
                dve.tensor_tensor(H[:, :, :], X[:, :, :], ps[:, BQ:BQ + 1, :].broadcast_to([P, EC, N2]), ALU.subtract).then_inc(xc_ready, 1)
                dve.wait_ge(sd_ready, n + 1 + AHEAD)
                dve.reciprocal(SD[:, :], SD[:, :])
                dve.drain()
                dve.tensor_tensor(H[:, :, :], H[:, :, :], SD[:, :].unsqueeze(1).broadcast_to([P, EC, N2]), ALU.mult)
                dve.drain()
                for o in range(EC):
                    mm = dve.tensor_scalar(H[:, o, :], H[:, o, :], VEC[:, v, V2_NW, o:o + 1], VEC[:, v, V2_NB, o:o + 1], ALU.mult, ALU.add)
                dve.drain().then_inc(h_ready, 1)

            def down(n, v):
                for d in range(EC):
                    dve.wait_ge(down_ps, n * EC + d + 1 + AHEAD)
                    dve.scalar_tensor_tensor(X[:, d, :], ps[:, BV + d % 2, :], VEC[:, v, V2_BO, d:d + 1], X[:, d, :], ALU.add, ALU.add)\
                       .then_inc(x_ready, 1)

            with dve.Fori(0, NPAIR) as b:
                dve.wait_ge(x_in, (b + 1) * 32 + AHEAD)
                dve.sem_inc(ln_in, 1)
                with dve.Fori(0, 2) as a:
                    norm(b * 3 + a, a)
                    with dve.Fori(0, H2 // 2) as h:
                        for u in range(2):
                            n = ((b * 2 + a) * (H2 // 2) + h) * 2 + u
                            dve.wait_ge(q_ps, n + 1 + AHEAD)
                            dve.tensor_scalar(QT[:, u, :], ps[:, BQ, :], column(u, 0), float(K2) ** -0.5, ALU.add, ALU.mult).then_inc(q_ready, 1)
                            for i in range(4):
                                dve.wait_ge(s_ps, n * 4 + i + 1 + AHEAD)
                                dve.tensor_reduce(NM[:, i:i + 1], ps[:, BS + i % 2, 0:L + 1], AX.X, ALU.max, negate=True).then_inc(max_ready, 1)
                            for i in range(4):
                                dve.wait_ge(exp_ready, n * 4 + i + 1 + AHEAD)
                                dve.reciprocal(RS[:, i:i + 1], RS[:, i:i + 1])
                                dve.drain()
                                dve.tensor_scalar(PR[:, i, :], PR[:, i, :], RS[:, i:i + 1], None, ALU.mult).then_inc(p_ready, 1)
                            for i in range(2):
                                dve.wait_ge(t_ps, n * 2 + i + 1 + AHEAD)
                                dve.wait_ge(c_ps, n + AHEAD)
                                dve.tensor_copy(PT[:, i, :, :], ps[:, BT, :].rearrange("p (t q) -> p t q", t=2)).then_inc(t_ready, 1)
                            dve.wait_ge(tb_ps, n + 1 + AHEAD)
                            dve.tensor_copy(PTB[:, :], ps[0:1, BT + 1, :]).then_inc(tb_ready, 1)
                            dve.wait_ge(c_ps, n + 1 + AHEAD)
                            dve.sem_inc(pack_used, 1)
                    down(b * 3 + a, a)
                    dve.drain().then_inc(ln_in, 1)
                norm(b * 3 + 2, 2)
                down(b * 3 + 2, 2)
                dve.drain().then_inc(x_used, 1)

CI = 128
(V3_TB, V3_WB, V3_GAMMA, V3_BETA, V3_MEAN, V3_VAR) = (0, 1, 3, 5, 7, 9)
NV3 = 11


def layer3(nc, x3T, ctx, theta_w, pg_w, pg_b, w_w, vec3, ident_in, out):
    with ExitStack() as stack:
        def sb(name, shape, dt=F32):
            return stack.enter_context(nc.sbuf_tensor("d_" + name, shape, dt))

        sems = []

        def sem(name):
            sems.append(stack.enter_context(nc.semaphore("d_" + name)))
            return sems[-1]

        WT = sb("wt", [P, LC, CI])
        WPG = sb("wpg", [P, LC, 2 * CI])
        BPG = sb("bpg", [1, 2 * CI])
        WW = sb("ww", [P, L])
        VEC = sb("vec", [P, NV3])
        ID = sb("id", [P, P])
        ONES = sb("ones", [1, P])
        EPS = sb("eps", [P, 1])
        BN = sb("bn", [P, 2, 2])
        XT = sb("xt", [P, EC, L])
        C = sb("c", [P, LC, E])
        X = sb("x", [P, LC, E])
        PG = sb("pg", [P, EC, 2 * CI])
        M = sb("m", [P, CI])
        TH = sb("th", [P, E])
        Y = sb("y", [P, E])
        O = sb("o", [P, LC, E])
        ps = stack.enter_context(nc.psum_tensor("d_ps", [P, 8, 512], F32))
        names = "consts_in memset_done bn_sqrt bn_in x_in in_used x_ps x_ready pg_ps pg_ready m_ps m_ready th_ps th_ready y_ps y_ready o_ps o_read out_ready out_stored".split()
        (consts_in, memset_done, bn_sqrt, bn_in, x_in, in_used, x_ps, x_ready, pg_ps, pg_ready, m_ps, m_ready, th_ps, th_ready,
         y_ps, y_ready, o_ps, o_read, out_ready, out_stored) = [sem(n) for n in names]
        block = stack.enter_context(nc.Block())

        @block.sync
        def _(sp):
            start_ahead(sp, sems)
            for dst, src in ((WT[:, :, :], theta_w), (WPG[:, :, :], pg_w), (BPG[:, :], pg_b), (WW[:, :], w_w), (VEC[:, :], vec3), (ID[:, :], ident_in)):
                sp.dma_start(dst, src).then_inc(consts_in, 16)
            with sp.Fori(0, B) as b:
                sp.wait_ge(in_used, b + AHEAD)
                sp.dma_start(XT[:, :, :], x3T[b]).then_inc(x_in, 16)
                sp.dma_start(C[:, :, :], ctx[b].rearrange("(k p) t -> p k t", p=P)).then_inc(x_in, 16)
                sp.wait_ge(out_ready, b + 1 + AHEAD)
                sp.dma_start(out[b].rearrange("(k p) t -> p k t", p=P), O[:, :, :]).then_inc(out_stored, 16)
            sp.wait_ge(out_stored, 16 * B + AHEAD)
        @block.gpsimd
        def _(pool):
            pool.memset(ONES[:, :], 1.0)
            pool.memset(EPS[:, :], LN_EPS).then_inc(memset_done, 1)

        @block.tensor
        def _(pe):
            pe.wait_ge(consts_in, 96 + AHEAD)
            pe.wait_ge(memset_done, 1 + AHEAD)
            with pe.Fori(0, B) as b:
                pe.wait_ge(x_in, (b + 1) * 32 + AHEAD)
                pe.wait_ge(o_read, b + AHEAD)
                for c in range(LC):
                    for k in range(EC):
                        mm = pe.transpose(ps[:, c, k * P:(k + 1) * P], XT[:, k, c * P:(c + 1) * P], ID[:, :])
                mm.then_inc(x_ps, 1)
                for m in range(EC):
                    for k in range(LC):
                        pe.matmul(ps[:, 2 + m // 2, (m % 2) * L:(m % 2 + 1) * L], C[:, k, m * P:(m + 1) * P], WPG[:, k, :],
                                  start=(k == 0), stop=False, skip_group_check=True)
                    mm = pe.matmul(ps[:, 2 + m // 2, (m % 2) * L:(m % 2 + 1) * L], ONES[:, :], BPG[:, :], start=False, stop=True,
                                   skip_group_check=True)
                mm.then_inc(pg_ps, 1)
                pe.wait_ge(x_ready, b + 1 + AHEAD)
                for k in range(LC):
                    mm = pe.matmul(ps[:, 5, :], WT[:, k, :], X[:, k, :], start=(k == 0), stop=(k == LC - 1))
                mm.then_inc(th_ps, 1)
                pe.wait_ge(pg_ready, b + 1 + AHEAD)
                for m in range(EC):
                    mm = pe.matmul(ps[:, 4, 0:CI], PG[:, m, 0:CI], PG[:, m, CI:], start=(m == 0), stop=(m == EC - 1))
                mm.then_inc(m_ps, 1)
                pe.wait_ge(m_ready, b + 1 + AHEAD)
                pe.wait_ge(th_ready, b + 1 + AHEAD)
                pe.matmul(ps[:, 6, :], M[:, :], TH[:, :], start=True, stop=True).then_inc(y_ps, 1)
                pe.wait_ge(y_ready, b + 1 + AHEAD)
                for c in range(LC):
                    mm = pe.matmul(ps[:, 2 + c, :], WW[:, c * P:(c + 1) * P], Y[:, :], start=True, stop=True)
                mm.then_inc(o_ps, 1)

        @block.scalar
        def _(act):
            act.wait_ge(memset_done, 1 + AHEAD)
            act.wait_ge(consts_in, 96 + AHEAD)
            act.activation(BN[:, 0, :], VEC[:, V3_VAR:V3_VAR + 2], ACT.Sqrt, bias=EPS[:, 0:1]).then_inc(bn_sqrt, 1)
            with act.Fori(0, B) as b:
                act.wait_ge(pg_ps, b + 1 + AHEAD)
                act.activation(PG[:, :, :], ps[:, 2:4, :].rearrange("p a (c t) -> p (a c) t", c=2), ACT.Copy).then_inc(pg_ready, 1)
                act.wait_ge(th_ps, b + 1 + AHEAD)
                act.activation(TH[:, :], ps[:, 5, :], ACT.Identity, bias=VEC[:, V3_TB:V3_TB + 1]).then_inc(th_ready, 1)
                act.wait_ge(y_ps, b + 1 + AHEAD)
                act.activation(Y[:, :], ps[:, 6, :], ACT.Copy).then_inc(y_ready, 1)

        @block.vector
        def _(dve):
            dve.wait_ge(bn_sqrt, 1 + AHEAD)
            dve.reciprocal(BN[:, 0, :], BN[:, 0, :])
            dve.tensor_tensor(BN[:, 1, :], VEC[:, V3_WB:V3_WB + 2], VEC[:, V3_MEAN:V3_MEAN + 2], ALU.subtract)
            dve.drain()
            dve.tensor_tensor(BN[:, 0, :], BN[:, 0, :], VEC[:, V3_GAMMA:V3_GAMMA + 2], ALU.mult)
            dve.drain()
            dve.tensor_tensor(BN[:, 1, :], BN[:, 1, :], BN[:, 0, :], ALU.mult)
            dve.drain()
            dve.tensor_tensor(BN[:, 1, :], BN[:, 1, :], VEC[:, V3_BETA:V3_BETA + 2], ALU.add)
            with dve.Fori(0, B) as b:
                dve.wait_ge(x_ps, b + 1 + AHEAD)
                dve.tensor_copy(X[:, :, :], ps[:, 0:2, :]).then_inc(x_ready, 1)
                dve.wait_ge(m_ps, b + 1 + AHEAD)
                dve.tensor_scalar(M[:, :], ps[:, 4, 0:CI], 1.0 / E, None, ALU.mult).then_inc(m_ready, 1)
                dve.wait_ge(o_ps, b + 1 + AHEAD)
                dve.wait_ge(out_stored, b * 16 + AHEAD)
                for c in range(LC):
                    dve.tensor_scalar(O[:, c, :], ps[:, 2 + c, :], BN[:, 0, c:c + 1], BN[:, 1, c:c + 1], ALU.mult, ALU.add)
                dve.drain().then_inc(o_read, 1)
                dve.tensor_tensor(O[:, :, :], O[:, :, :], X[:, :, :], ALU.add).then_inc(out_ready, 1)
                dve.drain().then_inc(in_used, 1)


def _l0(I):
    import numpy as np
    f=np.ascontiguousarray
    def pad(W):
        z=np.zeros((4,4,32,256),np.float32); z[:,:,:16,:]=W.reshape(4,4,16,256)
        return z.reshape(4,128,2,128).transpose(3,0,2,1)
    def padb(b):
        z=np.zeros((4,4,32),np.float32); z[:,:,:16]=b.reshape(4,4,16); return z.reshape(4,128).T
    wqk=f(np.stack([pad(I['L0_xattn_Wq']),pad(I['L0_xattn_Wk'])],axis=3))
    qkb=f(np.stack([padb(I['L0_xattn_bq']),padb(I['L0_xattn_bk'])],axis=1))
    aug=np.zeros((4,32,2,4),np.float32); aug[:,16,0]=4.0; aug[:,17,1]=1.0
    ms=np.zeros((128,4,32),np.float32); ms[0,:,16]=1.0
    wv=f(I['L0_xattn_Wv'].T.reshape(2,128,256).transpose(1,0,2))
    m=I['mask_Bx1x2048_bf1'].view(np.uint8)
    return dict(x=I['x'],xT=f(I['x'].transpose(0,2,1)),ctx=I['ctx_2048'],mask_row=f(np.broadcast_to(m,(8,128,512))),mask_col=f(m.reshape(8,4,128).transpose(0,2,1)),
      wqk=wqk,qkb=qkb,aug=aug.reshape(128,2,4),wv=wv,bv=f(np.broadcast_to(I['L0_xattn_bv'],(128,256))),mask_sel=ms.reshape(128,128),ident_in=np.eye(128,dtype=np.float32))


def _l1(I):
    import numpy as np
    f=np.ascontiguousarray
    c=I['ctx_2048']
    s0=f(c[:,2:18].reshape(8,4,128,16).transpose(0,2,1,3))
    n=lambda k:I['L1_xattn_'+k].reshape(-1,512)
    v=np.concatenate([n('ln1_w'),n('ln1_b'),n('ln2_w'),n('ln2_b'),n('maa_x'),n('maa_stack'),n('time_decay'),n('u'),n('gn_w'),n('gn_b'),n('ffn_maa_k'),n('ffn_maa_r')])
    vecs=f(v.reshape(16,4,128).transpose(2,0,1))
    w8=f(np.stack([I['L1_xattn_'+k].T.reshape(4,128,512).transpose(1,0,2) for k in ('Wk','Wv','Wr','Wg','Wo','Wfk','Wfr','Wfv')],axis=1))
    sel=np.zeros((8,16,16,8,16),np.float32)
    for h in range(8):
        for j in range(16): sel[h,j,j,h,:]=1
    sel=sel.reshape(128,16,128)
    blk=np.kron(np.eye(8,dtype=np.float32),np.ones((16,16),np.float32))
    return dict(ctxT=f(c.transpose(0,2,1)),s0=s0,vecs=vecs,w8=w8,maa_w1=f(I['L1_xattn_maa_w1'].reshape(4,128,160).transpose(1,0,2)),
      maa_w2=I['L1_xattn_maa_w2'].reshape(160,512),td_w1=f(I['L1_xattn_td_w1'].reshape(4,128,64).transpose(1,0,2)),td_w2=I['L1_xattn_td_w2'],
      sel=sel,selT=f(sel.transpose(2,1,0)),blk=f(np.stack([blk,blk/16])))


def _l2(I):
    import numpy as np
    f=np.ascontiguousarray; g=lambda k:I['L2_xattn_'+k]
    def hd(W): return W.reshape(4,128,16,128).transpose(2,1,0,3).reshape(16,128,512)
    packs=[];downs=[]
    for i in '12':
        z=np.zeros((16,128,3+256),np.float32)
        z[:,:,0]=g('bq'+i).reshape(16,128); z[:,:,1]=g('bk'+i).reshape(16,128); z[:,:,2]=g('bias_k'+i).reshape(16,128)
        z[:,0,3:131]=g('bv'+i).reshape(16,128); z[:,0,131:]=g('bias_v'+i).reshape(16,128)
        packs.append(np.concatenate([hd(g('wq'+i)),hd(g('wk'+i)),hd(g('wv'+i)),z],axis=2))
    for W in (g('wo1'),g('wo2'),g('w_fc2')):
        downs.append(W.reshape(16,128,4,128).transpose(2,1,0,3))
    fc1=np.concatenate([hd(g('w_fc1')),g('b_fc1').reshape(16,128,1)],axis=2)
    v=np.stack([np.stack([g('ln1_scale'),g('ln1_offset'),g('bo1')]),np.stack([g('ln2_scale'),g('ln2_offset'),g('bo2')]),np.stack([g('ln_mlp_scale'),g('ln_mlp_offset'),g('b_fc2')])])
    return dict(packs=f(np.concatenate(packs)),downs=f(np.concatenate(downs)),fc1=f(fc1),vec2=f(v.reshape(3,3,4,128).transpose(3,0,1,2)),ident_in=np.eye(128,dtype=np.float32))


def _l3(I):
    import numpy as np
    f=np.ascontiguousarray; g=lambda k:I['L3_xattn_'+k]
    def ci(W): return W.reshape(128,2,128).transpose(2,1,0)
    v=np.concatenate([g('theta_b').reshape(1,128)]+[g(k).reshape(2,128) for k in ('w_b','bn_gamma','bn_beta','bn_mean','bn_var')]).T
    return dict(theta_w=f(ci(g('theta_w'))),pg_w=f(np.concatenate([ci(g('phi_w')),ci(g('g_w'))],axis=2)),pg_b=np.concatenate([g('phi_b'),g('g_b')]).reshape(1,256),w_w=f(g('w_w').T),vec3=f(v),ident_in=np.eye(128,dtype=np.float32),ctx=I['ctx_2048'])


def build(nc, io, out):
    def scratch(name):
        return nc.dram_tensor(name, [B, P, EC, L], F32).ap()

    x1T, x2T, x3T = scratch("x1T"), scratch("x2T"), scratch("x3T")
    layer0(nc, x=io["x"], xT=io["xT"], ctx=io["ctx"], mask_row=io["mask_row"], mask_col=io["mask_col"], wqk=io["wqk"], qkb=io["qkb"],
           aug=io["aug"], wv=io["wv"], bv=io["bv"], mask_sel=io["mask_sel"], ident_in=io["ident_in"], x1T=x1T)
    layer1(nc, x1T=x1T, ctxT=io["ctxT"], s0=io["s0"], vecs=io["vecs"], w8=io["w8"], maa_w1=io["maa_w1"], maa_w2=io["maa_w2"],
           td_w1=io["td_w1"], td_w2=io["td_w2"], sel=io["sel"], selT=io["selT"], blk=io["blk"], x2T=x2T)
    layer2(nc, x2T=x2T, ctxT=io["ctxT"], packs=io["packs"], downs=io["downs"], fc1=io["fc1"], vec2=io["vec2"],
           ident_in=io["ident_in"], x3T=x3T)
    layer3(nc, x3T=x3T, ctx=io["ctx"], theta_w=io["theta_w"], pg_w=io["pg_w"], pg_b=io["pg_b"], w_w=io["w_w"], vec3=io["vec3"],
           ident_in=io["ident_in"], out=out)


def kernel(**inputs):
    import numpy as np
    import concourse.bacc as bacc
    from concourse.bass_utils import run_bass_kernel_spmd

    I = {k: np.asarray(v) for k, v in inputs.items()}
    arrays = {}
    for part in (_l0(I), _l1(I), _l2(I), _l3(I)):
        arrays.update(part)
    arrays = {k: np.ascontiguousarray(v) for k, v in arrays.items()}
    nc = bacc.Bacc("TRN2", target_bir_lowering=False, num_devices=1)
    io = {k: nc.dram_tensor("in_" + k, a.shape, mybir.dt.from_np(a.dtype), kind="ExternalInput").ap() for k, a in arrays.items()}
    out = nc.dram_tensor("out", (B, L, E), F32, kind="ExternalOutput").ap()
    build(nc, io, out)
    r = run_bass_kernel_spmd(nc, [{"in_" + k: a for k, a in arrays.items()}], core_ids=[0])
    return r.results[0]["out"]
```

```python
from contextlib import ExitStack

import concourse.bass as bass
from concourse import mybir

B, L, E = 8, 256, 512
P = 128
EC = E // P
LC = L // P
LN_EPS = 1e-5

H0, D0 = 16, L // 16
G0 = 4
HG = H0 // G0
CG = HG * D0
ROW_MASK, ROW_MAX = D0, D0 + 1
V2C = 2 * D0
VW = 3 * V2C + 1
MAX_FROM, MAX_RATE = 4, 2
NEG = -1e30

F32 = mybir.dt.float32
U8 = mybir.dt.uint8
F32R = mybir.dt.float32r
F16 = mybir.dt.float16
BF16 = mybir.dt.bfloat16
ALU = mybir.AluOpType
ACT = mybir.ActivationFunctionType
AX = mybir.AxisListType


AHEAD = 128


def start_ahead(eng, semaphores):
    for semaphore in semaphores:
        eng.sem_inc(semaphore, AHEAD)


def layer0(nc, x, xT, ctx, mask_row, mask_col, wqk, qkb, aug, wv, bv, mask_sel, ident_in, x1T):
    with ExitStack() as stack:
        def sb(name, shape, dt=F32):
            return stack.enter_context(nc.sbuf_tensor("a_" + name, shape, dt))

        sems = []

        def sem(name):
            sems.append(nc.alloc_semaphore("a_" + name))
            return sems[-1]

        def dma_sem(name):
            return stack.enter_context(nc.semaphore("a_" + name))

        WH = sb("wh", [P, G0, LC, 2, P], F32R)
        WL = sb("wl", [P, G0, LC, 2, P], F32R)
        WVH = sb("wvh", [P, LC, L], F32R)
        WVL = sb("wvl", [P, LC, L], F32R)
        QKB = sb("qkb", [P, 2, G0])
        AUG = sb("aug", [P, 2, G0])
        BVB = sb("bvb", [P, L])
        MSEL = sb("msel", [P, P])
        MSELR = sb("mselr", [P, P], F32R)
        M8R = sb("m8r", [P, E], U8)
        MBRR = sb("mbrr", [P, E], F32R)
        M8C = sb("m8c", [P, EC], U8)
        MCOL = sb("mcol", [P, EC])
        X = sb("x", [P, LC, E])
        C = sb("ctx", [P, LC, E])
        XH = sb("xh", [P, LC, E], F32R)
        XL = sb("xl", [P, LC, E], F32R)
        CH = sb("ch", [P, LC, E], F32R)
        CL = sb("cl", [P, LC, E], F32R)
        XT = sb("xT", [P, EC, L])
        XM = sb("xm", [P, EC, L])
        XQ = sb("xq", [P, EC, L])
        ID = sb("id", [P, P])
        ONES = sb("ones", [P, P])
        EPS = sb("eps", [P, 1])
        QF = sb("qf", [P, E])
        KF = sb("kf", [P, E])
        QH = sb("qh", [P, 2, E], F32R)
        QL = sb("ql", [P, 2, E], F32R)
        KK = sb("kk", [P, 2, 2, E], F32R)
        QM = sb("qm", [P, HG, E], F32R)
        KM = sb("km", [P, 2, HG, 2, E], F32R)
        NM = sb("nm", [P, 2, HG * EC])
        NMT = sb("nmT", [HG * EC, 2, P], F32R)
        VF = sb("vf", [P, EC, H0, V2C])
        VA = sb("va", [P, EC, H0, VW], BF16)
        EX = sb("ex", [P, 4, E])
        EH = sb("eh", [P, 2, EC, E], F16)
        EL = sb("el", [P, 2, EC, E], F16)
        U = sb("u", [P, 2, EC, HG, V2C])
        DEN = sb("den", [P, 2, EC, HG, 1])
        MEAN = sb("mean", [P, EC, L])
        VAR = sb("var", [P, EC, L])
        MSQ = sb("msq", [P, EC, HG, D0])
        ST = sb("st", [P, 4, L])
        RN = sb("rn", [P, 1])
        OUT = XQ
        WQK = EX[:, :, :].rearrange("p a (b c d) -> p a b c d", b=LC, c=2)
        WV = XQ[:, 0:LC, :]
        ps = stack.enter_context(nc.psum_tensor("a_ps", [P, 8, 512], F32))
        BQ, BK, BM, BT, BO = 0, 1, 2, 4, 6

        consts_in, inputs_in, stats_x_in, memset_done, inputs_read, stats_read = [sem(n) for n in ("consts_in", "inputs_in", "stats_x_in", "memset_done", "inputs_read", "stats_read")]
        xc_high, xc_split, weights_split, stats_in = sem("xc_high"), sem("xc_split"), sem("weights_split"), sem("stats_in")
        q_ps, k_ps, qf_ready, kf_ready, qh_ready, kh_ready, qk_split = [sem(n) for n in ("q_ps", "k_ps", "qf_ready", "kf_ready", "qh_ready", "kh_ready", "qk_split")]
        v_ps, vf_ready, v_square, v_split, st_ps, st_read, sq_ready = [sem(n) for n in ("v_ps", "vf_ready", "v_square", "v_split", "st_ps", "st_read", "sq_ready")]
        qm_in, km_in_even, km_in_odd, m_ps, m_read, nm_ready, nmT_ps, nmT_sb, max_in = [sem(n) for n in ("qm_in", "km_in", "km_in_odd", "m_ps", "m_read", "nm_ready", "nmT_ps", "nmT_sb", "max_in")]
        t_ps, ex_ready, eh_ready, el_dve, el_pool, o_ps, o_read = [sem(n) for n in ("t_ps", "ex_ready", "eh_ready", "el_dve", "el_pool", "o_ps", "o_read")]
        den_ready, u_read, var_x, var_v, std_ready, rstd_ready = [sem(n) for n in ("den_ready", "u_read", "var_x", "var_v", "std_ready", "rstd_ready")]
        out_free, out_stored, passed, out_ready = sem("out_free"), dma_sem("out_stored"), sem("passed"), sem("out_ready")
        km_in = (km_in_even, km_in_odd)
        N_IN, N_STATS, N_HEADS = 3 * 16, 2 * 16, HG * 16
        NS = HG * EC
        NE = NS // 2
        stack.callback(nc.all_engine_barrier)
        stack.callback(lambda: nc.clear_and_free_semaphores(sems))
        block = stack.enter_context(nc.Block())

        def tiles_beside(n):
            first = (n - MAX_FROM) * MAX_RATE
            return range(first, first + MAX_RATE) if 0 <= first < NS else range(0)

        TURN_AT = MAX_FROM + NS // MAX_RATE
        STATS_AT, MOMENTS_AT = 3, 7
        PROJECT_AT = TURN_AT + 2
        WEIGH = ((), (0, 1, 2), (3,), ())

        def after(b, g):
            return (b, g + 1) if g + 1 < G0 else (b + 1, 0)

        @block.sync
        def _(sp):
            start_ahead(sp, sems)

            def load_inputs(b):
                sp.wait_ge(inputs_read, b + AHEAD)
                sp.sem_inc(passed, 1)
                sp.dma_start(X[:, :, :], x[b].rearrange("(k p) t -> p k t", p=P)).then_inc(inputs_in, 16)
                sp.dma_start(C[:, :, :], ctx[b].rearrange("(k p) t -> p k t", p=P)).then_inc(inputs_in, 16)
                sp.dma_start(M8R[:, :], mask_row[b]).then_inc(inputs_in, 16)

            def load_statistics(b):
                sp.wait_ge(stats_read, b + AHEAD)
                sp.sem_inc(passed, 1)
                sp.dma_start(M8C[:, :], mask_col[b]).then_inc(stats_x_in, 16)
                sp.dma_start(XT[:, :, :], xT[b].rearrange("(k p) c -> p k c", p=P)).then_inc(stats_x_in, 16)

            def spread(b, g):
                it, s = b * G0 + g, g % 2
                sp.wait_ge(m_ps, it * NS + AHEAD)
                sp.sem_inc(passed, 1)
                sp.wait_ge(qh_ready, it + 1 + AHEAD)
                for h in range(HG):
                    rows = slice(32 * h, 32 * h + 32)
                    sp.dma_start(QM[rows, h, :].bitcast(F32), QH[rows, s, :].bitcast(F32)).then_inc(qm_in, 16)
                sp.wait_ge(t_ps, (it - 1) * NS + AHEAD)
                sp.sem_inc(passed, 1)
                sp.wait_ge(qk_split, it + 1 + AHEAD)
                for h in range(HG):
                    rows = slice(32 * h, 32 * h + 32)
                    sp.dma_start(KM[rows, s, h, :, :].bitcast(F32), KK[rows, s, :, :].bitcast(F32)).then_inc(km_in[s], 16)
                sp.wait_ge(nmT_sb, it + 1 + AHEAD)
                for h in range(HG):
                    sp.dma_start(QH[32 * h + ROW_MAX:32 * h + ROW_MAX + 1, s, :].bitcast(F32),
                                 NMT[h * EC:(h + 1) * EC, s, :].bitcast(F32)).then_inc(max_in, 16)

            for dst, src in ((WQK, wqk), (WV, wv), (QKB[:, :, :], qkb), (AUG[:, :, :], aug), (BVB[:, :], bv),
                             (MSEL[:, :], mask_sel), (ID[:, :], ident_in)):
                sp.dma_start(dst, src).then_inc(consts_in, 16)
            load_inputs(0)
            sp.wait_ge(memset_done, 1 + AHEAD)
            sp.sem_inc(passed, 1)
            spread(0, 0)
            load_statistics(0)
            spread(0, 1)
            spread(0, 2)
            with sp.Fori(0, B - 1) as b:
                load_inputs(b + 1)
                for g in (2, 3):
                    spread(*after(b, g))
                load_statistics(b + 1)
                for g in (0, 1):
                    spread(*after(b + 1, g))
            spread(B - 1, 3)

        @block.gpsimd
        def _(pool):
            pool.memset(QM[:, :, :].bitcast(F32), 0.0)
            pool.memset(ONES[:, :], 1.0)
            pool.memset(EPS[:, :], LN_EPS)
            pool.memset(VA[:, :, :, 0:1], 1.0)
            pool.memset(KM[:, :, :, :, :].bitcast(F32), 0.0).then_inc(memset_done, 1)

            def group_moments(b, g):
                it, s = b * G0 + g, g % 2
                pool.wait_ge(den_ready, it + 1 + AHEAD)
                pool.sem_inc(passed, 1)
                for c in range(EC):
                    pool.tensor_tensor(U[:, s, c, :, :], U[:, s, c, :, :], DEN[:, s, c, :, :].broadcast_to([P, HG, V2C]), ALU.mult)
                pool.drain()

            def group_moments_2(b, g):
                it, s = b * G0 + g, g % 2
                cols = slice(g * HG * D0, (g + 1) * HG * D0)
                mean = MEAN[:, :, cols].rearrange("p c (h d) -> p c h d", h=HG)
                var = VAR[:, :, cols].rearrange("p c (h d) -> p c h d", h=HG)
                pool.tensor_copy(mean, U[:, s, :, :, 0:D0])
                pool.tensor_tensor(MSQ[:, :, :, :], U[:, s, :, :, 0:D0], U[:, s, :, :, 0:D0], ALU.mult)
                pool.drain()
                pool.tensor_tensor(var, U[:, s, :, :, D0:], MSQ[:, :, :, :], ALU.subtract).then_inc(u_read, 1)
                pool.drain()
                if g == G0 - 1:
                    pool.tensor_scalar(VAR[:, :, :], VAR[:, :, :], 0.0, None, ALU.max).then_inc(var_v, 1)
                    pool.drain()

            def centre(b):
                pool.wait_ge(var_x, b + 1 + AHEAD)
                pool.sem_inc(passed, 1)
                pool.tensor_tensor(XM[:, :, :], XM[:, :, :], ST[:, 0:1, :].broadcast_to([P, EC, L]), ALU.subtract)
                pool.drain()

            def scale(b):
                pool.wait_ge(rstd_ready, b + 1 + AHEAD)
                pool.sem_inc(passed, 1)
                pool.tensor_tensor(XM[:, :, :], XM[:, :, :], ST[:, 3:4, :].broadcast_to([P, EC, L]), ALU.mult)
                pool.drain()

            def spread_out(b):
                pool.tensor_tensor(XM[:, :, :], XM[:, :, :], VAR[:, :, :], ALU.mult)
                pool.drain()

            def shift(b):
                pool.tensor_tensor(XM[:, :, :], XM[:, :, :], MEAN[:, :, :], ALU.add)
                pool.drain()

            def mask_out(b, half):
                for c in range(2 * half, 2 * half + 2):
                    pool.tensor_scalar(OUT[:, c, :], XM[:, c, :], MCOL[:, c:c + 1], None, ALU.mult)
                if half == 0:
                    return
                pool.drain().then_inc(out_ready, 1)
                pool.dma_start(x1T[b], OUT[:, :, :]).then_inc(out_stored, 16)

            def group(b, g, prior):
                it = b * G0 + g
                for h in range(HG):
                    for k in range(1, EC, 2):
                        n = h * EC + k
                        pool.wait_ge(eh_ready, it * NS + n + 1 + AHEAD)
                        pool.sem_inc(passed, 1)
                        pool.tensor_tensor(EL[:, h % 2, k, :], EX[:, n % 4, :], EH[:, h % 2, k, :], ALU.subtract).then_inc(el_pool, 1)
                        beside(b, g, n, prior)

            def beside(b, g, n, prior):
                if g == 0 and prior is not None:
                    if n == 5:
                        group_moments(prior, G0 - 1)
                    if n == 7:
                        group_moments_2(prior, G0 - 1)
                    if n == 13:
                        scale(prior)
                    if n == 15:
                        spread_out(prior)
                if g == 1 and prior is not None:
                    if n == 1:
                        shift(prior)
                    if n == 3:
                        mask_out(prior, 0)
                    if n == 5:
                        mask_out(prior, 1)
                    if n == 15:
                        pool.wait_ge(out_stored, (prior + 1) * 16)
                        pool.sem_inc(out_free, 1)
                if g > 0:
                    if n == 7:
                        group_moments(b, g - 1)
                    if n == 9:
                        group_moments_2(b, g - 1)
                if g == 3 and n == 13:
                    centre(b)

            group(0, 0, None)
            group(0, 1, None)
            with pool.Fori(0, B - 1) as b:
                group(b, 2, None)
                group(b, 3, None)
                group(b + 1, 0, b)
                group(b + 1, 1, b)
            group(B - 1, 2, None)
            group(B - 1, 3, None)
            group_moments(B - 1, G0 - 1)
            group_moments_2(B - 1, G0 - 1)
            scale(B - 1)
            spread_out(B - 1)
            shift(B - 1)
            mask_out(B - 1, 0)
            mask_out(B - 1, 1)
            pool.wait_ge(out_stored, B * 16)

        @block.tensor
        def _(pe):
            pe.wait_ge(memset_done, 1 + AHEAD)
            pe.wait_ge(weights_split, 1 + AHEAD)

            def project_queries(b, g):
                it = b * G0 + g
                if g == 0:
                    pe.wait_ge(xc_split, b + 1 + AHEAD)
                pe.wait_ge(nmT_sb, it + AHEAD)
                for k in range(LC):
                    pe.matmul(ps[:, BQ, :], WH[:, g, k, 0, :], XH[:, k, :], start=(k == 0), stop=False)
                    pe.matmul(ps[:, BQ, :], WH[:, g, k, 0, :], XL[:, k, :], start=False, stop=False)
                    mm = pe.matmul(ps[:, BQ, :], WL[:, g, k, 0, :], XH[:, k, :], start=False, stop=(k == LC - 1))
                mm.then_inc(q_ps, 1)

            def project_keys(b, g):
                pe.wait_ge(kf_ready, b * G0 + g + AHEAD)
                for k in range(LC):
                    pe.matmul(ps[:, BK, :], WH[:, g, k, 1, :], CH[:, k, :], start=(k == 0), stop=False)
                    pe.matmul(ps[:, BK, :], WH[:, g, k, 1, :], CL[:, k, :], start=False, stop=False)
                    pe.matmul(ps[:, BK, :], WL[:, g, k, 1, :], CH[:, k, :], start=False, stop=False)
                pe.matmul(ps[:, BK, :], MSELR[:, :], MBRR[:, :], start=False, stop=True).then_inc(k_ps, 1)

            def values(b):
                pe.wait_ge(eh_ready, b * G0 * NS + AHEAD)
                for c in range(EC):
                    out = ps[:, BT + c // 2, (c % 2) * L:(c % 2 + 1) * L]
                    for k in range(LC):
                        cols = slice(c * P, (c + 1) * P)
                        pe.matmul(out, CH[:, k, cols], WVH[:, k, :], start=(k == 0), stop=False, skip_group_check=True)
                        pe.matmul(out, CH[:, k, cols], WVL[:, k, :], start=False, stop=False, skip_group_check=True)
                        mm = pe.matmul(out, CL[:, k, cols], WVH[:, k, :], start=False, stop=(k == LC - 1), skip_group_check=True)
                mm.then_inc(v_ps, 1)

            def statistics(b, last):
                pe.wait_ge(stats_in, b + 1 + AHEAD)
                pe.wait_ge(sq_ready, b + 1 + AHEAD)
                pe.wait_ge(kf_ready, (b + 1) * G0 + (0 if last else 1) + AHEAD)
                pe.wait_ge(nmT_sb, (b + 1) * G0 + AHEAD)
                for c in range(EC):
                    pe.matmul(ps[:, BK, 0:L], ONES[:, :], XM[:, c, :], start=(c == 0), stop=(c == EC - 1), skip_group_check=True)
                for c in range(EC):
                    pe.matmul(ps[:, BK, L:2 * L], ONES[:, :], XQ[:, c, :], start=(c == 0), stop=(c == EC - 1), skip_group_check=True)
                for c in range(EC):
                    mm = pe.matmul(ps[:, BQ, 0:1], ONES[:, :], MCOL[:, c:c + 1], start=(c == 0), stop=(c == EC - 1))
                mm.then_inc(st_ps, 1)

            def maxima(b, g, n):
                it, s = b * G0 + g, g % 2
                if n == 0:
                    pe.wait_ge(qm_in, (it + 1) * N_HEADS + AHEAD)
                    pe.wait_ge(kh_ready, it + 1 + AHEAD)
                pe.wait_ge(m_read, it * NS + n - 1 + AHEAD)
                h, c = divmod(n, EC)
                pe.matmul(ps[:, BM + n % 2, :], QM[:, h, c * P:(c + 1) * P], KK[:, s, 0, :], start=True, stop=True).then_inc(m_ps, 1)

            def turn_maxima(b, g):
                it, s = b * G0 + g, g % 2
                pe.wait_ge(nm_ready, it + 1 + AHEAD)
                pe.wait_ge(qf_ready, it + 1 + AHEAD)
                if g == 0:
                    pe.wait_ge(st_read, b + AHEAD)
                pe.transpose(ps[0:NS, BQ, 128:128 + P], NM[:, s, :], ID[:, :]).then_inc(nmT_ps, 1)

            def scores(b, g, n):
                it, s = b * G0 + g, g % 2
                h, k = divmod(n, EC)
                if n == 0:
                    pe.wait_ge(max_in, (it + 1) * N_HEADS + AHEAD)
                    pe.wait_ge(km_in[s], (b * (G0 // 2) + g // 2 + 1) * N_HEADS + AHEAD)
                pe.wait_ge(eh_ready, it * NS + n - 1 + AHEAD)
                if g == 0 and n == 0:
                    pe.wait_ge(vf_ready, b + 1 + AHEAD)
                cols = slice(k * P, (k + 1) * P)
                pe.matmul(ps[:, BT + n % 2, :], KM[:, s, h, 0, cols], QH[:, s, :], start=True, stop=False)
                pe.matmul(ps[:, BT + n % 2, :], KM[:, s, h, 0, cols], QL[:, s, :], start=False, stop=False)
                pe.matmul(ps[:, BT + n % 2, :], KM[:, s, h, 1, cols], QH[:, s, :], start=False, stop=True).then_inc(t_ps, 1)

            def weighted(b, g, h, q):
                it = b * G0 + g
                if q == 0:
                    if h == 0:
                        pe.wait_ge(v_split, b * G0 + g + 1 + AHEAD)
                    pe.wait_ge(o_read, it * HG + h - 1 + AHEAD)
                    pe.wait_ge(el_dve, it * NE + (h + 1) * EC // 2 + AHEAD)
                    pe.wait_ge(el_pool, it * NE + (h + 1) * EC // 2 + AHEAD)
                for k in range(EC):
                    out = ps[:, BO + h % 2, q * VW:(q + 1) * VW]
                    cols = slice(q * P, (q + 1) * P)
                    pe.matmul(out, EH[:, h % 2, k, cols], VA[:, k, g * HG + h, :], start=(k == 0), stop=False, skip_group_check=True)
                    mm = pe.matmul(out[:, 0:VW - V2C], EL[:, h % 2, k, cols], VA[:, k, g * HG + h, 0:VW - V2C], start=False,
                                   stop=(k == EC - 1), skip_group_check=True)
                if q == EC - 1:
                    mm.then_inc(o_ps, 1)

            def group(b, g, left=2):
                for n in range(NS):
                    h, k = divmod(n, EC)
                    scores(b, g, n)
                    if left:
                        for m in tiles_beside(n):
                            maxima(*after(b, g), m)
                        if n == TURN_AT:
                            turn_maxima(*after(b, g))
                    if g == G0 - 1 and n == STATS_AT:
                        statistics(b, left == 0)
                    if left > 1 and n == PROJECT_AT:
                        project_queries(*after(*after(b, g)))
                    if left > 1 and n == PROJECT_AT + 1:
                        project_keys(*after(*after(b, g)))
                    for q in WEIGH[k]:
                        if h == 0:
                            previous(b, g, q)
                        else:
                            weighted(b, g, h - 1, q)

            def previous(b, g, q):
                if g == 0 and b is FIRST:
                    return
                if g > 0:
                    weighted(b, g - 1, HG - 1, q)
                else:
                    weighted(b - 1, G0 - 1, HG - 1, q)

            FIRST = 0
            project_queries(0, 0)
            project_keys(0, 0)
            values(0)
            for n in range(NS):
                maxima(0, 0, n)
            turn_maxima(0, 0)
            project_queries(0, 1)
            project_keys(0, 1)
            group(0, 0)
            group(0, 1)
            with pe.Fori(0, B - 1) as b:
                group(b, 2)
                group(b, 3)
                values(b + 1)
                group(b + 1, 0)
                group(b + 1, 1)
            group(B - 1, 2, left=1)
            group(B - 1, 3, left=0)
            for q in range(EC):
                weighted(B - 1, G0 - 1, HG - 1, q)

        @block.scalar
        def _(act):
            act.wait_ge(memset_done, 1 + AHEAD)

            def queries(b, g):
                it = b * G0 + g
                act.wait_ge(q_ps, it + 1 + AHEAD)
                act.wait_ge(qk_split, it + AHEAD)
                act.activation(QF[:, :], ps[:, BQ, :], ACT.Identity, bias=QKB[:, 0, g:g + 1], scale=float(D0) ** -0.5).then_inc(qf_ready, 1)

            def keys(b, g):
                it = b * G0 + g
                act.wait_ge(k_ps, it + 1 + AHEAD)
                act.activation(KF[:, :], ps[:, BK, :], ACT.Identity, bias=QKB[:, 1, g:g + 1]).then_inc(kf_ready, 1)

            def cut(b):
                act.wait_ge(inputs_in, (b + 1) * N_IN + AHEAD)
                act.wait_ge(k_ps, b * G0 + AHEAD)
                act.wait_ge(v_ps, b + AHEAD)
                act.activation(XH[:, :, :], X[:, :, :], ACT.Copy)
                act.activation(CH[:, :, :], C[:, :, :], ACT.Copy).then_inc(xc_high, 1)

            def square_values(b, g):
                heads = slice(g * HG, (g + 1) * HG)
                act.wait_ge(vf_ready, b + 1 + AHEAD)
                act.activation(VF[:, :, heads, D0:], VF[:, :, heads, 0:D0], ACT.Square)
                act.drain()
                act.wait_ge(o_ps, (b * G0 + g - 3) * HG + AHEAD)
                act.activation(VA[:, :, heads, 1:1 + V2C], VF[:, :, heads, :], ACT.Copy).then_inc(v_square, 1)

            def group(b, g, left=2, prior=None):
                it = b * G0 + g
                for h in range(HG):
                    for k in range(EC):
                        n = h * EC + k
                        act.wait_ge(t_ps, it * NS + n + 1 + AHEAD)
                        if k == 0:
                            act.wait_ge(o_ps, it * HG + h - 1 + AHEAD)
                        act.wait_ge(el_pool if k % 2 else el_dve, it * NE + n // 2 - 1 + AHEAD)
                        act.activation(EX[:, n % 4, :], ps[:, BT + n % 2, :], ACT.Exp).then_inc(ex_ready, 1)
                        act.activation(EH[:, h % 2, k, :], ps[:, BT + n % 2, :], ACT.Exp).then_inc(eh_ready, 1)
                        if left > 1 and n == PROJECT_AT:
                            queries(*after(*after(b, g)))
                        if left > 1 and n == PROJECT_AT + 1:
                            keys(*after(*after(b, g)))
                    if g == 0 and h == 0:
                        square_values(b, 0)
                    if h == 1 and g + 1 < G0:
                        square_values(b, g + 1)
                    if g == 2 and h == 1:
                        act.wait_ge(stats_in, b + 1 + AHEAD)
                        act.wait_ge(out_free, b + AHEAD)
                        act.activation(XQ[:, :, :], XM[:, :, :], ACT.Square).then_inc(sq_ready, 1)
                    if g == 2 and h == 0 and left > 1:
                        cut(b + 1)
                    if g == 0 and h == 2 and prior is not None:
                        roots(prior)

            def roots(b):
                act.wait_ge(var_x, b + 1 + AHEAD)
                act.activation(ST[:, 3, :], ST[:, 2, :], ACT.Sqrt, bias=EPS[:, 0:1])
                act.wait_ge(var_v, b + 1 + AHEAD)
                act.activation(VAR[:, :, :], VAR[:, :, :], ACT.Sqrt).then_inc(std_ready, 1)

            act.wait_ge(weights_split, 1 + AHEAD)
            cut(0)
            queries(0, 0)
            keys(0, 0)
            queries(0, 1)
            keys(0, 1)
            group(0, 0)
            group(0, 1)
            with act.Fori(0, B - 1) as b:
                group(b, 2)
                group(b, 3)
                group(b + 1, 0, prior=b)
                group(b + 1, 1)
            group(B - 1, 2, left=1)
            group(B - 1, 3, left=0)
            roots(B - 1)

        @block.vector
        def _(dve):
            dve.wait_ge(consts_in, 7 * 16 + AHEAD)
            for full, high, low in ((WQK, WH[:, :, :, :, :], WL[:, :, :, :, :]), (WV, WVH[:, :, :], WVL[:, :, :])):
                dve.tensor_copy(high, full)
                dve.drain()
                dve.tensor_tensor(low, full, high, ALU.subtract)
            dve.tensor_copy(MSELR[:, :], MSEL[:, :])
            dve.tensor_tensor(QKB[:, :, :], QKB[:, :, :], AUG[:, :, :], ALU.add)
            dve.drain()
            dve.tensor_scalar(QKB[:, 0, :], QKB[:, 0, :], float(D0) ** -0.5, None, ALU.mult).then_inc(weights_split, 1)

            def split(b, g):
                it, s = b * G0 + g, g % 2
                dve.wait_ge(t_ps, (it - 1) * NS + AHEAD)
                dve.wait_ge(km_in[s], (b * (G0 // 2) + g // 2) * N_HEADS + AHEAD)
                dve.wait_ge(qf_ready, it + 1 + AHEAD)
                dve.tensor_copy(QH[:, s, :], QF[:, :]).then_inc(qh_ready, 1)
                dve.wait_ge(kf_ready, it + 1 + AHEAD)
                dve.tensor_copy(KK[:, s, 0, :], KF[:, :]).then_inc(kh_ready, 1)
                dve.wait_ge(qh_ready, it + 1 + AHEAD)
                dve.tensor_tensor(QL[:, s, :], QF[:, :], QH[:, s, :], ALU.subtract)
                dve.wait_ge(kh_ready, it + 1 + AHEAD)
                dve.tensor_tensor(KK[:, s, 1, :], KF[:, :], KK[:, s, 0, :], ALU.subtract).then_inc(qk_split, 1)

            def take_max(b, g, n):
                it, s = b * G0 + g, g % 2
                dve.wait_ge(m_ps, it * NS + n + 1 + AHEAD)
                dve.tensor_reduce(NM[:, s, n:n + 1], ps[:, BM + n % 2, :], AX.X, ALU.max, negate=True).then_inc(m_read, 1)
                if n == NS - 1:
                    dve.drain().then_inc(nm_ready, 1)

            def turned_maxima(b, g):
                it, s = b * G0 + g, g % 2
                dve.wait_ge(nmT_ps, it + 1 + AHEAD)
                dve.wait_ge(max_in, (it - 1) * N_HEADS + AHEAD)
                dve.tensor_copy(NMT[:, s, :], ps[0:NS, BQ, 128:128 + P]).then_inc(nmT_sb, 1)

            def sums(b, g, h):
                it, s = b * G0 + g, g % 2
                if h == 0:
                    dve.wait_ge(u_read, it - 1 + AHEAD)
                dve.wait_ge(o_ps, it * HG + h + 1 + AHEAD)
                tile = ps[:, BO + h % 2, 0:EC * VW].rearrange("p (q v) -> p q v", q=EC)
                dve.reciprocal(DEN[:, s, :, h, :], tile[:, :, 0:1])
                dve.tensor_reduce(U[:, s, :, h, :], tile[:, :, 1:].rearrange("p q (a v) -> p q v a", a=3), AX.X, ALU.add)\
                   .then_inc(o_read, 1)
                if h == HG - 1:
                    dve.drain().then_inc(den_ready, 1)

            def cut(b):
                dve.wait_ge(inputs_in, (b + 1) * N_IN + AHEAD)
                dve.wait_ge(k_ps, b * G0 + AHEAD)
                dve.wait_ge(v_ps, b + AHEAD)
                dve.tensor_scalar(MBRR[:, :], M8R[:, :], -NEG, NEG, ALU.mult, ALU.add)
                dve.wait_ge(xc_high, b + 1 + AHEAD)
                dve.tensor_tensor(XL[:, :, :], X[:, :, :], XH[:, :, :], ALU.subtract)
                dve.tensor_tensor(CL[:, :, :], C[:, :, :], CH[:, :, :], ALU.subtract).then_inc(xc_split, 1)
                dve.drain().then_inc(inputs_read, 1)

            def take_values(b):
                dve.wait_ge(v_ps, b + 1 + AHEAD)
                dve.wait_ge(v_split, b * G0 + AHEAD)
                dve.tensor_tensor(VF[:, :, :, 0:D0], ps[:, BT:BT + 2, :].rearrange("p a (c h d) -> p (a c) h d", c=2, h=H0),
                                  BVB[:, :].rearrange("p (h d) -> p h d", h=H0).unsqueeze(1).broadcast_to([P, EC, H0, D0]), ALU.add)\
                   .then_inc(vf_ready, 1)

            def cut_values(b, g):
                heads = slice(g * HG, (g + 1) * HG)
                dve.wait_ge(v_square, b * G0 + g + 1 + AHEAD)
                dve.tensor_tensor(VF[:, :, heads, :], VF[:, :, heads, :], VA[:, :, heads, 1:1 + V2C], ALU.subtract)
                dve.drain()
                dve.tensor_copy(VA[:, :, heads, 1 + V2C:1 + 2 * V2C], VF[:, :, heads, :])
                dve.drain()
                dve.tensor_tensor(VA[:, :, heads, 1 + 2 * V2C:], VF[:, :, heads, :], VA[:, :, heads, 1 + V2C:1 + 2 * V2C], ALU.subtract)\
                   .then_inc(v_split, 1)

            def mask_x(b):
                dve.wait_ge(stats_x_in, (b + 1) * N_STATS + AHEAD)
                dve.wait_ge(out_ready, b + AHEAD)
                dve.tensor_copy(MCOL[:, :], M8C[:, :])
                dve.drain()
                for c in range(EC):
                    dve.tensor_scalar(XM[:, c, :], XT[:, c, :], MCOL[:, c:c + 1], None, ALU.mult)
                dve.drain().then_inc(stats_in, 1)
                dve.sem_inc(stats_read, 1)

            def moments(b):
                dve.wait_ge(st_ps, b + 1 + AHEAD)
                dve.reciprocal(RN[:, :], ps[:, BQ, 0:1])
                dve.drain()
                dve.tensor_scalar(ST[:, 0, :], ps[:, BK, 0:L], RN[:, 0:1], None, ALU.mult)
                dve.tensor_scalar(ST[:, 1, :], ps[:, BK, L:2 * L], RN[:, 0:1], None, ALU.mult)
                dve.drain().then_inc(st_read, 1)
                dve.tensor_tensor(ST[:, 2, :], ST[:, 0, :], ST[:, 0, :], ALU.mult)
                dve.drain()
                dve.tensor_tensor(ST[:, 2, :], ST[:, 1, :], ST[:, 2, :], ALU.subtract)
                dve.drain()
                dve.tensor_scalar(ST[:, 2, :], ST[:, 2, :], 0.0, None, ALU.max).then_inc(var_x, 1)

            def low_part(b, g, n):
                if n % 2 == 0:
                    dve.wait_ge(eh_ready, (b * G0 + g) * NS + n + 1 + AHEAD)
                    dve.tensor_tensor(EL[:, (n // EC) % 2, n % EC, :], EX[:, n % 4, :], EH[:, (n // EC) % 2, n % EC, :], ALU.subtract)\
                       .then_inc(el_dve, 1)

            def group(b, g, left=2, prior=None):
                if left:
                    split(*after(b, g))
                for n in range(NS):
                    h, k = divmod(n, EC)
                    if left:
                        for m in tiles_beside(n):
                            take_max(*after(b, g), m)
                        if n == TURN_AT:
                            turned_maxima(*after(b, g))
                    if g == G0 - 1 and n == MOMENTS_AT:
                        moments(b)
                    if n > 0:
                        low_part(b, g, n - 1)
                    if g == 0 and n == 4:
                        cut_values(b, 0)
                    if g + 1 < G0 and n == 12:
                        cut_values(b, g + 1)
                    if g == 1 and n == 13:
                        mask_x(b)
                    if g == 2 and n == 4 and left > 1:
                        cut(b + 1)
                    if g == 0 and n == 13 and prior is not None:
                        inverse_root(prior)
                    if k == 0 and h > 1:
                        sums(b, g, h - 2)
                    if k == 0 and h == 1 and (g > 0 or prior is not None):
                        sums(b if g > 0 else prior, g - 1 if g > 0 else G0 - 1, HG - 1)
                low_part(b, g, NS - 1)
                sums(b, g, HG - 2)

            def inverse_root(b):
                dve.wait_ge(std_ready, b + 1 + AHEAD)
                dve.reciprocal(ST[:, 3, :], ST[:, 3, :]).then_inc(rstd_ready, 1)

            cut(0)
            split(0, 0)
            take_values(0)
            for n in range(NS):
                take_max(0, 0, n)
            turned_maxima(0, 0)
            group(0, 0)
            group(0, 1)
            with dve.Fori(0, B - 1) as b:
                group(b, 2)
                group(b, 3)
                take_values(b + 1)
                group(b + 1, 0, prior=b)
                group(b + 1, 1)
            group(B - 1, 2, left=1)
            group(B - 1, 3, left=0)
            sums(B - 1, G0 - 1, HG - 1)
            inverse_root(B - 1)

S1 = 16
DM, DD = 32, 64
(V_LN1W, V_LN1B, V_LN2W, V_LN2B, V_MAAX, V_STACK, V_TD, V_U, V_GNW, V_GNB, V_FK, V_FR) = \
    (0, 1, 2, 3, 4, 5, 10, 11, 12, 13, 14, 15)
NV1 = 16
W_K, W_V, W_R, W_G, W_O, W_FK, W_FR, W_FV = range(8)
MIX_K, MIX_W, MIX_V, MIX_R, MIX_G = range(5)


def layer1(nc, x1T, prevs, s0, vecs, w8, maa_w1, maa_w2, td_w1, td_w2, sel, selT, blk, x2T):
    with ExitStack() as stack:
        def sb(name, shape, dt=F32):
            return stack.enter_context(nc.sbuf_tensor("b_" + name, shape, dt))

        sems = []

        def sem(name):
            sems.append(nc.alloc_semaphore("b_" + name))
            return sems[-1]

        W = sb("w", [P, 8, EC, E])
        W1 = sb("w1", [P, EC, 5 * DM])
        W2 = sb("w2", [P, 5, E])
        TW1 = sb("tw1", [P, EC, DD])
        TW2 = sb("tw2", [P, E])
        SELT = sb("selT", [P, S1, P])
        BO = sb("bo", [P, P])
        BM = sb("bm", [P, P])
        VEC = sb("vec", [P, NV1, EC])
        MEANW = sb("meanw", [P, P])
        EPS = sb("eps", [P, 1])
        X = sb("x", [P, EC, L])
        PV = sb("pv", [P, EC, 2])
        S0 = sb("s0", [P, EC, S1])
        XP = sb("xp", [P, EC, L + 1])
        SX = sb("sx", [P, EC, L])
        Z = sb("z", [P, EC, L])
        XC = sb("xc", [P, EC, L])
        SQ = sb("sq", [P, EC, L])
        SD = sb("sd", [P, L])
        XF = sb("xf", [P, 2, EC, L])
        KT, VT, RT, WT, GT, TH, BV, OG = [sb(n, [P, EC, L]) for n in ("kt", "vt", "rt", "wt", "gt", "th", "bv", "og")]
        T0 = sb("t0", [P, L])
        T1 = sb("t1", [P, L])
        TW = sb("tw", [P, L])
        VH = sb("vh", [P, EC, L], F32R)
        VL = sb("vl", [P, EC, L], F32R)
        SELR = sb("selr", [P, S1, P], F32R)
        A = sb("a", [P, 4, L])
        Y = sb("y", [P, 4, L])
        SB = sb("sb", [P, S1, L + 1])
        XS = SB[:, 0:EC, 0:L]
        SEL = SB[:, :, 0:P]
        ps = stack.enter_context(nc.psum_tensor("b_ps", [P, 8, 512], F32))

        def pair(bank):
            return ps[:, bank:bank + 2, :].rearrange("p a (c t) -> p (a c) t", c=2)

        PF, PA, PB, SM0, SM1 = pair(0), pair(2), pair(4), ps[:, 6, 0:L], ps[:, 7, 0:L]

        weights_in, x_in, x_used, memset_done = sem("weights_in"), sem("x_in"), sem("x_used"), sem("memset_done")
        sel_ready, vt_ready, v_low = sem("sel_ready"), sem("vt_ready"), sem("v_low")
        ln_in, mean_ps, xc_ready, sq_ready, var_ps, sd_ready = [sem(n) for n in ("ln_in", "mean_ps", "xc_ready", "sq_ready", "var_ps", "sd_ready")]
        xn_ready, xp_ready, gate_ready, fk_in, pv_in = sem("xn_ready"), sem("xp_ready"), sem("gate_ready"), sem("fk_in"), sem("pv_in")
        z_ready, h_ps, t_ready = sem("z_ready"), sem("h_ps"), sem("t_ready")
        mix_ps, mix_read, mix_ready, proj_ps, proj_read = [sem(n) for n in ("mix_ps", "mix_read", "mix_ready", "proj_ps", "proj_read")]
        tw_ps, tw_ready, w_ready, th_ready = sem("tw_ps"), sem("tw_ready"), sem("w_ready"), sem("th_ready")
        rku_ready, bonus_ps, bonus_read = sem("rku_ready"), sem("bonus_ps"), sem("bonus_read")
        vb_ps, vb_read, s_ready, s_used, y_ready, y_used = [sem(n) for n in ("vb_ps", "vb_read", "s_ready", "s_used", "y_ready", "y_used")]
        og_ready, gm_ps, gc_ready, gq_ready, gv_ps, gd_ready, root_ready, scaled, gn_ready = [sem(n) for n in ("og_ready", "gm_ps", "gc_ready", "gq_ready", "gv_ps", "gd_ready", "root_ready", "scaled", "gn_ready")]
        gated, wo_ps, x1_ready = sem("gated"), sem("wo_ps"), sem("x1_ready")
        ffn_in, ffr_ps, ffk_ps, rr_ready, kk_ready, kk2_ready, ffv_ps = [sem(n) for n in ("ffn_in", "ffr_ps", "ffk_ps", "rr_ready", "kk_ready", "kk2_ready", "ffv_ps")]
        out_ready, out_stored = sem("out_ready"), sem("out_stored")
        passed = sem("passed")
        projections_in = [stack.enter_context(nc.semaphore(f"b_projections_in{w}")) for w in range(W_G + 1)]
        NLN = 2
        GM, GV = ps[:, 4, 0:L], ps[:, 5, 0:L]
        AT_SUMS, AT_GM, AT_CENTRE, AT_GV, AT_ROOT, AT_SCALE, AT_GATE = 8, 9, 11, 13, 18, 19, 23
        STEPS = EC * S1
        stack.callback(nc.all_engine_barrier)
        stack.callback(lambda: nc.clear_and_free_semaphores(sems))
        block = stack.enter_context(nc.Block())

        def due(n, at):
            c, j = divmod(n - at - S1, S1)
            return c if j == 0 and 0 <= c < EC else None


        @block.sync
        def _(sp):
            start_ahead(sp, sems)
            for dst, src in ((W1[:, :, :], maa_w1), (W2[:, :, :], maa_w2),
                             (TW1[:, :, :], td_w1), (TW2[:, :], td_w2), (SEL, sel), (SELT[:, :, :], selT),
                             (BO[:, :], blk[0]), (BM[:, :], blk[1]), (VEC[:, :, :], vecs)):
                sp.dma_start(dst, src).then_inc(weights_in, 16)
            def load(b):
                sp.wait_ge(sel_ready, 1 + AHEAD)
                sp.wait_ge(y_ready, b * STEPS + AHEAD)
                sp.sem_inc(passed, 1)
                sp.dma_start(XS, x1T[b]).then_inc(x_in, 16)

            def load_states(b):
                sp.wait_ge(x_used, b + AHEAD)
                sp.sem_inc(passed, 1)
                sp.dma_start(PV[:, :, :], prevs[b]).then_inc(pv_in, 16)
                sp.dma_start(S0[:, :, :], s0[b]).then_inc(pv_in, 16)

            load(0)
            load_states(0)
            with sp.Fori(0, B - 1) as b:
                load(b + 1)
                sp.wait_ge(out_ready, b + 1 + AHEAD)
                sp.sem_inc(passed, 1)
                sp.dma_start(x2T[b], OG[:, :, :]).then_inc(out_stored, 16)
                load_states(b + 1)
            sp.wait_ge(out_ready, B + AHEAD)
            sp.dma_start(x2T[B - 1], OG[:, :, :]).then_inc(out_stored, 16)
            sp.wait_ge(out_stored, 16 * B + AHEAD)
        def project(pe, out, w, src):
            for o in range(EC):
                for k in range(EC):
                    mm = pe.matmul(out[:, o, :], W[:, w, k, o * P:(o + 1) * P], src[:, k, :], start=(k == 0),
                                   stop=(k == EC - 1), skip_group_check=True)
            return mm

        @block.tensor
        def _(pe):
            pe.wait_ge(weights_in, 16 * 9 + AHEAD)
            pe.wait_ge(memset_done, 1 + AHEAD)
            pe.wait_ge(sel_ready, 1 + AHEAD)

            def norm(n, src):
                pe.wait_ge(ln_in, n + 1 + AHEAD)
                for k in range(EC):
                    mm = pe.matmul(SM0, MEANW[:, :], src[:, k, :], start=(k == 0), stop=(k == EC - 1))
                mm.then_inc(mean_ps, 1)
                for k in range(EC):
                    pe.wait_ge(sq_ready, n * EC + k + 1 + AHEAD)
                    mm = pe.matmul(SM1, MEANW[:, :], SQ[:, k, :], start=(k == 0), stop=(k == EC - 1))
                mm.then_inc(var_ps, 1)

            with pe.Fori(0, B) as b:
                norm(b * NLN, X)
                pe.wait_ge(sd_ready, b * NLN + 1 + AHEAD)
                for k in range(EC):
                    pe.wait_ge(z_ready, b * EC + k + 1 + AHEAD)
                    pe.matmul(SM0, W1[:, k, 0:P], Z[:, k, :], start=(k == 0), stop=(k == EC - 1))
                for k in range(EC):
                    mm = pe.matmul(SM1[0:DM, :], W1[:, k, P:], Z[:, k, :], start=(k == 0), stop=(k == EC - 1))
                mm.then_inc(h_ps, 1)
                pe.wait_ge(t_ready, b + 1 + AHEAD)
                def mix(f):
                    if f > 0:
                        pe.wait_ge(mix_read, b * 5 + f + AHEAD)
                    for o in range(EC):
                        mm = pe.matmul(PF[:, o, :], W2[:, f, o * P:(o + 1) * P], T0[:, :] if f < 4 else T1[:, :], start=True, stop=True)
                    mm.then_inc(mix_ps, 1)

                mix(0)
                for f in range(5):
                    if f < 4:
                        mix(f + 1)
                    pe.wait_ge(mix_ready, b * 5 + f + 1 + AHEAD)
                    if f >= 2:
                        pe.wait_ge(proj_read, b * 5 + f - 1 + AHEAD)
                    dst = PA if f % 2 == 0 else PB
                    if f == MIX_W:
                        for k in range(EC):
                            mm = pe.matmul(SM0[0:DD, :], TW1[:, k, :], XF[:, f % 2, k, :], start=(k == 0), stop=(k == EC - 1))
                        mm.then_inc(tw_ps, 1)
                        pe.wait_ge(tw_ready, b + 1 + AHEAD)
                        for o in range(EC):
                            mm = pe.matmul(dst[:, o, :], TW2[:, o * P:(o + 1) * P], TW[:, :], start=True, stop=True)
                    else:
                        w = {MIX_K: W_K, MIX_V: W_V, MIX_R: W_R, MIX_G: W_G}[f]
                        pe.wait_ge(projections_in[w], 16)
                        mm = project(pe, dst, w, XF[:, f % 2])
                    mm.then_inc(proj_ps, 1)
                pe.wait_ge(rku_ready, b + 1 + AHEAD)
                pe.wait_ge(proj_read, b * 5 + 4 + AHEAD)
                for o in range(EC):
                    mm = pe.matmul(PB[:, o, :], BO[:, :], Z[:, o, :], start=True, stop=True)
                mm.then_inc(bonus_ps, 1)
                pe.wait_ge(v_low, b + 1 + AHEAD)
                pe.sem_inc(passed, 1)

                def spread(n):
                    c, j = divmod(n, S1)
                    if n == 2:
                        pe.wait_ge(proj_read, b * 5 + 5 + AHEAD)
                    pe.wait_ge(vb_read, b * STEPS + n - 3 + AHEAD)
                    pe.matmul(ps[:, n % 4, 0:L], SELR[:, j, :], VH[:, c, :], start=True, stop=False)
                    pe.matmul(ps[:, n % 4, 0:L], SELR[:, j, :], VL[:, c, :], start=False, stop=True).then_inc(vb_ps, 1)

                def gather(n):
                    c, j = divmod(n, S1)
                    if j == 0:
                        pe.wait_ge(og_ready, b * EC + c - 1 + AHEAD)
                    pe.wait_ge(y_ready, b * STEPS + n + 1 + AHEAD)
                    pe.matmul(SM0 if c % 2 == 0 else SM1, SELT[:, j, :], Y[:, n % 4, :], start=(j == 0), stop=(j == S1 - 1)).then_inc(y_used, 1)

                for n in range(3):
                    spread(n)
                for n in range(STEPS + S1 + AT_GATE):
                    if n + 3 < STEPS:
                        spread(n + 3)
                    c = due(n, AT_GM)
                    if c is not None:
                        pe.wait_ge(og_ready, b * EC + c + 1 + AHEAD)
                        pe.matmul(GM, BM[:, :], OG[:, c, :], start=True, stop=True).then_inc(gm_ps, 1)
                    c = due(n, AT_GV)
                    if c is not None:
                        pe.wait_ge(gq_ready, b * EC + c + 1 + AHEAD)
                        pe.matmul(GV, BM[:, :], SQ[:, c, :], start=True, stop=True).then_inc(gv_ps, 1)
                    if 1 < n < STEPS + 2:
                        gather(n - 2)
                pe.wait_ge(gated, (b + 1) * EC + AHEAD)
                project(pe, PA, W_O, Z).then_inc(wo_ps, 1)
                norm(b * NLN + 1, X)
                pe.wait_ge(fk_in, b + 1 + AHEAD)
                project(pe, PB, W_FK, XF[:, 1]).then_inc(ffk_ps, 1)
                pe.wait_ge(ffn_in, b + 1 + AHEAD)
                project(pe, PA, W_FR, XF[:, 0]).then_inc(ffr_ps, 1)
                pe.wait_ge(kk2_ready, b + 1 + AHEAD)
                project(pe, PB, W_FV, KT).then_inc(ffv_ps, 1)

        @block.scalar
        def _(act):
            act.wait_ge(weights_in, 16 * 9 + AHEAD)
            act.wait_ge(memset_done, 1 + AHEAD)
            def norm(n, w, bias):
                for k in range(EC):
                    act.wait_ge(xc_ready, n * EC + k + 1 + AHEAD)
                    act.activation(SQ[:, k, :], XC[:, k, :], ACT.Square).then_inc(sq_ready, 1)
                act.wait_ge(var_ps, n + 1 + AHEAD)
                act.activation(SD[:, :], SM1, ACT.Sqrt, bias=EPS[:, 0:1]).then_inc(sd_ready, 1)
                for k in range(EC):
                    act.wait_ge(xn_ready, n * EC + k + 1 + AHEAD)
                    act.activation(XP[:, k, 1:L + 1], XC[:, k, :], ACT.Identity, scale=VEC[:, w, k:k + 1], bias=VEC[:, bias, k:k + 1])\
                       .then_inc(xp_ready, 1)

            with act.Fori(0, B) as b:
                norm(b * NLN, V_LN1W, V_LN1B)
                act.wait_ge(h_ps, b + 1 + AHEAD)
                act.activation(T0[:, :], SM0, ACT.Tanh)
                act.activation(T1[0:DM, :], SM1[0:DM, :], ACT.Tanh).then_inc(t_ready, 1)
                act.wait_ge(proj_ps, b * 5 + 1 + AHEAD)
                act.activation(KT[:, :, :], PA, ACT.Copy).then_inc(proj_read, 1)
                act.wait_ge(tw_ps, b + 1 + AHEAD)
                act.activation(TW[0:DD, :], SM0[0:DD, :], ACT.Tanh).then_inc(tw_ready, 1)
                act.wait_ge(proj_ps, b * 5 + 2 + AHEAD)
                for o in range(EC):
                    act.activation(TH[:, o, :], PB[:, o, :], ACT.Exp, bias=VEC[:, V_TD, o:o + 1])
                act.drain().then_inc(proj_read, 1)
                act.activation(WT[:, :, :], TH[:, :, :], ACT.Exp, scale=-1.0).then_inc(w_ready, 1)
                act.wait_ge(proj_ps, b * 5 + 3 + AHEAD)
                act.activation(VH[:, :, :], PA, ACT.Copy)
                act.activation(VT[:, :, :], PA, ACT.Copy).then_inc(proj_read, 1)
                act.drain().then_inc(vt_ready, 1)
                act.wait_ge(proj_ps, b * 5 + 4 + AHEAD)
                act.activation(RT[:, :, :], PB, ACT.Copy).then_inc(proj_read, 1)
                act.wait_ge(proj_ps, b * 5 + 5 + AHEAD)
                act.activation(GT[:, :, :], PA, ACT.Copy)
                act.activation(TH[:, :, :], PA, ACT.Tanh, scale=0.5).then_inc(proj_read, 1)
                act.drain().then_inc(th_ready, 1)
                def affine(c):
                    act.wait_ge(scaled, b * EC + c + 1 + AHEAD)
                    act.activation(XC[:, c, :], XC[:, c, :], ACT.Identity, scale=VEC[:, V_GNW, c:c + 1], bias=VEC[:, V_GNB, c:c + 1]).then_inc(gn_ready, 1)

                for c in range(EC):
                    act.wait_ge(gc_ready, b * EC + c + 1 + AHEAD)
                    if c == 0:
                        act.wait_ge(gate_ready, (b + 1) * EC + AHEAD)
                    act.activation(SQ[:, c, :], XC[:, c, :], ACT.Square).then_inc(gq_ready, 1)
                    act.wait_ge(gv_ps, b * EC + c + 1 + AHEAD)
                    act.activation(TH[:, c, :], GV, ACT.Sqrt, bias=EPS[:, 0:1]).then_inc(gd_ready, 1)
                    affine(c)
                norm(b * NLN + 1, V_LN2W, V_LN2B)
                act.wait_ge(ffk_ps, b + 1 + AHEAD)
                act.activation(KT[:, :, :], PB, ACT.Relu).then_inc(kk_ready, 1)
                act.wait_ge(ffr_ps, b + 1 + AHEAD)
                act.activation(RT[:, :, :], PA, ACT.Tanh, scale=0.5).then_inc(rr_ready, 1)

        @block.gpsimd
        def _(pool):
            pool.memset(MEANW[:, :], 1.0 / E)
            pool.memset(T1[:, :], 0.0)
            pool.memset(TW[:, :], 0.0)
            pool.memset(EPS[:, :], LN_EPS).then_inc(memset_done, 1)
            pool.wait_ge(weights_in, 16 * 9 + AHEAD)
            pool.wait_ge(x_in, 16 + AHEAD)
            for w in range(W_G):
                pool.dma_start(W[:, w], w8[:, w]).then_inc(projections_in[w], 16)
            pool.dma_start(W[:, W_G:], w8[:, W_G:]).then_inc(projections_in[W_G], 16)
            with pool.Fori(0, B) as b:
                pool.wait_ge(vt_ready, b + 1 + AHEAD)
                pool.sem_inc(passed, 1)
                pool.tensor_tensor(VL[:, :, :], VT[:, :, :], VH[:, :, :], ALU.subtract).then_inc(v_low, 1)
                for n in range(STEPS + S1 + AT_GATE + 1):
                    if n in (2, 5, 8, 11):
                        c = (n - 2) // 3
                        if c == 0:
                            pool.wait_ge(th_ready, b + 1 + AHEAD)
                            pool.sem_inc(passed, 1)
                        pool.tensor_scalar(TH[:, c, :], TH[:, c, :], 0.5, 0.5, ALU.mult, ALU.add)
                        pool.drain()
                        pool.tensor_tensor(GT[:, c, :], GT[:, c, :], TH[:, c, :], ALU.mult).then_inc(gate_ready, 1)
                    c = due(n, AT_SCALE)
                    if c is not None:
                        pool.wait_ge(root_ready, b * EC + c + 1 + AHEAD)
                        pool.tensor_tensor(XC[:, c, :], XC[:, c, :], TH[:, c, :], ALU.mult).then_inc(scaled, 1)
                    c = due(n, AT_GATE)
                    if c is not None:
                        pool.wait_ge(gn_ready, b * EC + c + 1 + AHEAD)
                        pool.tensor_tensor(Z[:, c, :], XC[:, c, :], GT[:, c, :], ALU.mult).then_inc(gated, 1)
                    if n >= STEPS:
                        continue
                    c, j = divmod(n, S1)
                    pool.wait_ge(s_ready, b * STEPS + n + 1 + AHEAD)
                    pool.wait_ge(y_used, b * STEPS + n - 3 + AHEAD)
                    pool.tensor_tensor(Y[:, n % 4, :], SB[:, j, 0:L], RT[:, c, :], ALU.mult).then_inc(y_ready, 1)

        @block.vector
        def _(dve):
            dve.wait_ge(weights_in, 16 * 9 + AHEAD)
            dve.tensor_copy(SELR[:, :, :], SEL).then_inc(sel_ready, 1)
            dve.drain()
            def vec(v, o):
                return VEC[:, v, o:o + 1]

            def norm(b, n, src, prev_col):
                dve.wait_ge(mean_ps, n + 1 + AHEAD)
                for k in range(EC):
                    dve.tensor_tensor(XC[:, k, :], src[:, k, :], SM0, ALU.subtract).then_inc(xc_ready, 1)
                dve.wait_ge(pv_in, (b + 1) * 32 + AHEAD)
                dve.tensor_copy(XP[:, :, 0:1], PV[:, :, prev_col:prev_col + 1])
                dve.wait_ge(sd_ready, n + 1 + AHEAD)
                dve.reciprocal(SD[:, :], SD[:, :])
                dve.drain()
                for k in range(EC):
                    dve.tensor_tensor(XC[:, k, :], XC[:, k, :], SD[:, :], ALU.mult).then_inc(xn_ready, 1)
                for k in range(EC):
                    dve.wait_ge(xp_ready, n * EC + k + 1 + AHEAD)
                    dve.tensor_tensor(SX[:, k, :], XP[:, k, 0:L], XP[:, k, 1:L + 1], ALU.subtract)
                dve.drain()

            with dve.Fori(0, B) as b:
                dve.wait_ge(x_in, (b + 1) * 16 + AHEAD)
                dve.tensor_copy(X[:, :, :], XS).then_inc(ln_in, 1)
                norm(b, b * NLN, X, 1)
                for o in range(EC):
                    dve.scalar_tensor_tensor(Z[:, o, :], SX[:, o, :], vec(V_MAAX, o), XP[:, o, 1:L + 1], ALU.mult, ALU.add).then_inc(z_ready, 1)
                for f in range(5):
                    dve.wait_ge(mix_ps, b * 5 + f + 1 + AHEAD)
                    if f >= 2:
                        dve.wait_ge(proj_ps, b * 5 + f - 1 + AHEAD)
                    for o in range(EC):
                        dve.scalar_tensor_tensor(XF[:, f % 2, o, :], PF[:, o, :], vec(V_STACK + f, o), SX[:, o, :], ALU.add, ALU.mult)
                    dve.drain().then_inc(mix_read, 1)
                    dve.tensor_tensor(XF[:, f % 2], XF[:, f % 2], XP[:, :, 1:L + 1], ALU.add).then_inc(mix_ready, 1)
                dve.wait_ge(proj_read, b * 5 + 4 + AHEAD)
                dve.tensor_tensor(Z[:, :, :], RT[:, :, :], KT[:, :, :], ALU.mult)
                dve.drain()
                for o in range(EC):
                    dve.tensor_scalar(Z[:, o, :], Z[:, o, :], vec(V_U, o), None, ALU.mult)
                dve.drain().then_inc(rku_ready, 1)
                dve.wait_ge(bonus_ps, b + 1 + AHEAD)
                dve.tensor_tensor(BV[:, :, :], VT[:, :, :], PB, ALU.mult).then_inc(bonus_read, 1)
                dve.wait_ge(w_ready, b + 1 + AHEAD)
                dve.wait_ge(out_stored, b * 16 + AHEAD)
                dve.sem_inc(passed, 1)
                def scan(n):
                    c, j = divmod(n, S1)
                    dve.wait_ge(vb_read, b * STEPS + n + 1 + AHEAD)
                    dve.tensor_tensor_scan(SB[:, j, 1:L + 1], WT[:, c, :], A[:, n % 4, :], S0[:, c, j:j + 1], ALU.mult, ALU.add).then_inc(s_ready, 1)

                def take_sums(c):
                    dve.wait_ge(y_used, b * STEPS + (c + 1) * S1 + AHEAD)
                    dve.tensor_tensor(OG[:, c, :], BV[:, c, :], SM0 if c % 2 == 0 else SM1, ALU.add).then_inc(og_ready, 1)

                for n in range(STEPS + S1 + AT_GATE + 1):
                    c = due(n, AT_SUMS)
                    if c is not None:
                        take_sums(c)
                    c = due(n, AT_CENTRE)
                    if c is not None:
                        dve.wait_ge(gm_ps, b * EC + c + 1 + AHEAD)
                        dve.tensor_tensor(XC[:, c, :], OG[:, c, :], GM, ALU.subtract).then_inc(gc_ready, 1)
                    c = due(n, AT_ROOT)
                    if c is not None:
                        dve.wait_ge(gd_ready, b * EC + c + 1 + AHEAD)
                        dve.reciprocal(TH[:, c, :], TH[:, c, :]).then_inc(root_ready, 1)
                    if n == STEPS:
                        scan(STEPS - 1)
                    if n >= STEPS:
                        continue
                    c, j = divmod(n, S1)
                    if j % 8 == 0:
                        dve.wait_ge(y_ready, b * STEPS + n - 8 + AHEAD)
                        dve.tensor_copy(SB[:, j:j + 8, 0:1], S0[:, c, j:j + 8].unsqueeze(2))
                    dve.wait_ge(vb_ps, b * STEPS + n + 1 + AHEAD)
                    dve.tensor_tensor(A[:, n % 4, :], KT[:, c, :], ps[:, n % 4, 0:L], ALU.mult).then_inc(vb_read, 1)
                    if n > 0:
                        scan(n - 1)
                dve.wait_ge(wo_ps, b + 1 + AHEAD)
                dve.tensor_tensor(X[:, :, :], X[:, :, :], PA, ALU.add).then_inc(ln_in, 1)
                dve.drain()
                norm(b, b * NLN + 1, X, 0)
                for o in range(EC):
                    dve.scalar_tensor_tensor(XF[:, 1, o, :], SX[:, o, :], vec(V_FK, o), XP[:, o, 1:L + 1], ALU.mult, ALU.add)
                dve.drain().then_inc(fk_in, 1)
                for o in range(EC):
                    dve.scalar_tensor_tensor(XF[:, 0, o, :], SX[:, o, :], vec(V_FR, o), XP[:, o, 1:L + 1], ALU.mult, ALU.add)
                dve.drain().then_inc(ffn_in, 1)
                dve.wait_ge(kk_ready, b + 1 + AHEAD)
                dve.tensor_tensor(KT[:, :, :], KT[:, :, :], KT[:, :, :], ALU.mult).then_inc(kk2_ready, 1)
                dve.wait_ge(rr_ready, b + 1 + AHEAD)
                dve.tensor_scalar(RT[:, :, :], RT[:, :, :], 0.5, 0.5, ALU.mult, ALU.add)
                dve.drain()
                dve.wait_ge(ffv_ps, b + 1 + AHEAD)
                dve.tensor_tensor(OG[:, :, :], RT[:, :, :], PB, ALU.mult)
                dve.drain()
                dve.tensor_tensor(OG[:, :, :], OG[:, :, :], X[:, :, :], ALU.add).then_inc(out_ready, 1)
                dve.drain().then_inc(x_used, 1)

H2, K2, F2 = 16, 128, 2048
N2 = 2 * L
FC2 = F2 // P
W2 = EC * P
HSTEP = 4
PARTS = 12
(V2_NW, V2_NB, V2_BO) = range(3)
(C2_BQ, C2_BK, C2_KEY, C2_BV) = range(4)


def layer2(nc, x2T, ctxT, wq, wk, wv, heads, value_rows, part_mask, chunk_mask, downs, fc1, fc1_b, vec2, ident_in, x3T):
    with ExitStack() as stack:
        def sb(name, shape, dt=F32):
            return stack.enter_context(nc.sbuf_tensor("c_" + name, shape, dt))

        sems = []

        def sem(name):
            sems.append(nc.alloc_semaphore("c_" + name))
            return sems[-1]

        def dma_sem(name):
            return stack.enter_context(nc.semaphore("c_" + name))

        X = sb("x", [P, EC, N2])
        CTH = sb("cth", [P, EC, N2], F32R)
        CTL = sb("ctl", [P, EC, N2], F32R)
        HH = sb("hh", [P, EC, N2], F32R)
        HL = sb("hl", [P, EC, N2], F32R)
        SD = sb("sd", [P, N2])
        ID = sb("id", [P, P])
        MEANW = sb("meanw", [P, P])
        EPS = sb("eps", [P, 1])
        VEC = sb("vec", [P, 3, 3, EC])
        HC = sb("hc", [P, 2 * H2, 4])
        FB = sb("fb", [P, FC2, 1])
        PMASK = sb("pmask", [PARTS, 2])
        CMASK = sb("cmask", [PARTS, 4, P])
        COL = sb("col", [P, 2, 4])
        WR = sb("wr", [P, 6, W2])
        WH = sb("wh", [P, 6, W2], F32R)
        WL = sb("wl", [P, 6, W2], F32R)
        QH = sb("qh", [P, 2, N2], F32R)
        QL = sb("ql", [P, 2, N2], F32R)
        KH = sb("kh", [P, 2, 2, L + 2], F32R)
        KL = sb("kl", [P, 2, 2, L + 2], F32R)
        VH = sb("vh", [P, 2, 4, 2, P], F32R)
        VL = sb("vl", [P, 2, 4, 2, P], F32R)
        NM = sb("nm", [P, 4])
        NMS = sb("nms", [P, 4])
        RS = sb("rs", [P, 4])
        PR = sb("pr", [P, 4, L + 2])
        PB = sb("pb", [P, 3, 4])
        PBH = sb("pbh", [P, 4], F32R)
        PTH = sb("pth", [P, 2, 2, L], F32R)
        PTL = sb("ptl", [P, 2, 2, L], F32R)
        RW = sb("rw", [PARTS, 2, 2, P])
        RD = sb("rd", [PARTS, P])
        RDH = sb("rdh", [PARTS, P], F32R)
        RST = sb("rst", [P, 2, P], F32R)
        BD = sb("bd", [P, 4, P], F32R)
        G = sb("g", [P, H2, N2])
        GH = sb("gh", [P, 2, N2], F32R)
        GL = sb("gl", [P, 2, N2], F32R)
        H = G[:, 0:EC, :]
        SQ = G[:, EC:2 * EC, :]
        CT = G[:, 2 * EC:3 * EC, :]
        ps = stack.enter_context(nc.psum_tensor("c_ps", [P, 8, 512], F32))
        BQ, BK, BV, BS, BT, BC, BX = 0, 1, 2, 3, 5, 7, 4

        names = """consts_in x_in ct_in ct_read memset_done ln_in mean_ps xc_ready sq_ready var_ps sd_ready h_full h_high h_ready
            ct_high ct_ready q_ps k_ps v_ps q_high q_low k_high k_low v_high v_low s_ps max_ready exp_ready p_ready t_ps
            pt_high pt_low pb_ready tb_ps bd_ready col_ready rows_ready c_ps c_ready x_ready g_high g_low g_used
            fc_ps gelu_ready out_free passed"""
        S = {n: sem(n) for n in names.split()}
        (consts_in, x_in, ct_in, ct_read, memset_done, ln_in, mean_ps, xc_ready, sq_ready, var_ps, sd_ready, h_full, h_high, h_ready,
         ct_high, ct_ready, q_ps, k_ps, v_ps, q_high, q_low, k_high, k_low, v_high, v_low, s_ps, max_ready, exp_ready, p_ready, t_ps,
         pt_high, pt_low, pb_ready, tb_ps, bd_ready, col_ready, rows_ready, c_ps, c_ready, x_ready, g_high, g_low, g_used,
         fc_ps, gelu_ready, out_free, passed) = [S[n] for n in names.split()]
        out_stored = dma_sem("out_stored")
        piece_in = [sem(f"piece_in{i}") for i in range(5)]
        piece_high = [sem(f"piece_high{i}") for i in range(5)]
        piece_cut = [sem(f"piece_cut{i}") for i in range(5)]
        rows_in = [sem(f"rows_in{i}") for i in range(2)]
        NPAIR = B // 2
        stack.callback(nc.all_engine_barrier)
        stack.callback(lambda: nc.clear_and_free_semaphores(sems))
        block = stack.enter_context(nc.Block())

        VS = 4
        PER_PAIR, PER_ATT = 32, 12

        def slot_of(t, slot):
            if slot == VS:
                return t[:, 4:6, :].rearrange("p a (k m) -> p (a k) m", m=2 * P)
            return t[:, slot, :].rearrange("p (k m) -> p k m", k=EC)

        def piece(t, slot):
            return t[:, 4:6, :] if slot == VS else t[:, slot, :]

        def qk_count(b, a, n):
            return b * PER_PAIR + a * PER_ATT + n

        def v_count(b, a, j):
            return (b * 2 + a) * (H2 // 2) + j

        def head_steps(eng, head):
            head(0, 0, first=True)
            with eng.Fori(0, H2 // HSTEP - 1) as i:
                head(i * 2, 1)
                head(i * 2 + 1, 2)
                head(i * 2 + 1, 3)
                head(i * 2 + 2, 0)
            head(H2 // 2 - 2, 1)
            head(H2 // 2 - 1, 2)
            head(H2 // 2 - 1, 3)

        def is_head(j, c, n):
            return isinstance(j, int) and j * 2 + c % 2 == n

        @block.sync
        def _(sp):
            start_ahead(sp, sems)
            for dst, src in ((ID[:, :], ident_in), (VEC[:, :, :, :], vec2), (HC[:, :, :], heads), (FB[:, :, 0], fc1_b), (PMASK[:, :], part_mask),
                             (CMASK[:, :, :], chunk_mask)):
                sp.dma_start(dst, src).then_inc(consts_in, 16)

            def fetch(slot, count, src):
                sp.wait_ge(piece_cut[slot], count + AHEAD)
                sp.sem_inc(passed, 1)
                if slot == VS:
                    sp.dma_start(WR[:, 4:6, :].rearrange("p a m -> p (a m)"), src).then_inc(piece_in[slot], 16)
                else:
                    sp.dma_start(WR[:, slot, :], src).then_inc(piece_in[slot], 16)

            def load_ctx(b):
                sp.wait_ge(g_used, b * 48 - 16 + AHEAD)
                sp.sem_inc(passed, 1)
                for i in range(2):
                    sp.dma_start(CT[:, :, i * L:(i + 1) * L], ctxT[b * 2 + i].rearrange("(k p) c -> p k c", p=P)).then_inc(ct_in, 16)

            def pair(b, more):
                sp.wait_ge(out_free, b + AHEAD)
                sp.sem_inc(passed, 1)
                for i in range(2):
                    sp.dma_start(X[:, :, i * L:(i + 1) * L], x2T[b * 2 + i]).then_inc(x_in, 16)
                with sp.Fori(0, 2) as a:
                    fetch(VS, v_count(b, a, 0), wv[a * (H2 // 2)])

                    def head_pair(j, more):
                        for u in range(2):
                            fetch(2 * u, qk_count(b, a, j), wq[a * H2 + j * 2 + u])
                            fetch(2 * u + 1, qk_count(b, a, j), wk[a * H2 + j * 2 + u])
                        if more:
                            fetch(VS, v_count(b, a, j + 1), wv[a * (H2 // 2) + j + 1])
                        for u in range(2):
                            sp.wait_ge(rows_ready, ((b * 2 + a) * (H2 // 2) + j) * 2 + u - 1 + AHEAD)
                            sp.sem_inc(passed, 1)
                            sp.dma_start(RW[:, u, :, :], value_rows[a * H2 + j * 2 + u]).then_inc(rows_in[u], 16)

                    with sp.Fori(0, H2 // 2 - 1) as j:
                        head_pair(j, True)
                    head_pair(H2 // 2 - 1, False)
                    with sp.Fori(0, H2 // 4) as j:
                        for u in range(4):
                            fetch(u, b * PER_PAIR + a * PER_ATT + H2 // 2 + j, downs[a * H2 + j * 4 + u])
                if more:
                    load_ctx(b + 1)
                with sp.Fori(0, FC2 // 2) as f:
                    for u in range(2):
                        fetch(2 * u, b * PER_PAIR + 2 * PER_ATT + f, fc1[f * 2 + u])
                        fetch(2 * u + 1, b * PER_PAIR + 2 * PER_ATT + f, downs[2 * H2 + f * 2 + u])

            load_ctx(0)
            if NPAIR > 1:
                with sp.Fori(0, NPAIR - 1) as b:
                    pair(b, True)
            pair(NPAIR - 1, False)

        @block.gpsimd
        def _(pool):
            pool.memset(MEANW[:, :], 1.0 / E)
            pool.memset(EPS[:, :], LN_EPS)
            pool.memset(RST[:, :, :].bitcast(F32), 0.0)
            pool.memset(BD[:, :, :].bitcast(F32), 0.0).then_inc(memset_done, 1)

            def cut(slot, count):
                pool.wait_ge(piece_high[slot], count + 1 + AHEAD)
                pool.sem_inc(passed, 1)
                pool.tensor_tensor(piece(WL, slot), piece(WR, slot), piece(WH, slot), ALU.subtract).then_inc(piece_cut[slot], 1)

            def norm_low(n):
                for k in range(EC):
                    pool.wait_ge(h_high, n * EC + k + 1 + AHEAD)
                    pool.sem_inc(passed, 1)
                    pool.tensor_tensor(HL[:, k, :], H[:, k, :], HH[:, k, :], ALU.subtract).then_inc(h_ready, 1)

            with pool.Fori(0, NPAIR) as b:
                with pool.Fori(0, 2) as a:
                    cut(VS, v_count(b, a, 0))
                    for u in (1, 0, 3, 2):
                        cut(u, qk_count(b, a, 0))
                    norm_low(b * 3 + a)
                    with pool.Fori(1, H2 // 2) as j:
                        cut(VS, v_count(b, a, j))
                        for u in range(4):
                            cut(u, qk_count(b, a, j))
                    with pool.Fori(0, H2 // 4) as j:
                        for u in range(4):
                            cut(u, b * PER_PAIR + a * PER_ATT + H2 // 2 + j)
                F0 = b * PER_PAIR + 2 * PER_ATT
                cut(0, F0)
                cut(2, F0)
                norm_low(b * 3 + 2)
                with pool.Fori(0, FC2 // 2 - 1) as f:
                    for u in range(2):
                        cut(2 * u + 1, F0 + f)
                        cut(2 * u, F0 + f + 1)
                cut(1, F0 + FC2 // 2 - 1)
                cut(3, F0 + FC2 // 2 - 1)
                pool.wait_ge(x_ready, (b * 3 + 3) * EC + AHEAD)
                pool.sem_inc(passed, 1)
                for i in range(2):
                    pool.dma_start(x3T[b * 2 + i], X[:, :, i * L:(i + 1) * L]).then_inc(out_stored, 16)
                pool.wait_ge(out_stored, (b + 1) * 32)
                pool.sem_inc(out_free, 1)

        @block.tensor
        def _(pe):
            pe.wait_ge(consts_in, 6 * 16 + AHEAD)
            pe.wait_ge(memset_done, 1 + AHEAD)

            def product(out, stationary, moving, start=True, stop=True):
                (sh, sl), (mh, ml) = stationary, moving
                pe.matmul(out, sh, mh, start=start, stop=False, skip_group_check=True)
                pe.matmul(out, sh, ml, start=False, stop=False, skip_group_check=True)
                return pe.matmul(out, sl, mh, start=False, stop=stop, skip_group_check=True)

            def norm(n, before=None, middle=None):
                if before:
                    before()
                for k in range(EC):
                    pe.wait_ge(ln_in, n * EC + k + 1 + AHEAD)
                    mm = pe.matmul(ps[:, BQ, :], MEANW[:, :], X[:, k, :], start=(k == 0), stop=(k == EC - 1))
                mm.then_inc(mean_ps, 1)
                if middle:
                    middle()
                for k in range(EC):
                    pe.wait_ge(sq_ready, n * EC + k + 1 + AHEAD)
                    mm = pe.matmul(ps[:, BK, :], MEANW[:, :], SQ[:, k, :], start=(k == 0), stop=(k == EC - 1))
                mm.then_inc(var_ps, 1)

            def project(slot, count, high, low, bank, done):
                pe.wait_ge(piece_cut[slot], count + 1 + AHEAD)
                wh, wl = slot_of(WH, slot), slot_of(WL, slot)
                for k in range(EC):
                    mm = product(ps[:, bank, :], (wh[:, k, :], wl[:, k, :]), (high[:, k, :], low[:, k, :]), k == 0, k == EC - 1)
                mm.then_inc(done, 1)

            def queries(b, a, j, u):
                pe.wait_ge(q_low, (b * 2 + a) * H2 + j * 2 + u + AHEAD)
                project(2 * u, qk_count(b, a, j), HH, HL, BQ, q_ps)

            def keys(b, a, j, u):
                pe.wait_ge(k_low, (b * 2 + a) * H2 + j * 2 + u + AHEAD)
                project(2 * u + 1, qk_count(b, a, j), CTH, CTL, BK, k_ps)

            def values(b, a, j, half):
                pe.wait_ge(v_low, v_count(b, a, j) * 2 + half + AHEAD)
                pe.wait_ge(piece_cut[VS], v_count(b, a, j) + 1 + AHEAD)
                wh, wl = slot_of(WH, VS), slot_of(WL, VS)
                for t in range(2):
                    cols = slice((half * 2 + t) * P, (half * 2 + t + 1) * P)
                    for k in range(EC):
                        mm = product(ps[:, BV, t * 2 * P:(t + 1) * 2 * P], (CTH[:, k, cols], CTL[:, k, cols]), (wh[:, k, :], wl[:, k, :]),
                                     k == 0, k == EC - 1)
                mm.then_inc(v_ps, 1)

            def scores(N, u, i0):
                if i0 == 0:
                    pe.wait_ge(q_low, N + 1 + AHEAD)
                    pe.wait_ge(k_low, N + 1 + AHEAD)
                for i in range(i0, i0 + 2):
                    if i == 1:
                        pe.wait_ge(bd_ready, N + AHEAD)
                    pe.wait_ge(exp_ready, N * 4 + i - 1 + AHEAD)
                    cols = slice(i * P, (i + 1) * P)
                    product(ps[:, BS + 1 - i % 2, 0:L + 2], (QH[:, u, cols], QL[:, u, cols]), (KH[:, u, i // 2, :], KL[:, u, i // 2, :])).then_inc(s_ps, 1)

            def turn(N):
                for i in range(2):
                    pe.wait_ge(p_ready, N * 4 + 2 * i + 2 + AHEAD)
                    pe.wait_ge(pt_low, N * 2 + i - 1 + AHEAD)
                    for t in range(2):
                        for q in range(2):
                            mm = pe.transpose(ps[:, BT + i, t * L + q * P:t * L + (q + 1) * P], PR[:, 2 * i + q, t * P:(t + 1) * P], ID[:, :])
                    mm.then_inc(t_ps, 1)
                pe.wait_ge(pb_ready, N + 1 + AHEAD)
                pe.wait_ge(exp_ready, N * 4 + 4 + AHEAD)
                pe.transpose(ps[0:PARTS, BS, 384:384 + P], PB[:, :, :].rearrange("p a i -> p (a i)"), ID[:, :]).then_inc(tb_ps, 1)

            def context(N, u, v):
                pe.wait_ge(c_ready, N + AHEAD)
                pe.wait_ge(rows_ready, N + 1 + AHEAD)
                pe.wait_ge(bd_ready, N + 1 + AHEAD)
                pe.matmul(ps[:, BC, :], RST[:, u, :], BD[:, :, :].rearrange("p c q -> p (c q)"), start=True, stop=False, skip_group_check=True)
                for i in range(2):
                    pe.wait_ge(pt_low, N * 2 + i + 1 + AHEAD)
                    for t in range(2):
                        mm = product(ps[:, BC, i * L:(i + 1) * L], (VH[:, v, 2 * i + t, u, :], VL[:, v, 2 * i + t, u, :]),
                                     (PTH[:, i, t, :], PTL[:, i, t, :]), False, t == 1)
                mm.then_inc(c_ps, 1)

            def add_down(slot, count, g, first, last):
                pe.wait_ge(piece_cut[slot], count + 1 + AHEAD)
                wh, wl = slot_of(WH, slot), slot_of(WL, slot)
                for d in range(EC):
                    mm = product(ps[:, BX + d, :], (wh[:, d, :], wl[:, d, :]), (GH[:, g, :], GL[:, g, :]), first, last)
                mm.then_inc(g_used, 1)

            with pe.Fori(0, NPAIR) as b:
                with pe.Fori(0, 2) as a:
                    def first_values():
                        pe.wait_ge(ct_ready, b + 1 + AHEAD)
                        pe.sem_inc(passed, 1)
                        values(b, a, 0, 0)

                    norm(b * 3 + a, first_values, lambda: values(b, a, 0, 1))
                    pe.wait_ge(sd_ready, b * 3 + a + 1 + AHEAD)
                    keys(b, a, 0, 0)
                    pe.wait_ge(h_ready, (b * 3 + a + 1) * EC + AHEAD)
                    pe.sem_inc(passed, 1)
                    queries(b, a, 0, 0)

                    def head(j, c, first=False):
                        u, v = c % 2, c // 2
                        N = (b * 2 + a) * H2 + j * 2 + u
                        scores(N, u, 0)
                        if not first:
                            context(N - 1, 1 - u, ((c - 1) % 4) // 2)
                        scores(N, u, 2)
                        nj = j + u
                        if not is_head(j, c, H2 - 1):
                            queries(b, a, nj, 1 - u)
                            keys(b, a, nj, 1 - u)
                        turn(N)
                        if not (is_head(j, c, H2 - 2) or is_head(j, c, H2 - 1)):
                            values(b, a, j + 1, u)

                    head_steps(pe, head)
                    context((b * 2 + a + 1) * H2 - 1, 1, 1)
                    pe.wait_ge(c_ready, (b * 2 + a + 1) * H2 + AHEAD)
                    pe.sem_inc(passed, 1)

                    def down_step(j, u, first, last):
                        n = b * 48 + a * 16 + j * 4 + u
                        pe.wait_ge(g_low, n + 1 + AHEAD)
                        add_down(u, b * PER_PAIR + a * PER_ATT + H2 // 2 + j, u % 2, first, last)

                    for u in range(4):
                        down_step(0, u, u == 0, False)
                    with pe.Fori(1, H2 // 4 - 1) as j:
                        for u in range(4):
                            down_step(j, u, False, False)
                    for u in range(4):
                        down_step(H2 // 4 - 1, u, False, u == 3)
                norm(b * 3 + 2)
                pe.wait_ge(h_ready, (b * 3 + 3) * EC + AHEAD)
                pe.sem_inc(passed, 1)

                def up(f, u):
                    pe.wait_ge(gelu_ready, b * FC2 + f * 2 + u - 1 + AHEAD)
                    project(2 * u, b * PER_PAIR + 2 * PER_ATT + f, HH, HL, BQ + u, fc_ps)

                def down(f, u, first, last):
                    pe.wait_ge(g_low, b * 48 + 32 + f * 2 + u + 1 + AHEAD)
                    add_down(2 * u + 1, b * PER_PAIR + 2 * PER_ATT + f, u, first, last)

                up(0, 0)
                up(0, 1)
                down(0, 0, True, False)
                with pe.Fori(1, FC2 // 2) as f:
                    up(f, 0)
                    down(f - 1, 1, False, False)
                    up(f, 1)
                    down(f, 0, False, False)
                down(FC2 // 2 - 1, 1, False, True)

        @block.scalar
        def _(act):
            act.wait_ge(memset_done, 1 + AHEAD)

            def norm(n, middle=None):
                for k in range(EC):
                    act.wait_ge(xc_ready, n * EC + k + 1 + AHEAD)
                    act.activation(SQ[:, k, :], H[:, k, :], ACT.Square).then_inc(sq_ready, 1)
                if middle:
                    middle()
                act.wait_ge(var_ps, n + 1 + AHEAD)
                act.activation(SD[:, :], ps[:, BK, :], ACT.Sqrt, bias=EPS[:, 0:1]).then_inc(sd_ready, 1)
                for k in range(EC):
                    act.wait_ge(h_full, n * EC + k + 1 + AHEAD)
                    act.activation(HH[:, k, :], H[:, k, :], ACT.Copy).then_inc(h_high, 1)

            def cut(slot, count):
                act.wait_ge(piece_in[slot], (count + 1) * 16 + AHEAD)
                act.activation(piece(WH, slot), piece(WR, slot), ACT.Copy).then_inc(piece_high[slot], 1)

            def queries(N, u):
                act.wait_ge(col_ready, N + 1 + AHEAD)
                act.wait_ge(q_ps, N + 1 + AHEAD)
                act.activation(QH[:, u, :], ps[:, BQ, :], ACT.Identity, bias=COL[:, u, C2_BQ:C2_BQ + 1]).then_inc(q_high, 1)

            def keys(N, u):
                act.wait_ge(col_ready, N + 1 + AHEAD)
                act.wait_ge(k_ps, N + 1 + AHEAD)
                act.activation(KH[:, u, :, 0:L], ps[:, BK, :].rearrange("p (i t) -> p i t", i=2), ACT.Identity, bias=COL[:, u, C2_BK:C2_BK + 1])
                act.activation(KH[:, u, :, L:], COL[:, u, C2_KEY:C2_KEY + 1].unsqueeze(1).broadcast_to([P, 2, 2]), ACT.Copy)\
                   .then_inc(k_high, 1)

            def values(m, v, half):
                act.wait_ge(v_ps, m + 1 + AHEAD)
                act.activation(VH[:, v, 2 * half:2 * half + 2, :, :], ps[:, BV, :].rearrange("p (t h m) -> p t h m", t=2, h=2), ACT.Copy)\
                   .then_inc(v_high, 1)

            def context(N, u):
                act.wait_ge(c_ps, N + 1 + AHEAD)
                act.sem_inc(passed, 1)

            with act.Fori(0, NPAIR) as b:
                act.wait_ge(ct_in, (b + 1) * 32 + AHEAD)
                act.activation(CTH[:, :, :], CT, ACT.Copy).then_inc(ct_high, 1)
                with act.Fori(0, 2) as a:
                    act.wait_ge(v_ps, v_count(b, a, 0) * 2 + AHEAD)
                    cut(VS, v_count(b, a, 0))
                    act.wait_ge(g_used, b * 48 + a * 16 + AHEAD)
                    N0 = (b * 2 + a) * H2
                    cut(1, qk_count(b, a, 0))
                    values(v_count(b, a, 0) * 2, 0, 0)
                    for u in (0, 3, 2):
                        cut(u, qk_count(b, a, 0))
                    norm(b * 3 + a, lambda: values(v_count(b, a, 0) * 2 + 1, 0, 1))
                    act.wait_ge(v_ps, v_count(b, a, 1) * 2 + AHEAD)
                    cut(VS, v_count(b, a, 1))
                    keys(N0, 0)
                    queries(N0, 0)

                    def head(j, c, first=False):
                        u, v = c % 2, c // 2
                        N = (b * 2 + a) * H2 + j * 2 + u
                        for i in range(4):
                            act.wait_ge(max_ready, N * 4 + i + 1 + AHEAD)
                            act.wait_ge(tb_ps, N + AHEAD)
                            act.activation(PR[:, i, 0:L + 1], ps[:, BS + 1 - i % 2, 0:L + 1], ACT.Exp, bias=NMS[:, i:i + 1], scale=float(K2) ** -0.5,
                                           accum_out=RS[:, i:i + 1])\
                               .then_inc(exp_ready, 1)
                        if not first:
                            context(N - 1, 1 - u)
                            act.activation(G[:, j * 2 + u - 1, :], ps[:, BC, :], ACT.Identity, bias=COL[:, 1 - u, C2_BV:C2_BV + 1]).then_inc(c_ready, 1)
                        if not (is_head(j, c, H2 - 2) or is_head(j, c, H2 - 1)):
                            act.wait_ge(q_ps, N + 1 + AHEAD)
                            cut(2 * u, qk_count(b, a, j + 1))
                        if not is_head(j, c, H2 - 1):
                            queries(N + 1, 1 - u)
                        if not (is_head(j, c, H2 - 2) or is_head(j, c, H2 - 1)):
                            act.wait_ge(k_ps, N + 1 + AHEAD)
                            cut(2 * u + 1, qk_count(b, a, j + 1))
                        if not is_head(j, c, H2 - 1):
                            keys(N + 1, 1 - u)
                        for i in range(2):
                            act.wait_ge(t_ps, N * 2 + i + 1 + AHEAD)
                            act.wait_ge(c_ps, N + AHEAD)
                            act.activation(PTH[:, i, :, :], ps[:, BT + i, :].rearrange("p (t q) -> p t q", t=2), ACT.Copy).then_inc(pt_high, 1)
                        if not (is_head(j, c, H2 - 2) or is_head(j, c, H2 - 1)):
                            values(v_count(b, a, j + 1) * 2 + u, (1 - v), u)
                            if u and not is_head(j, c, H2 - 3):
                                act.wait_ge(v_ps, v_count(b, a, j + 2) * 2 + AHEAD)
                                cut(VS, v_count(b, a, j + 2))
                        if is_head(j, c, H2 - 1):
                            for k in range(4):
                                down_piece(0, k)
                            act.drain()
                            context_high(0, 0)
                            context_high(0, 1)

                    def down_piece(j, u):
                        act.wait_ge(k_ps if u % 2 else q_ps, N0 + H2 + AHEAD)
                        act.wait_ge(g_used, b * 48 + a * 16 + j * 4 + u - 3 + AHEAD)
                        cut(u, b * PER_PAIR + a * PER_ATT + H2 // 2 + j)

                    def context_high(j, u):
                        act.wait_ge(g_used, b * 48 + a * 16 + j * 4 + u - 1 + AHEAD)
                        act.sem_inc(passed, 1)
                        act.activation(GH[:, u % 2, :], G[:, j * 4 + u, :], ACT.Copy).then_inc(g_high, 1)

                    head_steps(act, head)
                    context(N0 + H2 - 1, 1)
                    act.activation(G[:, H2 - 1, :], ps[:, BC, :], ACT.Identity, bias=COL[:, 1, C2_BV:C2_BV + 1]).then_inc(c_ready, 1)
                    act.drain()
                    context_high(0, 2)
                    context_high(0, 3)
                    with act.Fori(1, H2 // 4) as j:
                        for u in range(4):
                            down_piece(j, u)
                            context_high(j, u)
                norm(b * 3 + 2)

                with act.Fori(0, FC2 // 2) as f:
                    for u in range(2):
                        n = f * 2 + u
                        act.wait_ge(fc_ps, b * FC2 + n + 1 + AHEAD)
                        act.wait_ge(g_low, b * 48 + 32 + n - 1 + AHEAD)
                        act.sem_inc(passed, 1)
                        act.activation(G[:, EC + u, :], ps[:, BQ + u, :], ACT.Gelu, bias=FB[:, f * 2 + u, :]).then_inc(gelu_ready, 1)

        @block.vector
        def _(dve):
            dve.wait_ge(consts_in, 6 * 16 + AHEAD)
            dve.wait_ge(memset_done, 1 + AHEAD)

            def norm(n, v, middle=None):
                dve.wait_ge(mean_ps, n + 1 + AHEAD)
                for k in range(EC):
                    dve.tensor_tensor(H[:, k, :], X[:, k, :], ps[:, BQ, :], ALU.subtract).then_inc(xc_ready, 1)
                if middle:
                    middle()
                dve.wait_ge(sd_ready, n + 1 + AHEAD)
                dve.reciprocal(SD[:, :], SD[:, :])
                dve.drain()
                for k in range(EC):
                    dve.tensor_tensor(H[:, k, :], H[:, k, :], SD[:, :], ALU.mult)
                    dve.drain()
                    dve.tensor_scalar(H[:, k, :], H[:, k, :], VEC[:, v, V2_NW, k:k + 1], VEC[:, v, V2_NB, k:k + 1], ALU.mult, ALU.add).then_inc(h_full, 1)

            def cut(slot, count):
                dve.wait_ge(piece_in[slot], (count + 1) * 16 + AHEAD)
                dve.tensor_copy(piece(WH, slot), piece(WR, slot)).then_inc(piece_high[slot], 1)

            def columns(N, a, j, u):
                dve.wait_ge(c_ready, N - 1 + AHEAD)
                dve.sem_inc(passed, 1)
                dve.tensor_copy(COL[:, u, :], HC[:, a * H2 + j * 2 + u, :]).then_inc(col_ready, 1)

            def rows(N, count, u):
                dve.wait_ge(rows_in[u], (count + 1) * 16 + AHEAD)
                dve.wait_ge(c_ps, N - 1 + AHEAD)
                dve.tensor_tensor(RD[:, :], RW[:, u, 0, :], RW[:, u, 1, :], ALU.subtract)
                dve.drain()
                dve.tensor_copy(RDH[:, :], RD[:, :])
                dve.drain()
                dve.tensor_scalar(RD[:, :], RD[:, :], PMASK[:, 0:1], None, ALU.mult)
                dve.drain()
                dve.scalar_tensor_tensor(RST[0:PARTS, u, :], RDH[:, :], PMASK[:, 1:2], RD[:, :], ALU.mult, ALU.add).then_inc(rows_ready, 1)

            def queries(N, u):
                dve.wait_ge(q_high, N + 1 + AHEAD)
                dve.scalar_tensor_tensor(QL[:, u, :], ps[:, BQ, :], COL[:, u, C2_BQ:C2_BQ + 1], QH[:, u, :], ALU.add, ALU.subtract).then_inc(q_low, 1)

            def keys(N, u):
                dve.wait_ge(k_high, N + 1 + AHEAD)
                dve.scalar_tensor_tensor(KL[:, u, :, 0:L], ps[:, BK, :].rearrange("p (i t) -> p i t", i=2), COL[:, u, C2_BK:C2_BK + 1],
                                         KH[:, u, :, 0:L], ALU.add, ALU.subtract)
                dve.tensor_tensor(KL[:, u, :, L:], COL[:, u, C2_KEY:C2_KEY + 1].unsqueeze(1).broadcast_to([P, 2, 2]), KH[:, u, :, L:], ALU.subtract)\
                   .then_inc(k_low, 1)

            def values(m, v, half):
                dve.wait_ge(v_high, m + 1 + AHEAD)
                dve.tensor_tensor(VL[:, v, 2 * half:2 * half + 2, :, :], ps[:, BV, :].rearrange("p (t h m) -> p t h m", t=2, h=2),
                                  VH[:, v, 2 * half:2 * half + 2, :, :], ALU.subtract).then_inc(v_low, 1)

            with dve.Fori(0, NPAIR) as b:
                dve.wait_ge(ct_high, b + 1 + AHEAD)
                dve.tensor_tensor(CTL[:, :, :], CT, CTH[:, :, :], ALU.subtract).then_inc(ct_ready, 1)
                dve.wait_ge(x_in, (b + 1) * 32 + AHEAD)
                dve.sem_inc(ln_in, EC)
                with dve.Fori(0, 2) as a:
                    N0 = (b * 2 + a) * H2
                    values(v_count(b, a, 0) * 2, 0, 0)
                    norm(b * 3 + a, a, lambda: values(v_count(b, a, 0) * 2 + 1, 0, 1))
                    columns(N0, a, 0, 0)
                    keys(N0, 0)
                    queries(N0, 0)

                    def head(j, c, first=False):
                        u, v = c % 2, c // 2
                        N = (b * 2 + a) * H2 + j * 2 + u

                        def weights(i):
                            dve.wait_ge(exp_ready, N * 4 + i + 1 + AHEAD)
                            dve.reciprocal(RS[:, i:i + 1], RS[:, i:i + 1])
                            dve.drain()
                            dve.tensor_scalar(PR[:, i, 0:L + 1], PR[:, i, 0:L + 1], RS[:, i:i + 1], None, ALU.mult).then_inc(p_ready, 1)

                        for i in range(4):
                            dve.wait_ge(s_ps, N * 4 + i + 1 + AHEAD)
                            dve.tensor_reduce(NM[:, i:i + 1], ps[:, BS + 1 - i % 2, 0:L + 1], AX.X, ALU.max, negate=True)
                            dve.drain()
                            dve.tensor_scalar(NMS[:, i:i + 1], NM[:, i:i + 1], float(K2) ** -0.5, None, ALU.mult).then_inc(max_ready, 1)
                            if i > 0:
                                weights(i - 1)
                            if i == 1 and not first and not is_head(j, c, H2 - 1):
                                values(v_count(b, a, j + u) * 2 + 1 - u, 1 - (c - 1) % 4 // 2, 1 - u)
                        weights(3)
                        dve.drain()
                        dve.tensor_copy(PBH[:, :], PR[:, :, L])
                        dve.drain()
                        dve.tensor_tensor(PB[:, 2, :], PR[:, :, L], PBH[:, :], ALU.subtract)
                        for part in range(2):
                            mm = dve.tensor_copy(PB[:, part, :], PBH[:, :])
                        dve.drain().then_inc(pb_ready, 1)
                        if not is_head(j, c, H2 - 1):
                            columns(N + 1, a, j + u, 1 - u)
                            queries(N + 1, 1 - u)
                            keys(N + 1, 1 - u)
                        rows(N, v_count(b, a, j), u)
                        for i in range(2):
                            if i:
                                dve.wait_ge(tb_ps, N + 1 + AHEAD)
                                dve.wait_ge(c_ps, N + AHEAD)
                                dve.tensor_tensor(BD[0:PARTS, :, :], CMASK[:, :, :],
                                                  ps[0:PARTS, BS, 384:384 + P].unsqueeze(1).broadcast_to([PARTS, 4, P]), ALU.mult).then_inc(bd_ready, 1)
                            dve.wait_ge(pt_high, N * 2 + i + 1 + AHEAD)
                            dve.tensor_tensor(PTL[:, i, :, :], ps[:, BT + i, :].rearrange("p (t q) -> p t q", t=2), PTH[:, i, :, :], ALU.subtract)\
                               .then_inc(pt_low, 1)

                    head_steps(dve, head)
                    with dve.Fori(0, H2 // 4) as j:
                        for u in range(4):
                            dve.wait_ge(g_high, b * 32 + a * 16 + j * 4 + u + 1 + AHEAD)
                            dve.sem_inc(passed, 1)
                            dve.tensor_tensor(GL[:, u % 2, :], G[:, j * 4 + u, :], GH[:, u % 2, :], ALU.subtract).then_inc(g_low, 1)
                    dve.wait_ge(g_used, b * 48 + a * 16 + 16 + AHEAD)
                    for d in range(EC):
                        dve.scalar_tensor_tensor(X[:, d, :], ps[:, BX + d, :], VEC[:, a, V2_BO, d:d + 1], X[:, d, :], ALU.add, ALU.add)\
                           .then_inc(x_ready, 1)
                        dve.drain().then_inc(ln_in, 1)
                F0 = b * PER_PAIR + 2 * PER_ATT
                cut(0, F0)
                cut(2, F0)
                norm(b * 3 + 2, 2)

                def chunk(f, u):
                    n = f * 2 + u
                    dve.wait_ge(gelu_ready, b * FC2 + n + 1 + AHEAD)
                    dve.wait_ge(g_used, b * 48 + 32 + n - 1 + AHEAD)
                    dve.tensor_copy(GH[:, u, :], G[:, EC + u, :])
                    dve.drain()
                    dve.tensor_tensor(GL[:, u, :], G[:, EC + u, :], GH[:, u, :], ALU.subtract).then_inc(g_low, 1)

                with dve.Fori(0, FC2 // 2 - 1) as f:
                    for u in range(2):
                        dve.wait_ge(g_used, b * 48 + 32 + f * 2 + u - 1 + AHEAD)
                        cut(2 * u + 1, F0 + f)
                        dve.wait_ge(fc_ps, b * FC2 + f * 2 + u + 1 + AHEAD)
                        cut(2 * u, F0 + f + 1)
                        chunk(f, u)
                for u in range(2):
                    dve.wait_ge(g_used, b * 48 + 32 + FC2 - 2 + u - 1 + AHEAD)
                    cut(2 * u + 1, F0 + FC2 // 2 - 1)
                    chunk(FC2 // 2 - 1, u)
                dve.wait_ge(g_used, b * 48 + 48 + AHEAD)
                for d in range(EC):
                    dve.scalar_tensor_tensor(X[:, d, :], ps[:, BX + d, :], VEC[:, 2, V2_BO, d:d + 1], X[:, d, :], ALU.add, ALU.add).then_inc(x_ready, 1)

CI = 128
(V3_TB, V3_WB, V3_GAMMA, V3_BETA, V3_MEAN, V3_VAR) = (0, 1, 3, 5, 7, 9)
NV3 = 11


def layer3(nc, x3T, ctx, theta_w, pg_w, pg_b, w_w, vec3, ident_in, out):
    with ExitStack() as stack:
        def sb(name, shape, dt=F32):
            return stack.enter_context(nc.sbuf_tensor("d_" + name, shape, dt))

        sems = []

        def sem(name):
            sems.append(stack.enter_context(nc.semaphore("d_" + name)))
            return sems[-1]

        WT = sb("wt", [P, LC, CI])
        WPG = sb("wpg", [P, LC, 2 * CI])
        BPG = sb("bpg", [P, 2 * CI])
        WW = sb("ww", [P, L])
        VEC = sb("vec", [P, NV3])
        ID = sb("id", [P, P])
        EPS = sb("eps", [P, 1])
        BN = sb("bn", [P, 2, 2])
        XT = sb("xt", [P, EC, L])
        C = sb("c", [P, LC, E])
        X = sb("x", [P, LC, E])
        PG = sb("pg", [P, EC, 2 * CI])
        M = sb("m", [P, CI])
        TH = sb("th", [P, E])
        Y = sb("y", [P, E])
        O = sb("o", [P, LC, E])
        ps = stack.enter_context(nc.psum_tensor("d_ps", [P, 8, 512], F32))
        names = "consts_in memset_done bn_sqrt bn_in x_in in_used x_ps x_ready pg_ps pg_ready m_ps m_ready th_ps th_ready y_ps y_ready o_ps o_read out_ready out_free passed".split()
        (consts_in, memset_done, bn_sqrt, bn_in, x_in, in_used, x_ps, x_ready, pg_ps, pg_ready, m_ps, m_ready, th_ps, th_ready,
         y_ps, y_ready, o_ps, o_read, out_ready, out_free, passed) = [sem(n) for n in names]
        out_stored = stack.enter_context(nc.semaphore("d_out_stored"))
        block = stack.enter_context(nc.Block())

        @block.sync
        def _(sp):
            start_ahead(sp, sems)
            for dst, src in ((WT[:, :, :], theta_w), (WPG[:, :, :], pg_w), (BPG[:, :], pg_b), (WW[:, :], w_w), (VEC[:, :], vec3), (ID[:, :], ident_in)):
                sp.dma_start(dst, src).then_inc(consts_in, 16)
            with sp.Fori(0, B) as b:
                sp.wait_ge(x_ps, b + AHEAD)
                sp.sem_inc(passed, 1)
                sp.wait_ge(pg_ps, b + AHEAD)
                sp.sem_inc(passed, 1)
                sp.dma_start(XT[:, :, :], x3T[b]).then_inc(x_in, 16)
                sp.dma_start(C[:, :, :], ctx[b].rearrange("(k p) t -> p k t", p=P)).then_inc(x_in, 16)
        @block.gpsimd
        def _(pool):
            pool.memset(EPS[:, :], LN_EPS).then_inc(memset_done, 1)
            with pool.Fori(0, B) as b:
                pool.wait_ge(out_ready, b + 1 + AHEAD)
                pool.sem_inc(passed, 1)
                pool.dma_start(out[b].rearrange("(k p) t -> p k t", p=P), O[:, :, :]).then_inc(out_stored, 16)
                pool.wait_ge(out_stored, (b + 1) * 16)
                pool.sem_inc(out_free, 1)

        @block.tensor
        def _(pe):
            pe.wait_ge(consts_in, 96 + AHEAD)
            pe.wait_ge(memset_done, 1 + AHEAD)
            with pe.Fori(0, B) as b:
                pe.wait_ge(x_in, (b + 1) * 32 + AHEAD)
                for c in range(LC):
                    for k in range(EC):
                        mm = pe.transpose(ps[:, c, k * P:(k + 1) * P], XT[:, k, c * P:(c + 1) * P], ID[:, :])
                mm.then_inc(x_ps, 1)
                pe.wait_ge(o_read, b + AHEAD)
                for m in range(EC):
                    for k in range(LC):
                        mm = pe.matmul(ps[:, 2 + m // 2, (m % 2) * L:(m % 2 + 1) * L], C[:, k, m * P:(m + 1) * P], WPG[:, k, :],
                                       start=(k == 0), stop=(k == LC - 1), skip_group_check=True)
                mm.then_inc(pg_ps, 1)
                pe.wait_ge(x_ready, b + 1 + AHEAD)
                for k in range(LC):
                    mm = pe.matmul(ps[:, 5, :], WT[:, k, :], X[:, k, :], start=(k == 0), stop=(k == LC - 1))
                mm.then_inc(th_ps, 1)
                pe.wait_ge(pg_ready, b + 1 + AHEAD)
                for m in range(EC):
                    mm = pe.matmul(ps[:, 4, 0:CI], PG[:, m, 0:CI], PG[:, m, CI:], start=(m == 0), stop=(m == EC - 1))
                mm.then_inc(m_ps, 1)
                pe.wait_ge(m_ready, b + 1 + AHEAD)
                pe.wait_ge(th_ready, b + 1 + AHEAD)
                pe.matmul(ps[:, 6, :], M[:, :], TH[:, :], start=True, stop=True).then_inc(y_ps, 1)
                pe.wait_ge(y_ready, b + 1 + AHEAD)
                for c in range(LC):
                    mm = pe.matmul(ps[:, 2 + c, :], WW[:, c * P:(c + 1) * P], Y[:, :], start=True, stop=True)
                mm.then_inc(o_ps, 1)

        @block.scalar
        def _(act):
            act.wait_ge(memset_done, 1 + AHEAD)
            act.wait_ge(consts_in, 96 + AHEAD)
            act.activation(BN[:, 0, :], VEC[:, V3_VAR:V3_VAR + 2], ACT.Sqrt, bias=EPS[:, 0:1]).then_inc(bn_sqrt, 1)
            with act.Fori(0, B) as b:
                act.wait_ge(x_ps, b + 1 + AHEAD)
                act.wait_ge(in_used, b + AHEAD)
                act.activation(X[:, :, :], ps[:, 0:2, :], ACT.Copy).then_inc(x_ready, 1)
                act.wait_ge(th_ps, b + 1 + AHEAD)
                act.activation(TH[:, :], ps[:, 5, :], ACT.Identity, bias=VEC[:, V3_TB:V3_TB + 1]).then_inc(th_ready, 1)
                act.wait_ge(y_ps, b + 1 + AHEAD)
                act.activation(Y[:, :], ps[:, 6, :], ACT.Copy).then_inc(y_ready, 1)

        @block.vector
        def _(dve):
            dve.wait_ge(bn_sqrt, 1 + AHEAD)
            dve.reciprocal(BN[:, 0, :], BN[:, 0, :])
            dve.tensor_tensor(BN[:, 1, :], VEC[:, V3_WB:V3_WB + 2], VEC[:, V3_MEAN:V3_MEAN + 2], ALU.subtract)
            dve.drain()
            dve.tensor_tensor(BN[:, 0, :], BN[:, 0, :], VEC[:, V3_GAMMA:V3_GAMMA + 2], ALU.mult)
            dve.drain()
            dve.tensor_tensor(BN[:, 1, :], BN[:, 1, :], BN[:, 0, :], ALU.mult)
            dve.drain()
            dve.tensor_tensor(BN[:, 1, :], BN[:, 1, :], VEC[:, V3_BETA:V3_BETA + 2], ALU.add)
            with dve.Fori(0, B) as b:
                dve.wait_ge(pg_ps, b + 1 + AHEAD)
                dve.tensor_tensor(PG[:, :, :], ps[:, 2:4, :].rearrange("p a (c t) -> p (a c) t", c=2),
                                  BPG[:, :].unsqueeze(1).broadcast_to([P, EC, 2 * CI]), ALU.add).then_inc(pg_ready, 1)
                dve.wait_ge(m_ps, b + 1 + AHEAD)
                dve.tensor_scalar(M[:, :], ps[:, 4, 0:CI], 1.0 / E, None, ALU.mult).then_inc(m_ready, 1)
                dve.wait_ge(o_ps, b + 1 + AHEAD)
                dve.wait_ge(out_free, b + AHEAD)
                for c in range(LC):
                    dve.tensor_scalar(O[:, c, :], ps[:, 2 + c, :], BN[:, 0, c:c + 1], BN[:, 1, c:c + 1], ALU.mult, ALU.add)
                dve.drain().then_inc(o_read, 1)
                dve.tensor_tensor(O[:, :, :], O[:, :, :], X[:, :, :], ALU.add).then_inc(out_ready, 1)
                dve.drain().then_inc(in_used, 1)


def _l0(I):
    import numpy as np
    f=np.ascontiguousarray
    def pad(W):
        z=np.zeros((4,4,32,256),np.float32); z[:,:,:16,:]=W.reshape(4,4,16,256)
        return z.reshape(4,128,2,128).transpose(3,0,2,1)
    def padb(b):
        z=np.zeros((4,4,32),np.float32); z[:,:,:16]=b.reshape(4,4,16); return z.reshape(4,128).T
    wqk=f(np.stack([pad(I['L0_xattn_Wq']),pad(I['L0_xattn_Wk'])],axis=3))
    qkb=f(np.stack([padb(I['L0_xattn_bq']),padb(I['L0_xattn_bk'])],axis=1))
    aug=np.zeros((4,32,2,4),np.float32); aug[:,16,0]=4.0; aug[:,17,1]=1.0
    ms=np.zeros((128,4,32),np.float32); ms[0,:,16]=1.0
    wv=f(I['L0_xattn_Wv'].T.reshape(2,128,256).transpose(1,0,2))
    m=I['mask_Bx1x2048_bf1'].view(np.uint8)
    return dict(x=I['x'],xT=f(I['x'].transpose(0,2,1)),ctx=I['ctx_2048'],mask_row=f(np.broadcast_to(m,(8,128,512))),mask_col=f(m.reshape(8,4,128).transpose(0,2,1)),
      wqk=wqk,qkb=qkb,aug=aug.reshape(128,2,4),wv=wv,bv=f(np.broadcast_to(I['L0_xattn_bv'],(128,256))),mask_sel=ms.reshape(128,128),ident_in=np.eye(128,dtype=np.float32))


def _l1(I):
    import numpy as np
    f=np.ascontiguousarray
    c=I['ctx_2048']
    s0=f(c[:,2:18].reshape(8,4,128,16).transpose(0,2,1,3))
    n=lambda k:I['L1_xattn_'+k].reshape(-1,512)
    v=np.concatenate([n('ln1_w'),n('ln1_b'),n('ln2_w'),n('ln2_b'),n('maa_x'),n('maa_stack'),n('time_decay'),n('u'),n('gn_w'),n('gn_b'),n('ffn_maa_k'),n('ffn_maa_r')])
    vecs=f(v.reshape(16,4,128).transpose(2,0,1))
    w8=f(np.stack([I['L1_xattn_'+k].T.reshape(4,128,512).transpose(1,0,2) for k in ('Wk','Wv','Wr','Wg','Wo','Wfk','Wfr','Wfv')],axis=1))
    sel=np.zeros((8,16,16,8,16),np.float32)
    for h in range(8):
        for j in range(16): sel[h,j,j,h,:]=1
    sel=sel.reshape(128,16,128)
    blk=np.kron(np.eye(8,dtype=np.float32),np.ones((16,16),np.float32))
    w2=np.zeros((128,5,512),np.float32)
    for i in range(5): w2[(i%4)*32:(i%4)*32+32,i]=I['L1_xattn_maa_w2'][i]
    tw2=np.zeros((128,512),np.float32); tw2[:64]=I['L1_xattn_td_w2']
    prevs=f(c[:,:2].reshape(8,2,4,128).transpose(0,3,2,1))
    return dict(prevs=prevs,ctxT=f(c.transpose(0,2,1)),s0=s0,vecs=vecs,w8=w8,maa_w1=f(I['L1_xattn_maa_w1'].reshape(4,128,160).transpose(1,0,2)),
      maa_w2=w2,td_w1=f(I['L1_xattn_td_w1'].reshape(4,128,64).transpose(1,0,2)),td_w2=tw2,
      sel=sel,selT=f(sel.transpose(2,1,0)),blk=f(np.stack([blk,blk/16])))


def _l2(I):
    import numpy as np
    f=np.ascontiguousarray; g=lambda k:I['L2_xattn_'+k]
    def hd(W): return W.reshape(4,128,16,128).transpose(2,1,0,3).reshape(16,128,512)
    def two(W): return W.reshape(4,128,8,256).transpose(2,1,0,3).reshape(8,128,1024)
    heads=np.stack([np.stack([g(k+i).reshape(16,128) for k in ('bq','bk','bias_k','bv')]) for i in '12'])
    rows=np.concatenate([np.stack([g('bias_v'+i).reshape(16,128),g('bv'+i).reshape(16,128)],1) for i in '12'])
    downs=[W.reshape(16,128,512) for W in (g('wo1'),g('wo2'),g('w_fc2'))]
    pm=np.zeros((12,2),np.float32); pm[:,1]=1; pm[4:8]=(1,-1)
    cm=np.zeros((3,4,4,128),np.float32)
    for c in range(4): cm[:,c,c]=1
    v=np.stack([np.stack([g('ln1_scale'),g('ln1_offset'),g('bo1')]),np.stack([g('ln2_scale'),g('ln2_offset'),g('bo2')]),np.stack([g('ln_mlp_scale'),g('ln_mlp_offset'),g('b_fc2')])])
    return dict(wq=f(np.concatenate([hd(g('wq1')),hd(g('wq2'))])),wk=f(np.concatenate([hd(g('wk1')),hd(g('wk2'))])),
                wv2=f(np.concatenate([two(g('wv1')),two(g('wv2'))])),heads=f(heads.transpose(3,0,2,1).reshape(128,32,4)),
                value_rows=f(np.broadcast_to(rows[:,None],(32,12,2,128))),part_mask=pm,chunk_mask=f(cm.reshape(12,4,128)),
                downs=f(np.concatenate(downs)),fc1=f(hd(g('w_fc1'))),fc1_b=f(g('b_fc1').reshape(16,128).T),
                vec2=f(v.reshape(3,3,4,128).transpose(3,0,1,2)),ident_in=np.eye(128,dtype=np.float32))


def _l3(I):
    import numpy as np
    f=np.ascontiguousarray; g=lambda k:I['L3_xattn_'+k]
    def ci(W): return W.reshape(128,2,128).transpose(2,1,0)
    v=np.concatenate([g('theta_b').reshape(1,128)]+[g(k).reshape(2,128) for k in ('w_b','bn_gamma','bn_beta','bn_mean','bn_var')]).T
    return dict(theta_w=f(ci(g('theta_w'))),pg_w=f(np.concatenate([ci(g('phi_w')),ci(g('g_w'))],axis=2)),pg_b=f(np.broadcast_to(np.concatenate([g('phi_b'),g('g_b')]),(128,256))),w_w=f(g('w_w').T),vec3=f(v),ident_in=np.eye(128,dtype=np.float32),ctx=I['ctx_2048'])


def build(nc, io, out):
    def scratch(name):
        return nc.dram_tensor(name, [B, P, EC, L], F32).ap()

    x1T, x2T, x3T = scratch("x1T"), scratch("x2T"), scratch("x3T")
    layer0(nc, x=io["x"], xT=io["xT"], ctx=io["ctx"], mask_row=io["mask_row"], mask_col=io["mask_col"], wqk=io["wqk"], qkb=io["qkb"],
           aug=io["aug"], wv=io["wv"], bv=io["bv"], mask_sel=io["mask_sel"], ident_in=io["ident_in"], x1T=x1T)
    layer1(nc, x1T=x1T, prevs=io["prevs"], s0=io["s0"], vecs=io["vecs"], w8=io["w8"], maa_w1=io["maa_w1"], maa_w2=io["maa_w2"],
           td_w1=io["td_w1"], td_w2=io["td_w2"], sel=io["sel"], selT=io["selT"], blk=io["blk"], x2T=x2T)
    layer2(nc, x2T=x2T, ctxT=io["ctxT"], wq=io["wq"], wk=io["wk"], wv=io["wv2"], heads=io["heads"],
           value_rows=io["value_rows"], part_mask=io["part_mask"], chunk_mask=io["chunk_mask"], downs=io["downs"], fc1=io["fc1"],
           fc1_b=io["fc1_b"], vec2=io["vec2"],
           ident_in=io["ident_in"], x3T=x3T)
    layer3(nc, x3T=x3T, ctx=io["ctx"], theta_w=io["theta_w"], pg_w=io["pg_w"], pg_b=io["pg_b"], w_w=io["w_w"], vec3=io["vec3"],
           ident_in=io["ident_in"], out=out)


def kernel(**inputs):
    import numpy as np
    import concourse.bacc as bacc
    from concourse.bass_utils import run_bass_kernel_spmd

    I = {k: np.asarray(v) for k, v in inputs.items()}
    arrays = {}
    for part in (_l0(I), _l1(I), _l2(I), _l3(I)):
        arrays.update(part)
    arrays = {k: np.ascontiguousarray(v) for k, v in arrays.items()}
    nc = bacc.Bacc("TRN2", target_bir_lowering=False, num_devices=1)
    io = {k: nc.dram_tensor("in_" + k, a.shape, mybir.dt.from_np(a.dtype), kind="ExternalInput").ap() for k, a in arrays.items()}
    out = nc.dram_tensor("out", (B, L, E), F32, kind="ExternalOutput").ap()
    build(nc, io, out)
    r = run_bass_kernel_spmd(nc, [{"in_" + k: a for k, a in arrays.items()}], core_ids=[0])
    return r.results[0]["out"]
```
